# Optimizing a Trainium2 kernel written in Bass

```python
import numpy as np
import jax
import jax.numpy as jnp

def _softmax(x, axis=-1):
    return jax.nn.softmax(x, axis=axis)

def _gelu(x):
    return jax.nn.gelu(x, approximate=True)

def _silu(x):
    return jax.nn.silu(x)

def _sigmoid(x):
    return jax.nn.sigmoid(x)

def _layernorm(x, axis=-1, eps=1e-05):
    m = jnp.mean(x, axis=axis, keepdims=True)
    v = jnp.var(x, axis=axis, keepdims=True)
    return (x - m) / jnp.sqrt(v + eps)

def _scatter_add(tgt, idx, src, axis=0):
    return tgt.at[idx].add(src)

def _segment_sum(src, seg, n):
    return jax.ops.segment_sum(src, seg, n)
kernel_name = 'mk_flamingo_gated_d2_seqx_r8_f527b0'

def setup_inputs(seed: int=0):
    np.random.seed(seed)
    _w = jnp.asarray

    def _rec_inputs():
        import jax
        import jax.numpy as jnp
        _rk = jax.random.key(seed)
        x = -0.0002928 + 1 * jax.random.normal(jax.random.fold_in(_rk, 1), (8, 256, 128), jnp.float32)
        _lenS = 256 - jax.random.randint(jax.random.fold_in(_rk, 7), (8,), 0, max(1, 256 // 4) + 1, jnp.int32)
        _lenS2 = 256 - jax.random.randint(jax.random.fold_in(_rk, 8), (8,), 0, max(1, 256 // 4) + 1, jnp.int32)
        _ctx_1024P = jax.random.normal(jax.random.fold_in(_rk, 11), (8, 16, 128), jnp.float32)
        _ctx_1024c = jax.random.dirichlet(jax.random.fold_in(_rk, 511), 0.3 * jnp.ones((16,), jnp.float32), (8, 256))
        _ctx_1024t = jnp.einsum('bsk,bkd->bsd', _ctx_1024c, _ctx_1024P)
        _ctx_1024t = _ctx_1024t * jax.lax.rsqrt(jnp.mean(jnp.square(_ctx_1024t)) + 1e-12) * 0.953939
        ctx_1024 = -1.39393e-06 + 0.999914 * (_ctx_1024t + 0.3 * jax.random.normal(jax.random.fold_in(_rk, 611), (8, 256, 128), jnp.float32))
        itok_BxS_0_255 = jax.random.randint(jax.random.fold_in(_rk, 12), (8, 256), 0, 32, jnp.int32)
        _g = jax.random.normal(jax.random.fold_in(_rk, 9001), (2, 2), jnp.float32)
        _g = jnp.sign(_g) * jnp.maximum(jnp.abs(_g), 1.0) + (_g == 0) * 1.0
        g_xattn = _g[0]
        g_ffn = _g[1]
        return (x, ctx_1024, itok_BxS_0_255, g_xattn, g_ffn)
    x, ctx_1024, itok_BxS_0_255, g_xattn, g_ffn = _rec_inputs()

    def _L0_xattn_setup():
        import jax, jax.numpy as jnp
        import numpy as np
        EMB = 128
        NH = 8
        HD = EMB // NH
        EPS = 1e-06

        def _mlstm_head(q, k, v, ig, fg):
            S, DH = q.shape
            log_fg = jax.nn.log_sigmoid(fg)
            cs = jnp.concatenate([jnp.zeros((1, 1), q.dtype), jnp.cumsum(log_fg, axis=0)], axis=0)
            fg_mat_full = cs - cs.T
            ltr = jnp.tril(jnp.ones((S, S), bool))
            log_fg_matrix = jnp.where(ltr, fg_mat_full[1:, 1:], -jnp.inf)
            log_D = log_fg_matrix + ig.T
            max_log_D = jnp.max(log_D, axis=-1, keepdims=True)
            D = jnp.exp(log_D - max_log_D)
            qk = q @ (k.T / jnp.sqrt(jnp.asarray(DH, q.dtype)))
            C = qk * D
            normalizer = jnp.maximum(jnp.abs(C.sum(-1, keepdims=True)), jnp.exp(-max_log_D))
            return C / (normalizer + EPS) @ v
        key = jax.random.key(seed)
        ks = jax.random.split(key, 6)
        B, S = (2, 256)
        q = jax.random.normal(ks[0], (B, S, EMB), jnp.float32)
        k = jax.random.normal(ks[1], (B, S, EMB), jnp.float32)
        v = jax.random.normal(ks[2], (B, S, EMB), jnp.float32)
        igate_kernel = jax.random.normal(ks[3], (3 * EMB, NH), jnp.float32) * 0.02
        igate_bias = jax.random.normal(ks[4], (NH,), jnp.float32) * 0.1
        fgate_kernel = jax.random.normal(ks[5], (3 * EMB, NH), jnp.float32) * 0.02
        fgate_bias = jnp.linspace(3.0, 6.0, NH).astype(jnp.float32)
        return dict(q=q, k=k, v=v, igate_kernel=igate_kernel, igate_bias=igate_bias, fgate_kernel=fgate_kernel, fgate_bias=fgate_bias)
    _L0_xattn_all = _L0_xattn_setup()
    _L0_xattn_in = {k: v for k, v in _L0_xattn_all.items() if k in ('igate_kernel', 'igate_bias', 'fgate_kernel', 'fgate_bias')}
    del _L0_xattn_all

    def _L0_ffn_setup():
        import jax, jax.numpy as jnp
        import numpy as np
        B, S, D = (2, 256, 128)
        H, E, P, K = (8, 8, 128, 2)
        SCALE = 1.0 / np.sqrt(P)

        def _get_sel_gate(x, w, route_scale):
            logits = jnp.einsum('bsd,ed->bse', x, w).astype(jnp.float32)
            raw = logits.reshape(x.shape[0], x.shape[1], H, E)
            probs = jax.nn.sigmoid(raw)
            vals, idx = jax.lax.top_k(probs, K)
            vals = vals / jnp.clip(vals.sum(-1, keepdims=True), 1e-09)
            vals = vals * route_scale
            gate = (jax.nn.one_hot(idx, E, dtype=vals.dtype) * vals[..., None]).sum(-2)
            return gate
        key = jax.random.key(seed)
        ks = jax.random.split(key, 8)
        std = 1.0 / np.sqrt(D)
        return {'x': jax.random.normal(ks[0], (B, S, D), jnp.float32), 'q_w': jax.random.normal(ks[1], (H * P, D), jnp.float32) * std, 'k_w': jax.random.normal(ks[2], (H * P, D), jnp.float32) * std, 'v_w': jax.random.normal(ks[3], (H * E, D, P), jnp.float32) * std, 'o_w': jax.random.normal(ks[4], (H * E, P, D), jnp.float32) * (1.0 / np.sqrt(H * P)), 'sel_v_w': jax.random.normal(ks[5], (H * E, D), jnp.float32) * std, 'sel_o_w': jax.random.normal(ks[6], (H * E, D), jnp.float32) * std, 'route_scale': jnp.ones((1,), jnp.float32)}
    _L0_ffn_all = _L0_ffn_setup()
    _L0_ffn_in = {k: v for k, v in _L0_ffn_all.items() if k in ('q_w', 'k_w', 'v_w', 'o_w', 'sel_v_w', 'sel_o_w', 'route_scale')}
    del _L0_ffn_all

    def _L1_xattn_setup():
        import jax, jax.numpy as jnp
        import numpy as np
        N_LAYERS = 4
        H = 16
        LOOKBACK = 128
        EPS = 1e-06
        ROPE_BASE = 10000.0
        NEG = jnp.float32(-1e+30)

        def rmsnorm(x, w):
            return x * jax.lax.rsqrt(jnp.mean(x * x, axis=-1, keepdims=True) + EPS) * w

        def rope_cache(L, hd):
            inv = 1.0 / ROPE_BASE ** (jnp.arange(0, hd, 2, dtype=jnp.float32) / hd)
            t = jnp.arange(L, dtype=jnp.float32)
            f = t[:, None] * inv[None, :]
            emb = jnp.concatenate([f, f], axis=-1)
            return (jnp.cos(emb), jnp.sin(emb))

        def apply_rope(x, cos, sin):
            d = x.shape[-1]
            x1, x2 = (x[..., :d // 2], x[..., d // 2:])
            rot = jnp.concatenate([-x2, x1], axis=-1)
            return x * cos + rot * sin

        def split_heads(x, n_heads):
            B, L, D = x.shape
            return x.reshape(B, L, n_heads, D // n_heads).transpose(0, 2, 1, 3)

        def merge_heads(x):
            B, h, L, d = x.shape
            return x.transpose(0, 2, 1, 3).reshape(B, L, h * d)

        def sdpa(q, k, v, bias):
            scale = q.shape[-1] ** (-0.5)
            s = jnp.einsum('bhqd,bhkd->bhqk', q, k) * scale + bias
            p = jax.nn.softmax(s, axis=-1)
            return jnp.einsum('bhqk,bhkd->bhqd', p, v)

        def forward(x, memory, seg_ids, Wqkv, bqkv, Wo, bo, Wq_c, Wkv_c, Wo_c, Wg, Wu, Wd, n1, n2, n3, nf):
            B, L, D = x.shape
            S = memory.shape[1]
            hd = D // H
            cos, sin = rope_cache(L, hd)
            i = jnp.arange(L)
            causal_bias = jnp.where(i[None, :] <= i[:, None], 0.0, NEG)[None, None]
            j = jnp.arange(S)
            allowed = (j[None, None, :] <= seg_ids[:, :, None]) & (j[None, None, :] > seg_ids[:, :, None] - LOOKBACK)
            cross_bias = jnp.where(allowed, 0.0, NEG)[:, None]
            for l in range(N_LAYERS):
                h = rmsnorm(x, n1[l])
                qkv = h @ Wqkv[l].T + bqkv[l]
                q, k, v = jnp.split(qkv, 3, axis=-1)
                q = apply_rope(split_heads(q, H), cos, sin)
                k = apply_rope(split_heads(k, H), cos, sin)
                v = split_heads(v, H)
                o = merge_heads(sdpa(q, k, v, causal_bias)) @ Wo[l].T + bo[l]
                x = x + o
                h2 = rmsnorm(x, n2[l])
                qc = split_heads(h2 @ Wq_c[l].T, H)
                kv = memory @ Wkv_c[l].T
                kc, vc = jnp.split(kv, 2, axis=-1)
                kc, vc = (split_heads(kc, H), split_heads(vc, H))
                oc = merge_heads(sdpa(qc, kc, vc, cross_bias)) @ Wo_c[l].T
                x = x + oc
                h3 = rmsnorm(x, n3[l])
                x = x + jax.nn.silu(h3 @ Wg[l].T) * (h3 @ Wu[l].T) @ Wd[l].T
            return rmsnorm(x, nf)
        key = jax.random.key(seed)
        ks = jax.random.split(key, 16)
        B, L, S, D, F = (2, 256, 32, 128, 512)
        w = 0.02
        inp = {'x': jax.random.normal(ks[0], (B, L, D), jnp.float32), 'memory': jax.random.normal(ks[1], (B, S, D), jnp.float32), 'seg_ids': jnp.sort(jax.random.randint(ks[2], (B, L), 0, S), axis=-1), 'Wqkv': jax.random.normal(ks[3], (N_LAYERS, 3 * D, D), jnp.float32) * w, 'bqkv': jnp.zeros((N_LAYERS, 3 * D), jnp.float32), 'Wo': jax.random.normal(ks[4], (N_LAYERS, D, D), jnp.float32) * w, 'bo': jnp.zeros((N_LAYERS, D), jnp.float32), 'Wq_c': jax.random.normal(ks[5], (N_LAYERS, D, D), jnp.float32) * w, 'Wkv_c': jax.random.normal(ks[6], (N_LAYERS, 2 * D, D), jnp.float32) * w, 'Wo_c': jax.random.normal(ks[7], (N_LAYERS, D, D), jnp.float32) * w, 'Wg': jax.random.normal(ks[8], (N_LAYERS, F, D), jnp.float32) * w, 'Wu': jax.random.normal(ks[9], (N_LAYERS, F, D), jnp.float32) * w, 'Wd': jax.random.normal(ks[10], (N_LAYERS, D, F), jnp.float32) * w, 'n1': jnp.ones((N_LAYERS, D), jnp.float32), 'n2': jnp.ones((N_LAYERS, D), jnp.float32), 'n3': jnp.ones((N_LAYERS, D), jnp.float32), 'nf': jnp.ones((D,), jnp.float32)}
        return inp
    _L1_xattn_all = _L1_xattn_setup()
    _L1_xattn_in = {k: v for k, v in _L1_xattn_all.items() if k in ('Wqkv', 'bqkv', 'Wo', 'bo', 'Wq_c', 'Wkv_c', 'Wo_c', 'Wg', 'Wu', 'Wd', 'n1', 'n2', 'n3', 'nf')}
    del _L1_xattn_all

    def _L1_ffn_setup():
        import jax, jax.numpy as jnp
        import numpy as np
        import math
        D_MODEL = 128
        D_FF = 512
        NUM_EXPERTS = 8
        NUM_SHARED = 1
        E_ROUTED = NUM_EXPERTS - NUM_SHARED
        TOP_K = 2
        CAP_FACTOR = 1.25
        B, S = (4, 256)
        T = B * S
        CAPACITY = math.ceil(CAP_FACTOR * T * TOP_K / E_ROUTED)
        SHARED_SCALE = 1.0

        def _layernorm(x, g, b, eps=1e-05):
            mu = jnp.mean(x, axis=-1, keepdims=True)
            var = jnp.mean((x - mu) ** 2, axis=-1, keepdims=True)
            return (x - mu) * jax.lax.rsqrt(var + eps) * g + b
        key = jax.random.key(seed)
        ks = jax.random.split(key, 10)
        s = 0.02
        return {'x': jax.random.normal(ks[0], (B, S, D_MODEL), dtype=jnp.float32), 'ln_g': jnp.ones((D_MODEL,), jnp.float32), 'ln_b': jnp.zeros((D_MODEL,), jnp.float32), 'Wr': jax.random.normal(ks[1], (D_MODEL, E_ROUTED), jnp.float32) * s, 'W1': jax.random.normal(ks[2], (E_ROUTED, D_MODEL, D_FF), jnp.float32) * s, 'W3': jax.random.normal(ks[3], (E_ROUTED, D_MODEL, D_FF), jnp.float32) * s, 'W2': jax.random.normal(ks[4], (E_ROUTED, D_FF, D_MODEL), jnp.float32) * s, 'W1s': jax.random.normal(ks[5], (D_MODEL, D_FF), jnp.float32) * s, 'W3s': jax.random.normal(ks[6], (D_MODEL, D_FF), jnp.float32) * s, 'W2s': jax.random.normal(ks[7], (D_FF, D_MODEL), jnp.float32) * s}
    _L1_ffn_all = _L1_ffn_setup()
    _L1_ffn_in = {k: v for k, v in _L1_ffn_all.items() if k in ('ln_g', 'ln_b', 'Wr', 'W1', 'W3', 'W2', 'W1s', 'W3s', 'W2s')}
    del _L1_ffn_all
    return {'x': x, 'ctx_1024': ctx_1024, 'itok_BxS_0_255': itok_BxS_0_255, 'g_xattn': g_xattn, 'g_ffn': g_ffn, 'L0_xattn_igate_kernel': _L0_xattn_in['igate_kernel'], 'L0_xattn_igate_bias': _L0_xattn_in['igate_bias'], 'L0_xattn_fgate_kernel': _L0_xattn_in['fgate_kernel'], 'L0_xattn_fgate_bias': _L0_xattn_in['fgate_bias'], 'L0_ffn_q_w': _L0_ffn_in['q_w'], 'L0_ffn_k_w': _L0_ffn_in['k_w'], 'L0_ffn_v_w': _L0_ffn_in['v_w'], 'L0_ffn_o_w': _L0_ffn_in['o_w'], 'L0_ffn_sel_v_w': _L0_ffn_in['sel_v_w'], 'L0_ffn_sel_o_w': _L0_ffn_in['sel_o_w'], 'L0_ffn_route_scale': _L0_ffn_in['route_scale'], 'L1_xattn_Wqkv': _L1_xattn_in['Wqkv'], 'L1_xattn_bqkv': _L1_xattn_in['bqkv'], 'L1_xattn_Wo': _L1_xattn_in['Wo'], 'L1_xattn_bo': _L1_xattn_in['bo'], 'L1_xattn_Wq_c': _L1_xattn_in['Wq_c'], 'L1_xattn_Wkv_c': _L1_xattn_in['Wkv_c'], 'L1_xattn_Wo_c': _L1_xattn_in['Wo_c'], 'L1_xattn_Wg': _L1_xattn_in['Wg'], 'L1_xattn_Wu': _L1_xattn_in['Wu'], 'L1_xattn_Wd': _L1_xattn_in['Wd'], 'L1_xattn_n1': _L1_xattn_in['n1'], 'L1_xattn_n2': _L1_xattn_in['n2'], 'L1_xattn_n3': _L1_xattn_in['n3'], 'L1_xattn_nf': _L1_xattn_in['nf'], 'L1_ffn_ln_g': _L1_ffn_in['ln_g'], 'L1_ffn_ln_b': _L1_ffn_in['ln_b'], 'L1_ffn_Wr': _L1_ffn_in['Wr'], 'L1_ffn_W1': _L1_ffn_in['W1'], 'L1_ffn_W3': _L1_ffn_in['W3'], 'L1_ffn_W2': _L1_ffn_in['W2'], 'L1_ffn_W1s': _L1_ffn_in['W1s'], 'L1_ffn_W3s': _L1_ffn_in['W3s'], 'L1_ffn_W2s': _L1_ffn_in['W2s']}

def reference(x, ctx_1024, itok_BxS_0_255, g_xattn, g_ffn, L0_xattn_igate_kernel, L0_xattn_igate_bias, L0_xattn_fgate_kernel, L0_xattn_fgate_bias, L0_ffn_q_w, L0_ffn_k_w, L0_ffn_v_w, L0_ffn_o_w, L0_ffn_sel_v_w, L0_ffn_sel_o_w, L0_ffn_route_scale, L1_xattn_Wqkv, L1_xattn_bqkv, L1_xattn_Wo, L1_xattn_bo, L1_xattn_Wq_c, L1_xattn_Wkv_c, L1_xattn_Wo_c, L1_xattn_Wg, L1_xattn_Wu, L1_xattn_Wd, L1_xattn_n1, L1_xattn_n2, L1_xattn_n3, L1_xattn_nf, L1_ffn_ln_g, L1_ffn_ln_b, L1_ffn_Wr, L1_ffn_W1, L1_ffn_W3, L1_ffn_W2, L1_ffn_W1s, L1_ffn_W3s, L1_ffn_W2s):
    import jax
    import jax.numpy as jnp

    def _L0_xattn_ref(q, k, v, igate_kernel, igate_bias, fgate_kernel, fgate_bias):
        import jax, jax.numpy as jnp
        import numpy as np
        EMB = 128
        NH = 8
        HD = EMB // NH
        EPS = 1e-06

        def _mlstm_head(q, k, v, ig, fg):
            S, DH = q.shape
            log_fg = jax.nn.log_sigmoid(fg)
            cs = jnp.concatenate([jnp.zeros((1, 1), q.dtype), jnp.cumsum(log_fg, axis=0)], axis=0)
            fg_mat_full = cs - cs.T
            ltr = jnp.tril(jnp.ones((S, S), bool))
            log_fg_matrix = jnp.where(ltr, fg_mat_full[1:, 1:], -jnp.inf)
            log_D = log_fg_matrix + ig.T
            max_log_D = jnp.max(log_D, axis=-1, keepdims=True)
            D = jnp.exp(log_D - max_log_D)
            qk = q @ (k.T / jnp.sqrt(jnp.asarray(DH, q.dtype)))
            C = qk * D
            normalizer = jnp.maximum(jnp.abs(C.sum(-1, keepdims=True)), jnp.exp(-max_log_D))
            return C / (normalizer + EPS) @ v
        B, S, H = q.shape
        x = jnp.concatenate([q, k, v], axis=-1)
        ig = x @ igate_kernel + igate_bias
        fg = x @ fgate_kernel + fgate_bias
        qh = q.reshape(B, S, NH, HD).swapaxes(1, 2)
        kh = k.reshape(B, S, NH, HD).swapaxes(1, 2)
        vh = v.reshape(B, S, NH, HD).swapaxes(1, 2)
        igp = ig.swapaxes(1, 2)[..., None]
        fgp = fg.swapaxes(1, 2)[..., None]
        h = jax.vmap(jax.vmap(_mlstm_head))(qh, kh, vh, igp, fgp)
        hf = h.astype(jnp.float32)
        h = (hf * jax.lax.rsqrt(jnp.mean(jnp.square(hf), axis=-1, keepdims=True) + 1e-06)).astype(h.dtype)
        return h.swapaxes(1, 2).reshape(B, S, H)

    def _L0_ffn_ref(x, q_w, k_w, v_w, o_w, sel_v_w, sel_o_w, route_scale):
        import jax, jax.numpy as jnp
        import numpy as np
        B, S, D = (2, 256, 128)
        H, E, P, K = (8, 8, 128, 2)
        SCALE = 1.0 / np.sqrt(P)

        def _get_sel_gate(x, w, route_scale):
            logits = jnp.einsum('bsd,ed->bse', x, w).astype(jnp.float32)
            raw = logits.reshape(x.shape[0], x.shape[1], H, E)
            probs = jax.nn.sigmoid(raw)
            vals, idx = jax.lax.top_k(probs, K)
            vals = vals / jnp.clip(vals.sum(-1, keepdims=True), 1e-09)
            vals = vals * route_scale
            gate = (jax.nn.one_hot(idx, E, dtype=vals.dtype) * vals[..., None]).sum(-2)
            return gate
        rs = route_scale[0]
        gate_v = _get_sel_gate(x, sel_v_w, rs)
        gate_o = _get_sel_gate(x, sel_o_w, rs)
        q = jnp.einsum('bsd,hpd->bhsp', x, q_w.reshape(H, P, D))
        k = jnp.einsum('bsd,hpd->bhsp', x, k_w.reshape(H, P, D))
        xv = jnp.einsum('bsd,hedp->bshep', x, v_w.reshape(H, E, D, P))
        v = jnp.einsum('bshep,bshe->bhsp', xv, gate_v)
        att = jax.nn.softmax(jnp.einsum('bhqp,bhkp->bhqk', q, k) * SCALE, axis=-1)
        ctx = jnp.einsum('bhqk,bhkp->bqhp', att, v)
        weighted = ctx[:, :, :, None, :] * gate_o[..., None]
        out = jnp.einsum('bshep,hepd->bsd', weighted, o_w.reshape(H, E, P, D))
        return out

    def _L1_xattn_ref(x, memory, seg_ids, Wqkv, bqkv, Wo, bo, Wq_c, Wkv_c, Wo_c, Wg, Wu, Wd, n1, n2, n3, nf):
        import jax, jax.numpy as jnp
        import numpy as np
        N_LAYERS = 4
        H = 16
        LOOKBACK = 128
        EPS = 1e-06
        ROPE_BASE = 10000.0
        NEG = jnp.float32(-1e+30)

        def rmsnorm(x, w):
            return x * jax.lax.rsqrt(jnp.mean(x * x, axis=-1, keepdims=True) + EPS) * w

        def rope_cache(L, hd):
            inv = 1.0 / ROPE_BASE ** (jnp.arange(0, hd, 2, dtype=jnp.float32) / hd)
            t = jnp.arange(L, dtype=jnp.float32)
            f = t[:, None] * inv[None, :]
            emb = jnp.concatenate([f, f], axis=-1)
            return (jnp.cos(emb), jnp.sin(emb))

        def apply_rope(x, cos, sin):
            d = x.shape[-1]
            x1, x2 = (x[..., :d // 2], x[..., d // 2:])
            rot = jnp.concatenate([-x2, x1], axis=-1)
            return x * cos + rot * sin

        def split_heads(x, n_heads):
            B, L, D = x.shape
            return x.reshape(B, L, n_heads, D // n_heads).transpose(0, 2, 1, 3)

        def merge_heads(x):
            B, h, L, d = x.shape
            return x.transpose(0, 2, 1, 3).reshape(B, L, h * d)

        def sdpa(q, k, v, bias):
            scale = q.shape[-1] ** (-0.5)
            s = jnp.einsum('bhqd,bhkd->bhqk', q, k) * scale + bias
            p = jax.nn.softmax(s, axis=-1)
            return jnp.einsum('bhqk,bhkd->bhqd', p, v)

        def forward(x, memory, seg_ids, Wqkv, bqkv, Wo, bo, Wq_c, Wkv_c, Wo_c, Wg, Wu, Wd, n1, n2, n3, nf):
            B, L, D = x.shape
            S = memory.shape[1]
            hd = D // H
            cos, sin = rope_cache(L, hd)
            i = jnp.arange(L)
            causal_bias = jnp.where(i[None, :] <= i[:, None], 0.0, NEG)[None, None]
            j = jnp.arange(S)
            allowed = (j[None, None, :] <= seg_ids[:, :, None]) & (j[None, None, :] > seg_ids[:, :, None] - LOOKBACK)
            cross_bias = jnp.where(allowed, 0.0, NEG)[:, None]
            for l in range(N_LAYERS):
                h = rmsnorm(x, n1[l])
                qkv = h @ Wqkv[l].T + bqkv[l]
                q, k, v = jnp.split(qkv, 3, axis=-1)
                q = apply_rope(split_heads(q, H), cos, sin)
                k = apply_rope(split_heads(k, H), cos, sin)
                v = split_heads(v, H)
                o = merge_heads(sdpa(q, k, v, causal_bias)) @ Wo[l].T + bo[l]
                x = x + o
                h2 = rmsnorm(x, n2[l])
                qc = split_heads(h2 @ Wq_c[l].T, H)
                kv = memory @ Wkv_c[l].T
                kc, vc = jnp.split(kv, 2, axis=-1)
                kc, vc = (split_heads(kc, H), split_heads(vc, H))
                oc = merge_heads(sdpa(qc, kc, vc, cross_bias)) @ Wo_c[l].T
                x = x + oc
                h3 = rmsnorm(x, n3[l])
                x = x + jax.nn.silu(h3 @ Wg[l].T) * (h3 @ Wu[l].T) @ Wd[l].T
            return rmsnorm(x, nf)
        return forward(x, memory, seg_ids, Wqkv, bqkv, Wo, bo, Wq_c, Wkv_c, Wo_c, Wg, Wu, Wd, n1, n2, n3, nf)

    def _L1_ffn_ref(x, ln_g, ln_b, Wr, W1, W3, W2, W1s, W3s, W2s):
        import jax, jax.numpy as jnp
        import numpy as np
        import math
        D_MODEL = 128
        D_FF = 512
        NUM_EXPERTS = 8
        NUM_SHARED = 1
        E_ROUTED = NUM_EXPERTS - NUM_SHARED
        TOP_K = 2
        CAP_FACTOR = 1.25
        B, S = (4, 256)
        T = B * S
        CAPACITY = math.ceil(CAP_FACTOR * T * TOP_K / E_ROUTED)
        SHARED_SCALE = 1.0

        def _layernorm(x, g, b, eps=1e-05):
            mu = jnp.mean(x, axis=-1, keepdims=True)
            var = jnp.mean((x - mu) ** 2, axis=-1, keepdims=True)
            return (x - mu) * jax.lax.rsqrt(var + eps) * g + b
        Bx, Sx, D = x.shape
        Tn = Bx * Sx
        h = _layernorm(x, ln_g, ln_b).reshape(Tn, D)
        logits = h @ Wr
        top_vals, top_idx = jax.lax.top_k(logits, TOP_K)
        gates = jax.nn.softmax(top_vals, axis=-1)
        idx = top_idx.T.reshape(-1)
        gat = gates.T.reshape(-1)
        tok = jnp.tile(jnp.arange(Tn), TOP_K)
        onehot = jax.nn.one_hot(idx, E_ROUTED, dtype=jnp.int32)
        pos = jnp.sum(jnp.cumsum(onehot, axis=0) * onehot, axis=-1) - 1
        keep = pos < CAPACITY
        pos_c = jnp.where(keep, pos, CAPACITY)
        xe = jnp.zeros((E_ROUTED, CAPACITY, D), h.dtype).at[idx, pos_c].set(h[tok], mode='drop')
        a = jnp.einsum('ecd,edf->ecf', xe, W1)
        b = jnp.einsum('ecd,edf->ecf', xe, W3)
        ye = jnp.einsum('ecf,efd->ecd', jax.nn.silu(a) * b, W2)
        out_slots = ye[jnp.clip(idx, 0, E_ROUTED - 1), jnp.clip(pos_c, 0, CAPACITY - 1)]
        out_slots = out_slots * (gat * keep.astype(gat.dtype))[:, None]
        routed = jnp.zeros((Tn, D), h.dtype).at[tok].add(out_slots)
        shared = jax.nn.silu(h @ W1s) * (h @ W3s) @ W2s
        out = routed + SHARED_SCALE * shared
        return out.reshape(Bx, Sx, D)
    x = x + jnp.tanh(g_xattn[0]) * _L0_xattn_ref(_layernorm(x, axis=-1), ctx_1024, ctx_1024, L0_xattn_igate_kernel, L0_xattn_igate_bias, L0_xattn_fgate_kernel, L0_xattn_fgate_bias)
    x = x + jnp.tanh(g_ffn[0]) * _L0_ffn_ref(_layernorm(x, axis=-1), L0_ffn_q_w, L0_ffn_k_w, L0_ffn_v_w, L0_ffn_o_w, L0_ffn_sel_v_w, L0_ffn_sel_o_w, L0_ffn_route_scale)
    x = x + jnp.tanh(g_xattn[1]) * _L1_xattn_ref(_layernorm(x, axis=-1), ctx_1024, itok_BxS_0_255, L1_xattn_Wqkv, L1_xattn_bqkv, L1_xattn_Wo, L1_xattn_bo, L1_xattn_Wq_c, L1_xattn_Wkv_c, L1_xattn_Wo_c, L1_xattn_Wg, L1_xattn_Wu, L1_xattn_Wd, L1_xattn_n1, L1_xattn_n2, L1_xattn_n3, L1_xattn_nf)
    x = x + jnp.tanh(g_ffn[1]) * _L1_ffn_ref(_layernorm(x, axis=-1), L1_ffn_ln_g, L1_ffn_ln_b, L1_ffn_Wr, L1_ffn_W1, L1_ffn_W3, L1_ffn_W2, L1_ffn_W1s, L1_ffn_W3s, L1_ffn_W2s)
    return x

_drawn_inputs = setup_inputs


def setup_inputs(seed=0):
    import zlib

    import numpy as np

    out = dict(_drawn_inputs(seed))
    spreads = {'g_ffn': (-1.0, 0.6),
     'L1_xattn_bqkv': (0.0, 0.1),
     'L1_xattn_bo': (0.0, 0.1),
     'L1_xattn_n1': (1.0, 0.6),
     'L1_xattn_n2': (1.0, 0.6),
     'L1_xattn_n3': (1.0, 0.6),
     'L1_xattn_nf': (1.0, 0.2),
     'L1_ffn_ln_g': (1.0, 0.6),
     'L1_ffn_ln_b': (0.0, 0.8)}
    factors = {'L0_xattn_igate_bias': 64.0,
     'L0_xattn_fgate_kernel': 5.705,
     'L1_xattn_Wq_c': 8.0,
     'L1_ffn_Wr': 7.441,
     'L1_ffn_W1': 6.741,
     'L1_ffn_W3': 6.688,
     'L1_ffn_W2': 6.689,
     'L1_ffn_W1s': 3.83,
     'L1_ffn_W3s': 3.785,
     'L1_ffn_W2s': 3.786}
    for name, (base, spread) in spreads.items():
        noise = np.random.default_rng([zlib.crc32(name.encode()), seed]).standard_normal(out[name].shape)
        drawn = base * np.exp(spread * noise) if base else spread * noise
        out[name] = jnp.asarray(drawn.astype(out[name].dtype))
    for name, factor in factors.items():
        out[name] = (out[name] * factor).astype(out[name].dtype)
    return out
```

```python
import concourse.bass as bass
from concourse import mybir
from contextlib import ExitStack

FP32 = mybir.dt.float32
BF16 = mybir.dt.bfloat16
ALU = mybir.AluOpType
ACT = mybir.ActivationFunctionType
AX = mybir.AxisListType

P = 128
B, S, D = 8, 256, 128
TB = S // P
NT = B * TB
NTOK = B * S
NEG = -1e30
CAPACITY = 366
LAYERS = 4


class Memory:

    def __init__(self, nc, stack):
        self.nc, self.stack = nc, stack

    def sb(self, name, shape, dtype=FP32):
        return self.stack.enter_context(self.nc.sbuf_tensor(name, shape, dtype))

    def bank(self, name, dtype=FP32, cols=512):
        return self.stack.enter_context(self.nc.psum_tensor(name, [P, cols], dtype))

    def sem(self, name):
        return self.stack.enter_context(self.nc.semaphore(name))


def load_inputs(nc, k, io):
    with ExitStack() as stack:
        m = Memory(nc, stack)
        C = m.sb("ctx_natural", [P, NT, D])
        graw = m.sb("graw", [P, 4])
        banks = [m.bank(f"ctxT_bank{i}") for i in range(4)]
        x_in, ctx_in, g_in = m.sem("x_in"), m.sem("ctx_in"), m.sem("g_in")
        const_made, transposed = m.sem("const_made"), m.sem("ctx_transposed")
        block = stack.enter_context(nc.Block())

        @block.sync
        def _(sp):
            sp.dma_start(C[:], io["ctx_1024"].rearrange("b (t p) d -> p (b t) d", p=P)).then_inc(ctx_in, 16)
            sp.dma_start(k.X[:], io["x"].rearrange("b (t p) d -> p (b t) d", p=P)).then_inc(x_in, 16)
            sp.dma_start(graw[:, 0:2], io["g_xattn"].rearrange("(a n) -> a n", a=1).broadcast_to([P, 2])).then_inc(g_in, 16)
            sp.dma_start(graw[:, 2:4], io["g_ffn"].rearrange("(a n) -> a n", a=1).broadcast_to([P, 2])).then_inc(g_in, 16)
            sp.wait_ge(x_in, 16)

        @block.gpsimd
        def _(pool):
            nc.gpsimd.memset(k.ident[:], 0.0)
            nc.gpsimd.memset(k.ones[:], 1.0)
            nc.gpsimd.memset(k.minus_half[:], -0.5)
            for e in range(8):
                nc.gpsimd.memset(k.rev[:, e:e + 1], 8.0 - e)
            nc.gpsimd.memset(k.causal[:], 0.0)
            pool.drain()
            nc.gpsimd.affine_select(out=k.ident[:], in_=k.ident[:], compare_op=ALU.not_equal, fill=1.0,
                                    base=0, pattern=[[-1, P]], channel_multiplier=1)
            nc.gpsimd.affine_select(out=k.causal[:, 0, :], in_=k.causal[:, 0, :], compare_op=ALU.is_ge, fill=NEG,
                                    base=0, pattern=[[-1, P]], channel_multiplier=1)
            nc.gpsimd.affine_select(out=k.causal[:, 1, :], in_=k.causal[:, 1, :], compare_op=ALU.is_ge, fill=NEG,
                                    base=0, pattern=[[1, P]], channel_multiplier=-1)
            pool.drain()
            nc.gpsimd.tensor_copy(k.identb[:], k.ident[:])
            nc.gpsimd.tensor_copy(k.causalb[:], k.causal[:]).then_inc(const_made, 1)

        @block.tensor
        def _(pe):
            pe.wait_ge(const_made, 1)
            pe.wait_ge(ctx_in, 16)
            for t in range(NT):
                nc.tensor.transpose(banks[t // 4][:, t % 4 * P:t % 4 * P + P], C[:, t, :], k.ident[:]).then_inc(transposed, 1)

        @block.scalar
        def _(act):
            act.wait_ge(g_in, 32)
            nc.scalar.activation(k.gate[:], graw[:], ACT.Tanh)
            for c in range(4):
                act.wait_ge(transposed, 4 * c + 4)
                nc.scalar.activation(k.ctxT[:, 512 * c:512 * c + 512], banks[c][:], ACT.Copy)

        @block.vector
        def _(dve):
            nc.vector.memset(k.ctx_ones[:, :, :, 16:17], 1.0)
            dve.wait_ge(ctx_in, 16)
            nc.vector.tensor_copy(k.ctx_ones[:, :, :, 0:16], C[:].rearrange("p t (h d) -> p t h d", h=8))


def layer_norm(nc, k, src, dst, dstT=None, scale=None, shift=None, tag=""):
    with ExitStack() as stack:
        m = Memory(nc, stack)
        stats, mv, rstd = m.sb(tag + "stats", [P, NT, 6]), m.sb(tag + "mv", [P, NT, 2]), m.sb(tag + "rstd", [P, NT])
        banks = [m.bank(f"{tag}nT_bank{i}") for i in range(4)]
        var_ready, rstd_ready, normed, transposed = (m.sem(tag + n) for n in ("var_ready", "rstd_ready", "normed", "transposed"))
        block = stack.enter_context(nc.Block())

        @block.vector
        def _(dve):
            for t in range(NT):
                nc.vector.bn_stats(stats[:, t, :], src[:, t, :])
            dve.drain()
            for t in range(NT):
                nc.vector.bn_aggr(mv[:, t, :], stats[:, t, :])
            dve.drain()
            nc.vector.tensor_scalar(mv[:, :, 1], mv[:, :, 1], 1e-5, None, ALU.add).then_inc(var_ready, 1)
            dve.wait_ge(rstd_ready, 1)
            for t in range(NT):
                nc.vector.tensor_scalar(dst[:, t, :], src[:, t, :], mv[:, t, 0:1], rstd[:, t:t + 1],
                                        ALU.subtract, ALU.mult).then_inc(normed, 1)

        @block.gpsimd
        def _(pool):
            pool.wait_ge(var_ready, 1)
            nc.gpsimd.tensor_tensor(rstd[:], mv[:, :, 1], k.minus_half[:, 0:NT], ALU.pow).then_inc(rstd_ready, 1)

        if dstT is not None:
            @block.tensor
            def _(pe):
                for t in range(NT):
                    pe.wait_ge(normed, t + 1)
                    nc.tensor.transpose(banks[t // 4][:, t % 4 * P:t % 4 * P + P], dst[:, t, :], k.ident[:]).then_inc(transposed, 1)

            @block.scalar
            def _(act):
                for c in range(4):
                    act.wait_ge(transposed, 4 * c + 4)
                    if scale is None:
                        nc.scalar.activation(dstT[:, 512 * c:512 * c + 512], banks[c][:], ACT.Copy)
                    else:
                        nc.scalar.activation(dstT[:, 512 * c:512 * c + 512], banks[c][:], ACT.Identity,
                                             scale=scale, bias=shift)


def mlstm(nc, k, io):
    NH, HD = 8, 16
    with ExitStack() as stack:
        m = Memory(nc, stack)
        Xn, XnT = m.sb("m_Xn", [P, NT, D]), m.sb("m_XnT", [P, NTOK])
        layer_norm(nc, k, k.X, Xn, XnT, tag="m_")
        neg_max, aT, enT = m.sb("neg_max", [NH, NTOK]), m.sb("aT", [P, NT, NH]), m.sb("enT", [P, NT, NH])
        sel = m.sb("sel", [NH, NH, P])
        mlstm_gates(nc, k, io, XnT, neg_max, aT, enT, sel)
        HO = m.sb("HO", [P, NT, NH, HD + 1])
        mlstm_heads(nc, k, io, XnT, neg_max, aT, sel, HO)
        mlstm_finish(nc, k, enT, HO)


def mlstm_gates(nc, k, io, XnT, neg_max, aT, enT, sel):
    NH = 8
    with ExitStack() as stack:
        m = Memory(nc, stack)
        wi, wf = m.sb("wi", [P, 3, NH]), m.sb("wf", [P, 3, NH])
        bi, bf = m.sb("bi", [NH, 1]), m.sb("bf", [NH, 1])
        IG, F, T, CS, A, M = (m.sb("g_" + n, [NH, NTOK]) for n in ("IG", "F", "T", "CS", "A", "M"))
        banks = [m.bank(f"gate_bank{i}") for i in range(8)]
        w_in, projected, pre_ready, abs_ready, log_ready = (m.sem("mg_" + n) for n in ("w_in", "projected", "pre_ready", "abs_ready", "log_ready"))
        a_ready, sum_ready, en_ready, transposed = (m.sem("mg_" + n) for n in ("a_ready", "sum_ready", "en_ready", "transposed"))
        block = stack.enter_context(nc.Block())

        @block.sync
        def _(sp):
            sp.dma_start(wi[:], io["L0_xattn_igate_kernel"].rearrange("(c p) n -> p c n", p=P)).then_inc(w_in, 16)
            sp.dma_start(wf[:], io["L0_xattn_fgate_kernel"].rearrange("(c p) n -> p c n", p=P)).then_inc(w_in, 16)
            sp.dma_start(bi[:], io["L0_xattn_igate_bias"].rearrange("(n a) -> n a", a=1)).then_inc(w_in, 16)
            sp.dma_start(bf[:], io["L0_xattn_fgate_bias"].rearrange("(n a) -> n a", a=1)).then_inc(w_in, 16)

        @block.gpsimd
        def _(pool):
            nc.gpsimd.memset(sel[:], 0.0)
            pool.drain()
            nc.gpsimd.affine_select(out=sel[:], in_=sel[:], compare_op=ALU.not_equal, fill=1.0,
                                    base=0, pattern=[[-1, NH], [0, P]], channel_multiplier=1)

        @block.tensor
        def _(pe):
            pe.wait_ge(w_in, 64)
            for c in range(4):
                for g, w in enumerate((wi, wf)):
                    for part, src in enumerate((XnT, k.ctxT, k.ctxT)):
                        last = nc.tensor.matmul(banks[4 * g + c][0:NH, :], w[:, part, :], src[:, 512 * c:512 * c + 512],
                                                start=part == 0, stop=part == 2)
                    last.then_inc(projected, 1)
            pe.wait_ge(a_ready, 1)
            pe.wait_ge(en_ready, 1)
            for t in range(NT):
                nc.tensor.transpose(banks[0][:, NH * t:NH * t + NH], A[:, P * t:P * t + P], k.ident[0:NH, 0:NH])
                last = nc.tensor.transpose(banks[1][:, NH * t:NH * t + NH], M[:, P * t:P * t + P], k.ident[0:NH, 0:NH])
            last.then_inc(transposed, 1)

        @block.scalar
        def _(act):
            for c in range(4):
                act.wait_ge(projected, 2 * c + 2)
                nc.scalar.activation(IG[:, 512 * c:512 * c + 512], banks[c][0:NH, :], ACT.Identity, bias=bi[:, 0:1])
                nc.scalar.activation(F[:, 512 * c:512 * c + 512], banks[4 + c][0:NH, :], ACT.Identity, bias=bf[:, 0:1]).then_inc(pre_ready, 1)
            act.wait_ge(abs_ready, 1)
            nc.scalar.activation(T[:], T[:], ACT.Exp, scale=-1.0)
            act.drain()
            nc.scalar.activation(T[:], T[:], ACT.Ln, bias=k.ones[0:NH, 0:1]).then_inc(log_ready, 1)
            act.wait_ge(sum_ready, 1)
            nc.scalar.activation(M[:], CS[:], ACT.Exp, scale=-1.0).then_inc(en_ready, 1)

        @block.vector
        def _(dve):
            dve.wait_ge(pre_ready, 4)
            nc.vector.scalar_tensor_tensor(T[:], F[:], -1.0, F[:], ALU.mult, ALU.max).then_inc(abs_ready, 1)
            dve.wait_ge(log_ready, 1)
            nc.vector.scalar_tensor_tensor(F[:], F[:], 0.0, T[:], ALU.min, ALU.subtract)
            dve.drain()
            for b in range(B):
                row = slice(S * b, S * b + S)
                nc.vector.tensor_tensor_scan(CS[:, row], k.ones[0:NH, 0:S], F[:, row], 0.0, ALU.mult, ALU.add)
            dve.drain()
            nc.vector.tensor_tensor(A[:], IG[:], CS[:], ALU.subtract).then_inc(a_ready, 1)
            dve.drain()
            for b in range(B):
                row = slice(S * b, S * b + S)
                nc.vector.tensor_tensor_scan(M[:, row], A[:, row], A[:, row], -3e38, ALU.max, ALU.max)
            dve.drain()
            nc.vector.tensor_scalar(neg_max[:], M[:], -1.0, None, ALU.mult)
            nc.vector.tensor_tensor(CS[:], CS[:], M[:], ALU.add).then_inc(sum_ready, 1)
            dve.wait_ge(transposed, 1)
            nc.vector.tensor_copy(aT[:].rearrange("p t h -> p (t h)"), banks[0][:, 0:NT * NH])
            nc.vector.tensor_copy(enT[:].rearrange("p t h -> p (t h)"), banks[1][:, 0:NT * NH])


def mlstm_heads(nc, k, io, XnT, neg_max, aT, sel, HO):
    NH, HD = 8, 16
    W = S + P
    with ExitStack() as stack:
        m = Memory(nc, stack)
        q16, k16 = m.sb("q16", [HD, NH, S]), m.sb("k16", [HD, NH, S])
        a_now = m.sb("a_now", [P, TB, NH])
        DT, CT = m.sb("DT", [P, 2, W]), m.sb("CT", [P, 2, W])
        sc = [m.bank(f"mh_sc{i}") for i in range(2)]
        ex = [m.bank(f"mh_ex{i}") for i in range(2)]
        ob = m.bank("mh_out")
        split, scored, exponents, decayed, weighted, summed, stored = (
            m.sem("mh_" + n) for n in ("split", "scored", "exponents", "decayed", "weighted", "summed", "stored"))
        block = stack.enter_context(nc.Block())

        @block.sync
        def _(sp):
            def bring(b):
                for h in range(NH):
                    sp.dma_start(q16[:, h, :], XnT[HD * h:HD * h + HD, bass.ds(b * S, S)]).then_inc(split, 16)
                    sp.dma_start(k16[:, h, :], k.ctxT[HD * h:HD * h + HD, bass.ds(b * S, S)]).then_inc(split, 16)
            bring(0)
            sp.dma_start(k.v_w[:], io["L0_ffn_v_w"].rearrange("e d p -> d e p")).then_inc(k.experts_in, 16)
            sp.dma_start(k.o_w[:], io["L0_ffn_o_w"].rearrange("e p d -> p e d")).then_inc(k.experts_in, 16)
            with sp.Fori(1, B) as b:
                sp.wait_ge(scored, b * NH)
                bring(b)

        @block.tensor
        def _(pe):
            with pe.Fori(0, B) as b:
                pe.wait_ge(split, b * (32 * NH) + 32 * NH)

                def scores(h):
                    if h >= 2:
                        pe.wait_ge(weighted, b * NH + (h - 1))
                    nc.tensor.matmul(sc[h % 2][:, 0:S], k16[:, h, 0:P], q16[:, h, :], start=True, stop=True)
                    nc.tensor.matmul(sc[h % 2][:, S:W], k16[:, h, P:S], q16[:, h, P:S], start=True, stop=True).then_inc(scored, 1)
                    nc.tensor.matmul(ex[h % 2][:, 0:S], sel[:, h, :], neg_max[:, bass.ds(b * S, S)], start=True, stop=False)
                    nc.tensor.matmul(ex[h % 2][:, 0:P], k.identb[:], k.causalb[:, 1, :], start=False, stop=True)
                    nc.tensor.matmul(ex[h % 2][:, S:W], sel[:, h, :], neg_max[:, bass.ds(b * S + P, P)], start=True, stop=False)
                    nc.tensor.matmul(ex[h % 2][:, S:W], k.identb[:], k.causalb[:, 1, :], start=False, stop=True).then_inc(exponents, 1)

                scores(0)
                for h in range(NH):
                    if h + 1 < NH:
                        scores(h + 1)
                    pe.wait_ge(weighted, b * NH + (h + 1))
                    c = CT[:, h % 2, :]
                    v = lambda jt: k.ctx_ones[:, bass.ds(b * TB + jt, 1), h, :].rearrange("p a d -> p (a d)")
                    o = lambda t: ob[:, (t * NH + h) * (HD + 1):(t * NH + h + 1) * (HD + 1)]
                    nc.tensor.matmul(o(0), c[:, 0:P], v(0), start=True, stop=True)
                    nc.tensor.matmul(o(1), c[:, P:S], v(0), start=True, stop=False)
                    nc.tensor.matmul(o(1), c[:, S:W], v(1), start=False, stop=True).then_inc(summed, 1)
                pe.wait_ge(stored, b + 1)

        @block.scalar
        def _(act):
            with act.Fori(0, B) as b:
                nc.scalar.activation(a_now[:], aT[:, bass.ds(b * TB, TB), :], ACT.Copy)
                act.drain()
                for h in range(NH):
                    act.wait_ge(exponents, b * NH + (h + 1))
                    if h >= 2:
                        act.wait_ge(weighted, b * NH + (h - 1))
                    nc.scalar.activation(DT[:, h % 2, 0:S], ex[h % 2][:, 0:S], ACT.Exp, bias=a_now[:, 0, h:h + 1])
                    nc.scalar.activation(DT[:, h % 2, S:W], ex[h % 2][:, S:W], ACT.Exp, bias=a_now[:, 1, h:h + 1]).then_inc(decayed, 1)
                act.wait_ge(summed, b * NH + NH)
                nc.scalar.activation(HO[:, bass.ds(b * TB, TB), :, :].rearrange("p t h d -> p (t h d)"), ob[:, 0:TB * NH * (HD + 1)], ACT.Copy).then_inc(stored, 1)

        @block.vector
        def _(dve):
            with dve.Fori(0, B) as b:
                for h in range(NH):
                    dve.wait_ge(decayed, b * NH + (h + 1))
                    if h >= 2:
                        dve.wait_ge(summed, b * NH + (h - 1))
                    nc.vector.scalar_tensor_tensor(CT[:, h % 2, :], sc[h % 2][:, 0:W], HD ** -0.5, DT[:, h % 2, :],
                                                   ALU.mult, ALU.mult).then_inc(weighted, 1)


def mlstm_finish(nc, k, enT, HO):
    NH, HD = 8, 16
    G = NT * NH
    with ExitStack() as stack:
        m = Memory(nc, stack)
        den, ms, rms = m.sb("den", [P, G]), m.sb("ms", [P, G]), m.sb("rms", [P, G])
        Hn, SQ = m.sb("Hn", [P, G, HD]), m.sb("SQ", [P, G, HD])
        ms_ready, rms_ready = m.sem("ms_ready"), m.sem("rms_ready")
        block = stack.enter_context(nc.Block())
        ho = HO[:].rearrange("p t h d -> p (t h) d")

        @block.vector
        def _(dve):
            nc.vector.scalar_tensor_tensor(den[:], ho[:, :, HD], -1.0, ho[:, :, HD], ALU.mult, ALU.max)
            dve.drain()
            nc.vector.tensor_tensor(den[:], den[:], enT[:].rearrange("p t h -> p (t h)"), ALU.max)
            dve.drain()
            nc.vector.tensor_scalar(den[:], den[:], 1e-6, None, ALU.add)
            dve.drain()
            nc.vector.reciprocal(den[:], den[:])
            dve.drain()
            nc.vector.tensor_tensor(Hn[:], ho[:, :, 0:HD], den[:].unsqueeze(2).broadcast_to([P, G, HD]), ALU.mult)
            dve.drain()
            nc.vector.tensor_tensor(SQ[:], Hn[:], Hn[:], ALU.mult)
            dve.drain()
            nc.vector.tensor_reduce(ms[:], SQ[:], AX.X, ALU.add)
            dve.drain()
            nc.vector.tensor_scalar(ms[:], ms[:], 1.0 / HD, 1e-6, ALU.mult, ALU.add).then_inc(ms_ready, 1)
            dve.wait_ge(rms_ready, 1)
            nc.vector.tensor_tensor(Hn[:], Hn[:], rms[:].unsqueeze(2).broadcast_to([P, G, HD]), ALU.mult)
            dve.drain()
            x = k.X[:].rearrange("p t d -> p (t d)")
            nc.vector.scalar_tensor_tensor(x, Hn[:].rearrange("p g d -> p (g d)"), k.gate[:, 0:1], x, ALU.mult, ALU.add)

        @block.gpsimd
        def _(pool):
            pool.wait_ge(ms_ready, 1)
            nc.gpsimd.tensor_tensor(rms[:], ms[:], k.minus_half[:, 0:G], ALU.pow).then_inc(rms_ready, 1)


def top_two(nc, dve, p, one1, one2, m1, m2, scratch, first, rev, groups, n):
    def wide(a):
        return a.unsqueeze(2).broadcast_to([P, groups, n])
    rank = rev[:, 0:n].unsqueeze(1).broadcast_to([P, groups, n])
    for values, peak, one in ((p, m1, one1), (scratch, m2, one2)):
        if one is one2:
            nc.vector.scalar_tensor_tensor(scratch, one1, NEG, p, ALU.mult, ALU.add)
            dve.drain()
        nc.vector.tensor_reduce(peak, values, AX.X, ALU.max)
        dve.drain()
        nc.vector.tensor_tensor(scratch, values, wide(peak), ALU.is_equal)
        dve.drain()
        nc.vector.tensor_tensor(scratch, scratch, rank, ALU.mult)
        dve.drain()
        nc.vector.tensor_reduce(first, scratch, AX.X, ALU.max)
        dve.drain()
        nc.vector.tensor_tensor(one, rank, wide(first), ALU.is_equal)
        dve.drain()


def switch_head(nc, k, io):
    NH, E = 8, 8
    with ExitStack() as stack:
        m = Memory(nc, stack)
        Xn, XnT = m.sb("s_Xn", [P, NT, D]), m.sb("s_XnT", [P, NTOK])
        layer_norm(nc, k, k.X, Xn, XnT, tag="s_")
        G = m.sb("router_gates", [P, NT, 2, NH, E])
        QK = m.sb("QK", [P, NH, P])
        with ExitStack() as inner:
            switch_gates(nc, k, io, Memory(nc, inner), XnT, G, QK)
        switch_attention(nc, k, io, XnT, G, QK, Xn)
        with ExitStack() as inner:
            block = inner.enter_context(nc.Block())

            @block.vector
            def _(dve):
                nc.vector.scalar_tensor_tensor(k.X[:], Xn[:], k.gate[:, 2:3], k.X[:], ALU.mult, ALU.add)


def switch_gates(nc, k, io, m, XnT, G, QK):
    NH, E = 8, 8
    groups = NT * 2 * NH
    sel, selT = m.sb("sel_w", [P, D]), m.sb("sel_wT", [P, P])
    qn, kn = m.sb("q_w", [P, NH, D]), m.sb("k_w", [P, NH, D])
    prob, one1, one2, scratch = (m.sb("sg_" + n, [P, groups, E]) for n in ("prob", "one1", "one2", "scratch"))
    m1, m2, first, scale = (m.sb("sg_" + n, [P, groups]) for n in ("m1", "m2", "first", "scale"))
    rs = m.sb("route_scale", [P, 1])
    banks = [m.bank(f"sg_bank{i}") for i in range(4)]
    tb = m.bank("sg_selT")
    qk_bank = [m.bank(f"sg_qk{i}") for i in range(2)]
    w_in, sel_t, sel_c, qk_made, logits, exped = (m.sem("sg_" + n) for n in ("w_in", "sel_t", "sel_c", "qk_made", "logits", "exped"))
    block = m.stack.enter_context(nc.Block())

    @block.sync
    def _(sp):
        sp.dma_start(sel[0:64, :], io["L0_ffn_sel_v_w"]).then_inc(w_in, 16)
        sp.dma_start(sel[64:128, :], io["L0_ffn_sel_o_w"]).then_inc(w_in, 16)
        sp.dma_start(rs[:], io["L0_ffn_route_scale"].rearrange("(a n) -> a n", a=1).broadcast_to([P, 1])).then_inc(w_in, 16)
        sp.dma_start(qn[:], io["L0_ffn_q_w"].rearrange("(h p) d -> p h d", p=P)).then_inc(w_in, 16)
        sp.dma_start(kn[:], io["L0_ffn_k_w"].rearrange("(h p) d -> p h d", p=P)).then_inc(w_in, 16)

    @block.tensor
    def _(pe):
        pe.wait_ge(w_in, 80)
        nc.tensor.transpose(tb[:, 0:P], sel[:], k.ident[:]).then_inc(sel_t, 1)
        pe.wait_ge(sel_c, 1)
        for t in range(NT):
            nc.tensor.matmul(banks[t // 4][:, t % 4 * P:t % 4 * P + P], XnT[:, P * t:P * t + P], selT[:],
                             start=True, stop=True).then_inc(logits, 1)
        for h in range(NH):
            nc.tensor.matmul(qk_bank[h // 4][:, h % 4 * P:h % 4 * P + P], qn[:, h, :], kn[:, h, :],
                             start=True, stop=True).then_inc(qk_made, 1)

    @block.scalar
    def _(act):
        act.wait_ge(sel_t, 1)
        nc.scalar.activation(selT[:], tb[:, 0:P], ACT.Copy).then_inc(sel_c, 1)
        flat = prob[:].rearrange("p g e -> p (g e)")
        for c in range(4):
            act.wait_ge(logits, 4 * c + 4)
            nc.scalar.activation(flat[:, 512 * c:512 * c + 512], banks[c][:], ACT.Exp, scale=-1.0).then_inc(exped, 1)
        for c in range(2):
            act.wait_ge(qk_made, 4 * c + 4)
            nc.scalar.activation(QK[:, 4 * c:4 * c + 4, :].rearrange("p h d -> p (h d)"), qk_bank[c][:], ACT.Copy)

    @block.vector
    def _(dve):
        dve.wait_ge(exped, 4)
        nc.vector.tensor_scalar(prob[:], prob[:], 1.0, None, ALU.add)
        dve.drain()
        nc.vector.reciprocal(prob[:], prob[:])
        dve.drain()
        top_two(nc, dve, prob[:], one1[:], one2[:], m1[:], m2[:], scratch[:], first[:], k.rev, groups, E)
        nc.vector.tensor_tensor(scale[:], m1[:], m2[:], ALU.add)
        dve.drain()
        nc.vector.tensor_scalar(scale[:], scale[:], 1e-9, None, ALU.max)
        dve.drain()
        nc.vector.reciprocal(scale[:], scale[:])
        nc.vector.tensor_tensor(one1[:], one1[:], one2[:], ALU.add)
        dve.drain()
        dve.wait_ge(w_in, 80)
        nc.vector.tensor_scalar(scale[:], scale[:], rs[:, 0:1], None, ALU.mult)
        nc.vector.tensor_tensor(prob[:], prob[:], one1[:], ALU.mult)
        dve.drain()
        nc.vector.tensor_tensor(G[:].rearrange("p t c h e -> p (t c h) e"), prob[:],
                                scale[:].unsqueeze(2).broadcast_to([P, groups, E]), ALU.mult)


def switch_attention(nc, k, io, XnT, G, QK, out):
    NH, E = 8, 8
    STEPS = 4 * NH
    with ExitStack() as stack:
        m = Memory(nc, stack)
        xb, zT, prob, probT, cT = m.sb("xb", [P, S]), m.sb("zT", [P, S]), m.sb("sa_prob", [P, TB, S]), m.sb("sa_probT", [P, TB, S]), m.sb("cT", [P, S])
        values, rec = m.sb("sa_values", [P, TB, P]), m.sb("sa_rec", [P, TB])
        neg_max, total, wo = m.sb("sa_neg_max", [P, TB]), m.sb("sa_total", [P, TB]), m.sb("sa_wo", [P, TB, E])
        product = m.sb("sa_product", [P, 2, E, P])
        pair = [m.bank(f"sa_pair{i}", cols=1024) for i in range(2)]
        sb_, tb_, zb_, cb_ = m.bank("sa_scores"), m.bank("sa_probT_bank"), m.bank("sa_z_bank"), m.bank("sa_ctx_bank")
        sem = lambda n: m.sem("sa_" + n)
        xb_ready, z_made, z_copied, scored, maxed = (sem(n) for n in ("xb_ready", "z_made", "z_copied", "scored", "maxed"))
        exped, turned, turn_copied, ctx_made, ctx_copied = (sem(n) for n in ("exped", "turned", "turn_copied", "ctx_made", "ctx_copied"))
        pair_made, product_made, product_free, values_ready = (sem(n) for n in ("pair_made", "product_made", "product_free", "values_ready"))
        block = stack.enter_context(nc.Block())

        @block.tensor
        def _(pe):
            pe.wait_ge(k.experts_in, k.EXPERTS_IN)
            with pe.Fori(0, B) as b:
                pe.wait_ge(xb_ready, b + 1)

                def z(h):
                    nc.tensor.matmul(zb_[:, 0:S], QK[:, h, :], xb[:], start=True, stop=True).then_inc(z_made, 1)

                def scores(h):
                    pe.wait_ge(z_copied, b * NH + (h + 1))
                    for t in range(TB):
                        last = nc.tensor.matmul(sb_[:, S * t:S * t + S], zT[:, P * t:P * t + P], xb[:], start=True, stop=True)
                    last.then_inc(scored, 1)

                def experts(n, lhsT, w, h):
                    pe.wait_ge(product_made, b * STEPS + (n + 1))
                    for half in range(2):
                        last = nc.tensor.matmul(pair[n % 2][:, 512 * half:512 * half + 512], lhsT,
                                                w[:, E * h + 4 * half:E * h + 4 * half + 4, :].rearrange("p e d -> p (e d)"),
                                                start=True, stop=True)
                    last.then_inc(pair_made, 1)
                    return last

                z(0)
                scores(0)
                for h in range(NH):
                    for t in range(TB):
                        last = experts(4 * h + t, xb[:, P * t:P * t + P], k.v_w, h)
                    pe.wait_ge(exped, b * NH + (h + 1))
                    for kt in range(TB):
                        for t in range(TB):
                            last = nc.tensor.transpose(tb_[:, S * kt + P * t:S * kt + P * t + P], prob[:, t, P * kt:P * kt + P], k.ident[:])
                    last.then_inc(turned, 1)
                    if h + 1 < NH:
                        z(h + 1)
                    pe.wait_ge(turn_copied, b * NH + (h + 1))
                    pe.wait_ge(values_ready, b * (2 * NH) + (2 * h + 2))
                    for kt in range(TB):
                        last = nc.tensor.matmul(cb_[:, 0:S], values[:, kt, :], probT[:, kt, :], start=kt == 0, stop=kt == 1)
                    last.then_inc(ctx_made, 1)
                    if h + 1 < NH:
                        scores(h + 1)
                    pe.wait_ge(ctx_copied, b * NH + (h + 1))
                    for t in range(TB):
                        last = experts(4 * h + 2 + t, cT[:, P * t:P * t + P], k.o_w, h)

        @block.scalar
        def _(act):
            with act.Fori(0, B) as b:
                nc.scalar.activation(xb[:], XnT[:, bass.ds(b * S, S)], ACT.Copy).then_inc(xb_ready, 1)

                def copy_z(h):
                    act.wait_ge(z_made, b * NH + (h + 1))
                    nc.scalar.activation(zT[:], zb_[:, 0:S], ACT.Copy, scale=float(P) ** -0.5).then_inc(z_copied, 1)

                def exps(h):
                    act.wait_ge(maxed, b * NH + (h + 1))
                    for t in range(TB):
                        last = nc.scalar.activation(prob[:, t, :], sb_[:, S * t:S * t + S], ACT.Exp, bias=neg_max[:, t:t + 1],
                                                    accum_out=total[:, t:t + 1])
                    last.then_inc(exped, 1)

                copy_z(0)
                exps(0)
                for h in range(NH):
                    act.wait_ge(turned, b * NH + (h + 1))
                    nc.scalar.activation(probT[:].rearrange("p a s -> p (a s)"), tb_[:], ACT.Copy).then_inc(turn_copied, 1)
                    if h + 1 < NH:
                        copy_z(h + 1)
                    act.wait_ge(ctx_made, b * NH + (h + 1))
                    nc.scalar.activation(cT[:], cb_[:, 0:S], ACT.Copy).then_inc(ctx_copied, 1)
                    if h + 1 < NH:
                        exps(h + 1)

        @block.vector
        def _(dve):
            dve.sem_inc(product_made, 2)
            with dve.Fori(0, B) as b:
                def find_max(h):
                    dve.wait_ge(scored, b * NH + (h + 1))
                    nc.vector.tensor_reduce(neg_max[:], sb_[:].rearrange("p (t s) -> p t s", t=TB), AX.X, ALU.max,
                                            negate=True).then_inc(maxed, 1)

                def gated(n, gate):
                    dve.wait_ge(pair_made, b * STEPS + (n + 1))
                    dve.wait_ge(product_free, b * STEPS + (n + 1))
                    nc.vector.tensor_tensor(product[:, n % 2, :, :], pair[n % 2][:].rearrange("p (e d) -> p e d", e=E),
                                            gate.unsqueeze(2).broadcast_to([P, E, P]), ALU.mult).then_inc(product_made, 1)

                find_max(0)
                for h in range(NH):
                    for t in range(TB):
                        gated(4 * h + t, G[:, bass.ds(b * TB + t, 1), 0, h, :].rearrange("p a e -> p (a e)"))
                    dve.wait_ge(exped, b * NH + (h + 1))
                    nc.vector.reciprocal(rec[:], total[:])
                    dve.drain()
                    for t in range(TB):
                        nc.vector.tensor_scalar(wo[:, t, :], G[:, bass.ds(b * TB + t, 1), 1, h, :].rearrange("p a e -> p (a e)"),
                                                rec[:, t:t + 1], None, ALU.mult)
                    if h + 1 < NH:
                        find_max(h + 1)
                    dve.drain()
                    for t in range(TB):
                        gated(4 * h + 2 + t, wo[:, t, :])

        @block.gpsimd
        def _(pool):
            pool.sem_inc(product_free, 2)
            with pool.Fori(0, B) as b:
                for n in range(STEPS):
                    h, t = n // 4, n % 2
                    pool.wait_ge(product_made, b * STEPS + (n + 3))
                    p = product[:, n % 2, :, :]
                    nc.gpsimd.tensor_tensor(p[:, 0:4, :], p[:, 0:4, :], p[:, 4:8, :], ALU.add)
                    pool.drain()
                    nc.gpsimd.tensor_tensor(p[:, 0:2, :], p[:, 0:2, :], p[:, 2:4, :], ALU.add)
                    pool.drain()
                    if n % 4 < 2:
                        nc.gpsimd.tensor_tensor(values[:, t, :], p[:, 0, :], p[:, 1, :], ALU.add).then_inc(values_ready, 1)
                        pool.drain().then_inc(product_free, 1)
                        continue
                    y = out[:, bass.ds(b * TB + t, 1), :].rearrange("p a d -> p (a d)")
                    if h == 0:
                        nc.gpsimd.tensor_tensor(y, p[:, 0, :], p[:, 1, :], ALU.add)
                    else:
                        nc.gpsimd.tensor_tensor(p[:, 0, :], p[:, 0, :], p[:, 1, :], ALU.add)
                        pool.drain()
                        nc.gpsimd.tensor_tensor(y, y, p[:, 0, :], ALU.add)
                    pool.drain().then_inc(product_free, 1)


WQ, WK, WV, WO_S, WQ_C, WK_C, WV_C, WO_C, WG, WU, WD = 0, 1, 2, 3, 4, 5, 6, 7, 8, 12, 16
BLOCKS = 20


def decoder(nc, k, io):
    with ExitStack() as stack:
        m = Memory(nc, stack)
        XX = m.sb("d_XX", [P, NT, D])
        layer_norm(nc, k, k.X, XX, tag="d_")
        c = DecoderConstants(m)
        decoder_constants(nc, k, io, c)
        decoder_layers(nc, k, io, c, XX)
        decoder_end(nc, k, c, XX)


class DecoderConstants:

    def __init__(self, m):
        self.cos, self.sin = m.sb("cos", [P, S]), m.sb("sin", [P, S])
        self.rot = m.sb("rot", [P, P])
        self.own = m.sb("own", [P, 4])
        self.blocked = m.sb("blocked", [P, NT, S], BF16)
        self.norms, self.bias_qk = m.sb("norms", [P, 3, LAYERS]), m.sb("bias_qk", [P, LAYERS, 2])
        self.bias_v, self.bias_o = m.sb("bias_v", [P, LAYERS, D]), m.sb("bias_o", [P, LAYERS, D])
        self.nf = m.sb("nf", [P, D])


def decoder_constants(nc, k, io, c):
    SCALE = 8 ** -0.5
    with ExitStack() as stack:
        m = Memory(nc, stack)
        ids, seg, low = m.sb("ids", [P, NT], mybir.dt.int32), m.sb("seg", [P, NT]), m.sb("low", [P, NT])
        jj, key = m.sb("jj", [P, S], mybir.dt.int32), m.sb("key", [P, S])
        above, below = m.sb("above", [P, NT, S]), m.sb("below", [P, NT, S])
        own = c.own
        loaded, iota_made = m.sem("dc_loaded"), m.sem("dc_iota_made")
        block = stack.enter_context(nc.Block())

        @block.sync
        def _(sp):
            def load(dst, src):
                sp.dma_start(dst, src).then_inc(loaded, 16)
            with nc.allow_non_contiguous_dma("small parameters, a column each"):
                load(ids[:], io["itok_BxS_0_255"].rearrange("b (t p) -> p (b t)", p=P))
                load(c.cos[:], io["rope_cos"])
                load(c.sin[:], io["rope_sin"])
                load(c.rot[:], io["rope_turn"])
                load(c.own[:], io["head_of_quadrant"])
                for i, n in enumerate(("n1", "n2", "n3")):
                    load(c.norms[:, i, :], io["L1_xattn_" + n].rearrange("l d -> d l"))
                for i in range(2):
                    load(c.bias_qk[:, :, i], io["L1_xattn_bqkv"][:, D * i:D * i + D].rearrange("l d -> d l"))
                load(c.bias_v[:], io["L1_xattn_bqkv"][:, 2 * D:3 * D].rearrange("(a l) d -> a l d", a=1).broadcast_to([P, LAYERS, D]))
                load(c.bias_o[:], io["L1_xattn_bo"].rearrange("(a l) d -> a l d", a=1).broadcast_to([P, LAYERS, D]))
                load(c.nf[:], io["L1_xattn_nf"].rearrange("(a d) -> a d", a=1).broadcast_to([P, D]))

        @block.gpsimd
        def _(pool):
            nc.gpsimd.iota(jj[:], pattern=[[1, S]], base=0, channel_multiplier=0)
            pool.drain()
            nc.gpsimd.tensor_copy(key[:], jj[:]).then_inc(iota_made, 1)

        @block.vector
        def _(dve):
            dve.wait_ge(loaded, 13 * 16)
            nc.vector.tensor_copy(seg[:], ids[:])
            nc.vector.tensor_scalar(c.bias_qk[:, :, 0], c.bias_qk[:, :, 0], SCALE, None, ALU.mult)
            dve.drain()
            nc.vector.tensor_scalar(low[:], seg[:], -128.0, None, ALU.add)
            dve.wait_ge(iota_made, 1)
            dve.drain()
            for t in range(NT):
                nc.vector.tensor_scalar(above[:, t, :], key[:], seg[:, t:t + 1], NEG, ALU.is_gt, ALU.mult)
                nc.vector.tensor_scalar(below[:, t, :], key[:], low[:, t:t + 1], NEG, ALU.is_le, ALU.mult)
            dve.drain()
            nc.vector.tensor_tensor(c.blocked[:], above[:], below[:], ALU.add)


def decoder_layers(nc, k, io, c, XX):
    NH, HD = 16, 8
    SCALE = HD ** -0.5
    W_LOADS = 8
    with ExitStack() as stack:
        m = Memory(nc, stack)
        WN, WT = m.sb("d_WN", [P, BLOCKS, P]), m.sb("d_WT", [P, BLOCKS, P])
        norm_w = m.sb("d_norm_w", [P, 3])
        bias = m.sb("d_bias", [P, 2])
        mem = m.sb("d_mem", [P, S])
        ss, r, h, hT = m.sb("d_ss", [P, TB]), m.sb("d_r", [P, TB]), m.sb("d_h", [P, TB, D]), m.sb("d_hT", [P, S])
        qk, turned_sin, qkr = m.sb("d_qk", [P, 2, S]), m.sb("d_turned_sin", [P, 2, S]), m.sb("d_qkr", [P, 2, S])
        qm = m.sb("d_qm", [P, 4, S])
        kc, qc = m.sb("d_kc", [P, S]), m.sb("d_qc", [P, S])
        V, VC = m.sb("d_V", [P, TB, NH, HD + 1]), m.sb("d_VC", [P, TB, NH, HD + 1])
        neg_max = m.sb("d_neg_max", [P, NH, TB])
        prob, probT = m.sb("d_prob", [P, 2, 512]), m.sb("d_probT", [P, 2, 512])
        rec, o, oT = m.sb("d_rec", [P, TB, NH]), m.sb("d_o", [P, TB, D]), m.sb("d_oT", [P, S])
        proj = m.sb("d_proj", [P, TB, D])
        tg, aT = m.sb("d_tg", [P, 4, S]), m.sb("d_aT", [P, 4, S])
        A = [m.bank(f"d_A{i}") for i in range(2)]
        T = [m.bank(f"d_T{i}") for i in range(2)]
        O = m.bank("d_O")
        G = [m.bank(f"d_G{i}") for i in range(3)]
        sem = lambda n: m.sem("dl_" + n)
        w_in, w_read, w_turned, w_ready, ones_set = (sem(n) for n in ("w_in", "w_read", "w_turned", "w_ready", "ones_set"))
        ss_ready, r_ready, h_ready, h_turned, hT_ready = (sem(n) for n in ("ss_ready", "r_ready", "h_ready", "h_turned", "hT_ready"))
        qk_made, qk_biased, qk_turned, roped, queries_ready = (sem(n) for n in ("qk_made", "qk_biased", "qk_turned", "roped", "queries_ready"))
        mem_ready, kc_made, kc_ready, vc_made, vc_ready, v_made, v_ready, qc_made, qc_ready = (
            sem(n) for n in ("mem_ready", "kc_made", "kc_ready", "vc_made", "vc_ready", "v_made", "v_ready", "qc_made", "qc_ready"))
        scored, maxed, exped, turned, turn_copied, attended = (sem(n) for n in ("scored", "maxed", "exped", "turned", "turn_copied", "attended"))
        o_ready, o_turned, oT_ready, projected = (sem(n) for n in ("o_ready", "o_turned", "oT_ready", "projected"))
        gated, upped, tanhed, act_ready, downed = (sem(n) for n in ("gated", "upped", "tanhed", "act_ready", "downed"))
        block = stack.enter_context(nc.Block())

        TILES = {0: [(0, 0, P, 0), (1, 0, S, P)], 1: [(0, 0, S, 0), (1, 0, S, S)]}
        WIDTH = {0: P + S, 1: 2 * S}

        def prob_blocks(kind):
            blocks = []
            for t, _, keys, col in TILES[kind]:
                for kt in range(keys // P):
                    blocks.append((t, kt, col + kt * P))
            blocks.sort(key=lambda b: (b[1], b[0]))
            return [(t, kt, col, i * P) for i, (t, kt, col) in enumerate(blocks)]

        @block.sync
        def _(sp):
            with sp.Fori(0, LAYERS) as l:
                sp.wait_ge(w_read, l + 1)
                def load(at, n, name, cols):
                    w = io["L1_xattn_" + name][bass.ds(l, 1)]
                    if cols:
                        src = w.rearrange("a p (c d) -> p (a c) d", c=n)
                    else:
                        src = w.rearrange("a (c p) d -> p (a c) d", c=n)
                    sp.dma_start(WN[:, at:at + n, :], src).then_inc(w_in, 16)
                load(WQ, 3, "Wqkv", False)
                load(WO_S, 1, "Wo", False)
                load(WQ_C, 1, "Wq_c", False)
                load(WK_C, 2, "Wkv_c", False)
                load(WO_C, 1, "Wo_c", False)
                load(WG, 4, "Wg", False)
                load(WU, 4, "Wu", False)
                load(WD, 4, "Wd", True)

        @block.tensor
        def _(pe):
            pe.sem_inc(w_read, 1)
            pe.wait_ge(ones_set, 1)
            with pe.Fori(0, LAYERS) as l:
                pe.wait_ge(w_in, l * (16 * W_LOADS) + 16 * W_LOADS)
                for g in range(BLOCKS // 4):
                    bank = (A + T + [O])[g]
                    for i in range(4):
                        last = nc.tensor.transpose(bank[:, P * i:P * i + P], WN[:, 4 * g + i, :], k.ident[:])
                    last.then_inc(w_turned, 1)
                pe.wait_ge(w_ready, l + 1)
                pe.sem_inc(w_read, 1)

                with pe.Fori(0, B) as b:
                    it = l * B + b

                    def turn_h(j):
                        pe.wait_ge(h_ready, it * 3 + (j + 1))
                        for t in range(TB):
                            last = nc.tensor.transpose(G[0][:, P * t:P * t + P], h[:, t, :], k.ident[:])
                        last.then_inc(h_turned, 1)
                        pe.wait_ge(hT_ready, it * 3 + (j + 1))

                    def attention(kind, keys, values, a):
                        n0 = it * (2 * NH) + a * NH

                        def scores(h):
                            j, g = h % 4, h // 4 * 32
                            bank = A[h % 2]
                            for t, k0, n, col in TILES[kind]:
                                nc.tensor.matmul(bank[:, col:col + n], qm[g:g + 32, j, P * t:P * t + P], keys[g:g + 32, k0:k0 + n],
                                                 start=True, stop=False)
                                if kind == 0:
                                    d = col + t * P
                                    last = nc.tensor.matmul(bank[:, d:d + P], k.identb[:], k.causalb[:, 0, :], start=False, stop=True)
                                else:
                                    last = nc.tensor.matmul(bank[:, col:col + n], k.identb[:],
                                                            c.blocked[:, bass.ds(b * TB + t, 1), :].rearrange("p a s -> p (a s)"),
                                                            start=False, stop=True)
                            last.then_inc(scored, 1)

                        def weighted(h):
                            pe.wait_ge(turn_copied, n0 + (h + 1))
                            for i, (t, kt, _, col) in enumerate(sorted(prob_blocks(kind))):
                                first, final = kt == 0, kt == (t if kind == 0 else 1)
                                last = nc.tensor.matmul(O[:, (t * NH + h) * (HD + 1):(t * NH + h + 1) * (HD + 1)],
                                                        probT[:, h % 2, col:col + P], values[:, kt, h, :], start=first, stop=final)
                            last.then_inc(attended, 1)

                        scores(0)
                        scores(1)
                        for h in range(NH):
                            pe.wait_ge(exped, n0 + (h + 1))
                            for t, kt, col, colT in prob_blocks(kind):
                                last = nc.tensor.transpose(T[h % 2][:, colT:colT + P], prob[:, h % 2, col:col + P], k.ident[:])
                            last.then_inc(turned, 1)
                            if h + 2 < NH:
                                scores(h + 2)
                            if h:
                                weighted(h - 1)
                        weighted(NH - 1)

                    def project(w, a):
                        pe.wait_ge(o_ready, it * 2 + (a + 1))
                        for t in range(TB):
                            last = nc.tensor.transpose(G[0][:, P * t:P * t + P], o[:, t, :], k.ident[:])
                        last.then_inc(o_turned, 1)
                        pe.wait_ge(oT_ready, it * 2 + (a + 1))
                        for t in range(TB):
                            last = nc.tensor.matmul(G[1][:, P * t:P * t + P], oT[:, P * t:P * t + P], WT[:, w, :], start=True, stop=True)
                        last.then_inc(projected, 1)

                    pe.wait_ge(mem_ready, it + 1)
                    nc.tensor.matmul(G[0][:, 0:S], WT[:, WK_C, :], mem[:], start=True, stop=True).then_inc(kc_made, 1)
                    for t in range(TB):
                        last = nc.tensor.matmul(G[2][:, P * t:P * t + P], mem[:, P * t:P * t + P], WT[:, WV_C, :], start=True, stop=True)
                    last.then_inc(vc_made, 1)
                    pe.wait_ge(kc_ready, it + 1)
                    turn_h(0)
                    for i, w in enumerate((WQ, WK)):
                        last = nc.tensor.matmul(G[1][:, S * i:S * i + S], WT[:, w, :], hT[:], start=True, stop=True)
                    last.then_inc(qk_made, 1)
                    pe.wait_ge(vc_ready, it + 1)
                    for t in range(TB):
                        last = nc.tensor.matmul(G[2][:, P * t:P * t + P], hT[:, P * t:P * t + P], WT[:, WV, :], start=True, stop=True)
                    last.then_inc(v_made, 1)
                    pe.wait_ge(qk_biased, it + 1)
                    nc.tensor.matmul(G[0][:], c.rot[:], qk[:].rearrange("p c s -> p (c s)"), start=True, stop=True).then_inc(qk_turned, 1)
                    pe.wait_ge(queries_ready, it * 2 + 1)
                    pe.wait_ge(v_ready, it + 1)
                    attention(0, qkr[:, 1, :], V, 0)
                    project(WO_S, 0)
                    turn_h(1)
                    nc.tensor.matmul(G[2][:, 0:S], WT[:, WQ_C, :], hT[:], start=True, stop=True).then_inc(qc_made, 1)
                    pe.wait_ge(queries_ready, it * 2 + 2)
                    attention(1, kc, VC, 1)
                    project(WO_C, 1)
                    turn_h(2)
                    for w, banks, made in ((WG, A, gated), (WU, T, upped)):
                        for f in range(4):
                            last = nc.tensor.matmul(banks[f // 2][:, f % 2 * S:f % 2 * S + S], WT[:, w + f, :], hT[:], start=True, stop=True)
                            if f % 2:
                                last.then_inc(made, 1)
                    pe.wait_ge(act_ready, it * 2 + 2)
                    for t in range(TB):
                        for f in range(4):
                            last = nc.tensor.matmul(G[1][:, P * t:P * t + P], aT[:, f, P * t:P * t + P], WT[:, WD + f, :], start=f == 0, stop=f == 3)
                    last.then_inc(downed, 1)

        @block.scalar
        def _(act):
            with act.Fori(0, LAYERS) as l:
                for g in range(BLOCKS // 4):
                    act.wait_ge(w_turned, l * (BLOCKS // 4) + (g + 1))
                    last = nc.scalar.activation(WT[:, 4 * g:4 * g + 4, :].rearrange("p c d -> p (c d)"), (A + T + [O])[g][:], ACT.Copy)
                nc.scalar.activation(norm_w[:], c.norms[:, :, bass.ds(l, 1)].rearrange("p n a -> p (n a)"), ACT.Copy)
                nc.scalar.activation(bias[:], c.bias_qk[:, bass.ds(l, 1), :].rearrange("p a n -> p (a n)"), ACT.Copy)
                act.drain().then_inc(w_ready, 1)
                with act.Fori(0, B) as b:
                    it = l * B + b

                    def copy_h(j):
                        act.wait_ge(h_turned, it * 3 + (j + 1))
                        nc.scalar.activation(hT[:], G[0][:, 0:S], ACT.Copy, scale=norm_w[:, j:j + 1]).then_inc(hT_ready, 1)

                    def exps(kind, a):
                        n0 = it * (2 * NH) + a * NH
                        for h in range(NH):
                            act.wait_ge(maxed, n0 + (h + 1))
                            for t, _, n, col in TILES[kind]:
                                last = nc.scalar.activation(prob[:, h % 2, col:col + n], A[h % 2][:, col:col + n], ACT.Exp,
                                                            bias=neg_max[:, h, t:t + 1])
                            last.then_inc(exped, 1)

                    def copy_o(a):
                        act.wait_ge(o_turned, it * 2 + (a + 1))
                        nc.scalar.activation(oT[:], G[0][:, 0:S], ACT.Copy).then_inc(oT_ready, 1)

                    nc.scalar.activation(mem[:], k.ctxT[:, bass.ds(b * S, S)], ACT.Copy).then_inc(mem_ready, 1)
                    act.wait_ge(kc_made, it + 1)
                    nc.scalar.activation(kc[:], G[0][:, 0:S], ACT.Copy).then_inc(kc_ready, 1)
                    copy_h(0)
                    act.wait_ge(qk_made, it + 1)
                    nc.scalar.activation(qk[:, 0, :], G[1][:, 0:S], ACT.Identity, scale=SCALE, bias=bias[:, 0:1])
                    nc.scalar.activation(qk[:, 1, :], G[1][:, S:2 * S], ACT.Identity, bias=bias[:, 1:2]).then_inc(qk_biased, 1)
                    exps(0, 0)
                    copy_o(0)
                    copy_h(1)
                    act.wait_ge(qc_made, it + 1)
                    nc.scalar.activation(qc[:], G[2][:, 0:S], ACT.Copy, scale=SCALE).then_inc(qc_ready, 1)
                    exps(1, 1)
                    copy_o(1)
                    copy_h(2)
                    for i in range(2):
                        act.wait_ge(gated, it * 2 + (i + 1))
                        nc.scalar.activation(tg[:, 2 * i:2 * i + 2, :].rearrange("p f s -> p (f s)"), A[i][:], ACT.Tanh, scale=0.5).then_inc(tanhed, 1)

        @block.gpsimd
        def _(pool):
            with pool.Fori(0, LAYERS * B) as it:
                def root(j):
                    pool.wait_ge(ss_ready, it * 3 + (j + 1))
                    nc.gpsimd.tensor_tensor(r[:], ss[:], k.minus_half[:, 0:TB], ALU.pow).then_inc(r_ready, 1)

                def mask(src):
                    nc.gpsimd.tensor_tensor(qm[:], src.unsqueeze(1).broadcast_to([P, 4, S]), c.own[:].unsqueeze(2).broadcast_to([P, 4, S]),
                                            ALU.mult).then_inc(queries_ready, 1)

                root(0)
                pool.wait_ge(roped, it + 1)
                mask(qkr[:, 0, :])
                root(1)
                pool.wait_ge(qc_ready, it + 1)
                mask(qc[:])
                root(2)

        @block.vector
        def _(dve):
            nc.vector.memset(V[:], 1.0)
            nc.vector.memset(VC[:], 1.0)
            dve.drain().then_inc(ones_set, 1)
            with dve.Fori(0, LAYERS) as l:
                with dve.Fori(0, B) as b:
                    it = l * B + b
                    x = XX[:, bass.ds(b * TB, TB), :]

                    def normed(j):
                        nc.vector.tensor_tensor(h[:], x, x, ALU.mult)
                        dve.drain()
                        nc.vector.tensor_reduce(ss[:], h[:], AX.X, ALU.add)
                        dve.drain()
                        nc.vector.tensor_scalar(ss[:], ss[:], 1.0 / D, 1e-6, ALU.mult, ALU.add).then_inc(ss_ready, 1)
                        dve.wait_ge(r_ready, it * 3 + (j + 1))
                        nc.vector.tensor_tensor(h[:], x, r[:].unsqueeze(2).broadcast_to([P, TB, D]), ALU.mult).then_inc(h_ready, 1)

                    def attention(kind, a):
                        n0 = it * (2 * NH) + a * NH

                        def find_max(h):
                            dve.wait_ge(scored, n0 + (h + 1))
                            if kind == 1:
                                nc.vector.tensor_reduce(neg_max[:, h, :], A[h % 2][:].rearrange("p (t s) -> p t s", t=TB),
                                                        AX.X, ALU.max, negate=True).then_inc(maxed, 1)
                            else:
                                for t, _, n, col in TILES[kind]:
                                    last = nc.vector.tensor_reduce(neg_max[:, h, t:t + 1], A[h % 2][:, col:col + n], AX.X, ALU.max, negate=True)
                                last.then_inc(maxed, 1)

                        find_max(0)
                        for h in range(NH):
                            if h + 1 < NH:
                                find_max(h + 1)
                            dve.wait_ge(turned, n0 + (h + 1))
                            nc.vector.tensor_copy(probT[:, h % 2, 0:WIDTH[kind]], T[h % 2][:, 0:WIDTH[kind]]).then_inc(turn_copied, 1)
                        dve.wait_ge(attended, n0 + NH)
                        o9 = O[:, 0:TB * NH * (HD + 1)].rearrange("p (t h d) -> p t h d", t=TB, h=NH)
                        nc.vector.reciprocal(rec[:], o9[:, :, :, HD])
                        dve.drain()
                        nc.vector.tensor_tensor(o[:].rearrange("p t (h d) -> p (t h) d", h=NH), o9[:, :, :, 0:HD].rearrange("p t h d -> p (t h) d"),
                                                rec[:].rearrange("p t h -> p (t h)").unsqueeze(2).broadcast_to([P, TB * NH, HD]),
                                                ALU.mult).then_inc(o_ready, 1)

                    def add_to_x(made, count, with_bias=False):
                        dve.wait_ge(made, count)
                        y = G[1][:, 0:TB * D].rearrange("p (t d) -> p t d", t=TB)
                        if with_bias:
                            nc.vector.tensor_tensor(proj[:], y, c.bias_o[:, bass.ds(l, 1), :].broadcast_to([P, TB, D]), ALU.add)
                            dve.drain()
                            y = proj[:]
                        nc.vector.tensor_tensor(x, x, y, ALU.add)
                        dve.drain()

                    dve.wait_ge(vc_made, it + 1)
                    nc.vector.tensor_copy(VC[:, :, :, 0:HD], G[2][:, 0:S].rearrange("p (t h d) -> p t h d", t=TB, h=NH)).then_inc(vc_ready, 1)
                    normed(0)
                    dve.wait_ge(v_made, it + 1)
                    nc.vector.tensor_tensor(V[:, :, :, 0:HD], G[2][:, 0:S].rearrange("p (t h d) -> p t h d", t=TB, h=NH),
                                            c.bias_v[:, bass.ds(l, 1), :].rearrange("p a (h d) -> p a h d", h=NH).broadcast_to([P, TB, NH, HD]),
                                            ALU.add).then_inc(v_ready, 1)
                    dve.wait_ge(qk_turned, it + 1)
                    wide = lambda a: a.unsqueeze(1).broadcast_to([P, 2, S])
                    nc.vector.tensor_tensor(turned_sin[:], G[0][:].rearrange("p (c s) -> p c s", c=2), wide(c.sin[:]), ALU.mult)
                    nc.vector.tensor_tensor(qkr[:], qk[:], wide(c.cos[:]), ALU.mult)
                    dve.drain()
                    nc.vector.tensor_tensor(qkr[:], qkr[:], turned_sin[:], ALU.add).then_inc(roped, 1)
                    attention(0, 0)
                    add_to_x(projected, it * 2 + 1, with_bias=True)
                    normed(1)
                    attention(1, 1)
                    add_to_x(projected, it * 2 + 2)
                    normed(2)
                    for i in range(2):
                        dve.wait_ge(tanhed, it * 2 + (i + 1))
                        g = tg[:, 2 * i:2 * i + 2, :].rearrange("p f s -> p (f s)")
                        nc.vector.scalar_tensor_tensor(g, g, 1.0, A[i][:], ALU.add, ALU.mult)
                        dve.drain()
                        dve.wait_ge(upped, it * 2 + (i + 1))
                        nc.vector.scalar_tensor_tensor(aT[:, 2 * i:2 * i + 2, :].rearrange("p f s -> p (f s)"), g, 0.5, T[i][:],
                                                       ALU.mult, ALU.mult).then_inc(act_ready, 1)
                    add_to_x(downed, it + 1)


def decoder_end(nc, k, c, XX):
    with ExitStack() as stack:
        m = Memory(nc, stack)
        SQ, ss, r = m.sb("e_SQ", [P, NT, D]), m.sb("e_ss", [P, NT]), m.sb("e_r", [P, NT])
        ss_ready, r_ready = m.sem("e_ss_ready"), m.sem("e_r_ready")
        block = stack.enter_context(nc.Block())

        @block.vector
        def _(dve):
            nc.vector.tensor_tensor(SQ[:], XX[:], XX[:], ALU.mult)
            dve.drain()
            nc.vector.tensor_reduce(ss[:], SQ[:], AX.X, ALU.add)
            dve.drain()
            nc.vector.tensor_scalar(ss[:], ss[:], 1.0 / D, 1e-6, ALU.mult, ALU.add).then_inc(ss_ready, 1)
            dve.wait_ge(r_ready, 1)
            nc.vector.tensor_tensor(XX[:], XX[:], r[:].unsqueeze(2).broadcast_to([P, NT, D]), ALU.mult)
            dve.drain()
            nc.vector.tensor_tensor(XX[:], XX[:], c.nf[:].unsqueeze(1).broadcast_to([P, NT, D]), ALU.mult)
            dve.drain()
            nc.vector.scalar_tensor_tensor(k.X[:], XX[:], k.gate[:, 1:2], k.X[:], ALU.mult, ALU.add)

        @block.gpsimd
        def _(pool):
            pool.wait_ge(ss_ready, 1)
            nc.gpsimd.tensor_tensor(r[:], ss[:], k.minus_half[:, 0:NT], ALU.pow).then_inc(r_ready, 1)


def moe(nc, k, io):
    with ExitStack() as stack:
        m = Memory(nc, stack)
        hT = m.sb("f_hT", [P, NTOK])
        acc = m.sb("f_acc", [P, NT, D])
        weight = m.sb("f_weight", [P, NT, 8])
        ln = m.sb("f_ln", [P, 2])
        wr = m.sb("f_wr", [P, 7])
        with ExitStack() as inner:
            n = Memory(nc, inner)
            loaded = n.sem("f_loaded")
            block = inner.enter_context(nc.Block())

            @block.sync
            def _(sp):
                sp.dma_start(ln[:, 0:1], io["L1_ffn_ln_g"].rearrange("(d a) -> d a", a=1)).then_inc(loaded, 16)
                sp.dma_start(ln[:, 1:2], io["L1_ffn_ln_b"].rearrange("(d a) -> d a", a=1)).then_inc(loaded, 16)
                sp.dma_start(wr[:], io["L1_ffn_Wr"]).then_inc(loaded, 16)
                sp.wait_ge(loaded, 48)
        with ExitStack() as inner:
            n = Memory(nc, inner)
            Xn = n.sb("f_Xn", [P, NT, D])
            layer_norm(nc, k, k.X, Xn, tag="f_")
            layer_norm(nc, k, Xn, Xn, hT, scale=ln[:, 0:1], shift=ln[:, 1:2], tag="fh_")
        moe_router(nc, k, hT, wr, weight)
        moe_experts(nc, k, io, hT, weight, acc)
        with ExitStack() as inner:
            block = inner.enter_context(nc.Block())

            @block.vector
            def _(dve):
                nc.vector.scalar_tensor_tensor(k.X[:], acc[:], k.gate[:, 3:4], k.X[:], ALU.mult, ALU.add)


def moe_router(nc, k, hT, wr, weight):
    E = 7
    with ExitStack() as stack:
        m = Memory(nc, stack)
        logit, scratch = m.sb("r_logit", [P, NT, E]), m.sb("r_scratch", [P, NT, E])
        one = m.sb("r_one", [P, 2, NT, E])
        oneb = m.sb("r_oneb", [P, 2, NT, E], BF16)
        m1, m2, first, e = (m.sb("r_" + n, [P, NT]) for n in ("m1", "m2", "first", "e"))
        gates = m.sb("r_gates", [P, 2, NT])
        before, beforeb, allb = m.sb("r_before", [P, P]), m.sb("r_beforeb", [P, P], BF16), m.sb("r_allb", [P, P], BF16)
        total, through = m.sb("r_total", [P, 2 * NT, E]), m.sb("r_through", [P, 2 * NT, E])
        lb, rb, tb = m.bank("r_logit_bank"), m.bank("r_rank_bank"), m.bank("r_total_bank")
        made, logits, diff_ready, exp_ready, one_ready, ranked = (m.sem("r_" + n) for n in ("made", "logits", "diff_ready", "exp_ready", "one_ready", "ranked"))
        block = stack.enter_context(nc.Block())

        @block.gpsimd
        def _(pool):
            nc.gpsimd.memset(before[:], 1.0)
            nc.gpsimd.memset(allb[:], 1.0)
            pool.drain()
            nc.gpsimd.affine_select(out=before[:], in_=before[:], compare_op=ALU.is_gt, fill=0.0,
                                    base=0, pattern=[[1, P]], channel_multiplier=-1)
            pool.drain()
            nc.gpsimd.tensor_copy(beforeb[:], before[:]).then_inc(made, 1)

        @block.tensor
        def _(pe):
            for t in range(NT):
                last = nc.tensor.matmul(lb[:, E * t:E * t + E], hT[:, P * t:P * t + P], wr[:], start=True, stop=True)
            last.then_inc(logits, 1)
            pe.wait_ge(made, 1)
            pe.wait_ge(one_ready, 1)
            flat = oneb[:].rearrange("p s t e -> p (s t e)")
            nc.tensor.matmul(rb[:, 0:2 * NT * E], beforeb[:], flat, start=True, stop=True)
            nc.tensor.matmul(tb[:, 0:2 * NT * E], allb[:], flat, start=True, stop=True).then_inc(ranked, 1)

        @block.scalar
        def _(act):
            act.wait_ge(diff_ready, 1)
            nc.scalar.activation(e[:], e[:], ACT.Exp).then_inc(exp_ready, 1)

        @block.vector
        def _(dve):
            dve.wait_ge(logits, 1)
            nc.vector.tensor_copy(logit[:].rearrange("p t e -> p (t e)"), lb[:, 0:NT * E])
            dve.drain()
            top_two(nc, dve, logit[:], one[:, 0], one[:, 1], m1[:], m2[:], scratch[:], first[:], k.rev, NT, E)
            nc.vector.tensor_copy(oneb[:], one[:]).then_inc(one_ready, 1)
            nc.vector.tensor_tensor(e[:], m2[:], m1[:], ALU.subtract).then_inc(diff_ready, 1)
            dve.wait_ge(exp_ready, 1)
            nc.vector.tensor_scalar(m1[:], e[:], 1.0, None, ALU.add)
            dve.drain()
            nc.vector.reciprocal(gates[:, 0, :], m1[:])
            dve.drain()
            nc.vector.tensor_tensor(gates[:, 1, :], e[:], gates[:, 0, :], ALU.mult)
            dve.wait_ge(ranked, 1)
            nc.vector.tensor_copy(total[:].rearrange("p t e -> p (t e)"), tb[:, 0:2 * NT * E])
            dve.drain()
            for x in range(E):
                nc.vector.tensor_tensor_scan(through[:, :, x], k.ones[:, 0:2 * NT], total[:, :, x], 0.0, ALU.mult, ALU.add)
            dve.drain()
            nc.vector.tensor_tensor(through[:], through[:], total[:], ALU.subtract)
            dve.drain()
            nc.vector.tensor_tensor(through[:].rearrange("p t e -> p (t e)"), through[:].rearrange("p t e -> p (t e)"),
                                    rb[:, 0:2 * NT * E], ALU.add)
            dve.drain()
            ones = one[:].rearrange("p s t e -> p (s t) e")
            nc.vector.scalar_tensor_tensor(ones, through[:], float(CAPACITY), ones, ALU.is_lt, ALU.mult)
            dve.drain()
            nc.vector.tensor_tensor(ones, ones, gates[:].rearrange("p s t -> p (s t)").unsqueeze(2).broadcast_to([P, 2 * NT, E]), ALU.mult)
            nc.vector.memset(weight[:], 1.0)
            dve.drain()
            nc.vector.tensor_tensor(weight[:, :, 0:E], one[:, 0], one[:, 1], ALU.add)


def moe_experts(nc, k, io, hT, weight, acc):
    E, F, N = 8, 4, 512
    CH = NTOK // N
    STEPS = 2 * CH
    with ExitStack() as stack:
        m = Memory(nc, stack)
        W1, W3, W2 = (m.sb("x_" + n, [P, 2, F, P]) for n in ("W1", "W3", "W2"))
        tg, aT, scaled_y = m.sb("x_tg", [P, 2, N]), m.sb("x_aT", [P, 2, F, N]), m.sb("x_scaled_y", [P, 2, 4, D])
        A, U, Y = ([m.bank(f"x_{n}{i}") for i in range(2)] for n in "AUY")
        w_in = [m.sem("x_w_in0"), m.sem("x_w_in1")]
        made, tanhed, acted, y_made, scaled, added = (m.sem("x_" + n) for n in ("made", "tanhed", "acted", "y_made", "scaled", "added"))
        block = stack.enter_context(nc.Block())

        @block.sync
        def _(sp):
            with sp.Fori(0, E // 2) as e2:
                for s in range(2):
                    e = e2 * 2 + s
                    sp.wait_ge(added, e * CH + CH)
                    sp.dma_start(W1[:, s], io["experts_W1"][bass.ds(e, 1)].rearrange("a d (f p) -> d (a f) p", p=P)).then_inc(w_in[s], 16)
                    sp.dma_start(W3[:, s], io["experts_W3"][bass.ds(e, 1)].rearrange("a d (f p) -> d (a f) p", p=P)).then_inc(w_in[s], 16)
                    sp.dma_start(W2[:, s], io["experts_W2"][bass.ds(e, 1)].rearrange("a (f p) d -> p (a f) d", p=P)).then_inc(w_in[s], 16)

        @block.tensor
        def _(pe):
            with pe.Fori(0, E // 2) as e2:
                def up(i):
                    s, c = i // CH, i % CH
                    if c == 0:
                        pe.wait_ge(w_in[s], e2 * 48 + 48)
                    for f in range(F):
                        pe.wait_ge(acted, e2 * (STEPS * F) + (i * F + f + 1))
                        nc.tensor.matmul(A[f % 2][:], W1[:, s, f, :], hT[:, N * c:N * c + N], start=True, stop=True)
                        nc.tensor.matmul(U[f % 2][:], W3[:, s, f, :], hT[:, N * c:N * c + N], start=True, stop=True).then_inc(made, 1)

                def down(i):
                    s = i // CH
                    pe.wait_ge(acted, e2 * (STEPS * F) + (i * F + F + 2))
                    pe.wait_ge(scaled, e2 * STEPS + (i + 1))
                    for t in range(4):
                        for f in range(F):
                            last = nc.tensor.matmul(Y[i % 2][:, P * t:P * t + P], aT[:, i % 2, f, P * t:P * t + P], W2[:, s, f, :],
                                                    start=f == 0, stop=f == F - 1)
                    last.then_inc(y_made, 1)

                up(0)
                for i in range(STEPS):
                    if i + 1 < STEPS:
                        up(i + 1)
                    down(i)

        @block.scalar
        def _(act):
            with act.Fori(0, E // 2) as e2:
                for n in range(STEPS * F):
                    act.wait_ge(made, e2 * (STEPS * F) + (n + 1))
                    nc.scalar.activation(tg[:, n % 2, :], A[n % 2][:], ACT.Tanh, scale=0.5).then_inc(tanhed, 1)

        @block.vector
        def _(dve):
            dve.sem_inc(acted, 2)
            dve.sem_inc(scaled, 2)
            with dve.Fori(0, E // 2) as e2:
                def hidden(i):
                    for f in range(F):
                        n = i * F + f
                        dve.wait_ge(tanhed, e2 * (STEPS * F) + (n + 1))
                        nc.vector.scalar_tensor_tensor(tg[:, n % 2, :], tg[:, n % 2, :], 1.0, A[n % 2][:], ALU.add, ALU.mult)
                        dve.drain()
                        nc.vector.scalar_tensor_tensor(aT[:, i % 2, f, :], tg[:, n % 2, :], 0.5, U[n % 2][:],
                                                       ALU.mult, ALU.mult).then_inc(acted, 1)

                def weigh(i):
                    s, c = i // CH, i % CH
                    dve.wait_ge(y_made, e2 * STEPS + (i + 1))
                    dve.wait_ge(added, e2 * STEPS + (i + 2 * CH - 1))
                    nc.vector.tensor_tensor(scaled_y[:, i % 2], Y[i % 2][:].rearrange("p (t d) -> p t d", t=4),
                                            weight[:, 4 * c:4 * c + 4, bass.ds(e2 * 2 + s, 1)].broadcast_to([P, 4, D]), ALU.mult).then_inc(scaled, 1)

                hidden(0)
                for i in range(STEPS):
                    if i + 1 < STEPS:
                        hidden(i + 1)
                    weigh(i)

        @block.gpsimd
        def _(pool):
            nc.gpsimd.memset(acc[:], 0.0)
            pool.drain().then_inc(added, 2 * CH)
            with pool.Fori(0, E // 2) as e2:
                for i in range(STEPS):
                    c = i % CH
                    pool.wait_ge(scaled, e2 * STEPS + (i + 3))
                    nc.gpsimd.tensor_tensor(acc[:, 4 * c:4 * c + 4, :], acc[:, 4 * c:4 * c + 4, :], scaled_y[:, i % 2], ALU.add).then_inc(added, 1)


class Kept:

    EXPERTS_IN = 32

    def __init__(self, nc, stack):
        m = Memory(nc, stack)
        self.X = m.sb("X", [P, NT, D])
        self.ctxT = m.sb("ctxT", [P, NTOK])
        self.ctx_ones = m.sb("ctx_ones", [P, NT, 8, 17])
        self.ident, self.identb = m.sb("ident", [P, P]), m.sb("identb", [P, P], BF16)
        self.causal, self.causalb = m.sb("causal", [P, 2, P]), m.sb("causalb", [P, 2, P], BF16)
        self.ones, self.minus_half = m.sb("ones", [P, S]), m.sb("minus_half", [P, S])
        self.gate = m.sb("gate", [P, 4])
        self.rev = m.sb("rev", [P, 8])


def build(nc, io, out):
    with ExitStack() as stack:
        k = Kept(nc, stack)
        load_inputs(nc, k, io)
        with ExitStack() as inner:
            m = Memory(nc, inner)
            k.v_w, k.o_w, k.experts_in = m.sb("v_w", [P, 64, P]), m.sb("o_w", [P, 64, P]), m.sem("experts_in")
            mlstm(nc, k, io)
            switch_head(nc, k, io)
        decoder(nc, k, io)
        moe(nc, k, io)
        store(nc, k, out)


def store(nc, k, out):
    with ExitStack() as stack:
        stored = Memory(nc, stack).sem("out_stored")
        block = stack.enter_context(nc.Block())

        @block.sync
        def _(sp):
            sp.dma_start(out.rearrange("b (t p) d -> p (b t) d", p=P), k.X[:]).then_inc(stored, 16)
            sp.wait_ge(stored, 16)


def rope_tables():
    import numpy as np
    hd, heads = 8, 16
    inv = (1.0 / np.float32(10000.0) ** (np.arange(0, hd, 2, dtype=np.float32) / np.float32(hd))).astype(np.float32)
    f = np.arange(S, dtype=np.float32)[:, None] * inv[None, :]
    emb = np.concatenate([f, f], axis=-1)
    turn = np.zeros((P, P), np.float32)
    for r in range(P):
        turn[r + 4 if r % hd < 4 else r - 4, r] = -1.0 if r % hd < 4 else 1.0
    own = (np.arange(P)[:, None] // hd % 4 == np.arange(4)[None, :]).astype(np.float32)
    return dict(rope_cos=np.tile(np.cos(emb).T, (heads, 1)).astype(np.float32),
                rope_sin=np.tile(np.sin(emb).T, (heads, 1)).astype(np.float32), rope_turn=turn, head_of_quadrant=own)


_OUTS = [((8, 256, 128), "float32")]


def kernel(**inputs):
    import numpy as _np
    import concourse.bacc as _bacc
    from concourse import mybir as _mybir
    from concourse.bass_utils import run_bass_kernel_spmd as _run

    nc = _bacc.Bacc("TRN2", target_bir_lowering=False, num_devices=1)
    laid = {name: _np.ascontiguousarray(a) for name, a in inputs.items()}
    laid.update(rope_tables())
    for w in ("W1", "W3", "W2"):
        laid["experts_" + w] = _np.concatenate([laid.pop("L1_ffn_" + w), laid.pop("L1_ffn_" + w + "s")[None]])
    arrays, io = {}, {}
    for name, a in laid.items():
        arrays[f"in_{name}"] = a
        io[name] = nc.dram_tensor(f"in_{name}", a.shape, _mybir.dt.from_np(a.dtype), kind="ExternalInput").ap()
    shape, dtype = _OUTS[0]
    out = nc.dram_tensor("out_0", shape, _mybir.dt.from_np(_np.dtype(dtype)), kind="ExternalOutput").ap()
    build(nc, io, out)
    r = _run(nc, [arrays], core_ids=[0])
    return r.results[0]["out_0"]
```

```python
import concourse.bass as bass
from concourse import mybir
from contextlib import ExitStack

FP32 = mybir.dt.float32
BF16 = mybir.dt.bfloat16
ALU = mybir.AluOpType
ACT = mybir.ActivationFunctionType
AX = mybir.AxisListType

P = 128
B, S, D = 8, 256, 128
TB = S // P
NT = B * TB
NTOK = B * S
NEG = -1e30
CAPACITY = 366
LAYERS = 4


class Memory:

    def __init__(self, nc, stack):
        self.nc, self.stack = nc, stack

    def sb(self, name, shape, dtype=FP32):
        return self.stack.enter_context(self.nc.sbuf_tensor(name, shape, dtype))

    def bank(self, name, dtype=FP32, cols=512):
        return self.stack.enter_context(self.nc.psum_tensor(name, [P, cols], dtype))

    def sem(self, name):
        return self.stack.enter_context(self.nc.semaphore(name))


def load_inputs(nc, k, io):
    with ExitStack() as stack:
        m = Memory(nc, stack)
        C = m.sb("ctx_natural", [P, NT, D])
        graw = m.sb("graw", [P, 4])
        banks = [m.bank(f"ctxT_bank{i}") for i in range(4)]
        x_in, ctx_in, g_in = m.sem("x_in"), m.sem("ctx_in"), m.sem("g_in")
        const_made, transposed = m.sem("const_made"), m.sem("ctx_transposed")
        block = stack.enter_context(nc.Block())

        @block.sync
        def _(sp):
            sp.dma_start(C[:], io["ctx_1024"].rearrange("b (t p) d -> p (b t) d", p=P)).then_inc(ctx_in, 16)
            sp.dma_start(k.X[:], io["x"].rearrange("b (t p) d -> p (b t) d", p=P)).then_inc(x_in, 16)
            sp.dma_start(graw[:, 0:2], io["g_xattn"].rearrange("(a n) -> a n", a=1).broadcast_to([P, 2])).then_inc(g_in, 16)
            sp.dma_start(graw[:, 2:4], io["g_ffn"].rearrange("(a n) -> a n", a=1).broadcast_to([P, 2])).then_inc(g_in, 16)
            sp.wait_ge(x_in, 16)

        @block.gpsimd
        def _(pool):
            nc.gpsimd.memset(k.ident[:], 0.0)
            nc.gpsimd.memset(k.ones[:], 1.0)
            nc.gpsimd.memset(k.minus_half[:], -0.5)
            for e in range(8):
                nc.gpsimd.memset(k.rev[:, e:e + 1], 8.0 - e)
            nc.gpsimd.memset(k.causal[:], 0.0)
            pool.drain()
            nc.gpsimd.affine_select(out=k.ident[:], in_=k.ident[:], compare_op=ALU.not_equal, fill=1.0,
                                    base=0, pattern=[[-1, P]], channel_multiplier=1)
            nc.gpsimd.affine_select(out=k.causal[:, 0, :], in_=k.causal[:, 0, :], compare_op=ALU.is_ge, fill=NEG,
                                    base=0, pattern=[[-1, P]], channel_multiplier=1)
            nc.gpsimd.affine_select(out=k.causal[:, 1, :], in_=k.causal[:, 1, :], compare_op=ALU.is_ge, fill=NEG,
                                    base=0, pattern=[[1, P]], channel_multiplier=-1)
            pool.drain()
            nc.gpsimd.tensor_copy(k.identb[:], k.ident[:])
            nc.gpsimd.tensor_copy(k.causalb[:], k.causal[:]).then_inc(const_made, 1)

        @block.tensor
        def _(pe):
            pe.wait_ge(const_made, 1)
            pe.wait_ge(ctx_in, 16)
            for t in range(NT):
                nc.tensor.transpose(banks[t // 4][:, t % 4 * P:t % 4 * P + P], C[:, t, :], k.ident[:]).then_inc(transposed, 1)

        @block.scalar
        def _(act):
            act.wait_ge(g_in, 32)
            nc.scalar.activation(k.gate[:], graw[:], ACT.Tanh)
            for c in range(4):
                act.wait_ge(transposed, 4 * c + 4)
                nc.scalar.activation(k.ctxT[:, 512 * c:512 * c + 512], banks[c][:], ACT.Copy)

        @block.vector
        def _(dve):
            nc.vector.memset(k.ctx_ones[:, :, :, 16:17], 1.0)
            dve.wait_ge(ctx_in, 16)
            nc.vector.tensor_copy(k.ctx_ones[:, :, :, 0:16], C[:].rearrange("p t (h d) -> p t h d", h=8))


def layer_norm(nc, k, src, dst, dstT=None, scale=None, shift=None, tag=""):
    with ExitStack() as stack:
        m = Memory(nc, stack)
        stats, mv, rstd = m.sb(tag + "stats", [P, NT, 6]), m.sb(tag + "mv", [P, NT, 2]), m.sb(tag + "rstd", [P, NT])
        banks = [m.bank(f"{tag}nT_bank{i}") for i in range(4)]
        var_ready, rstd_ready, normed, transposed = (m.sem(tag + n) for n in ("var_ready", "rstd_ready", "normed", "transposed"))
        block = stack.enter_context(nc.Block())

        @block.vector
        def _(dve):
            for t in range(NT):
                nc.vector.bn_stats(stats[:, t, :], src[:, t, :])
            dve.drain()
            for t in range(NT):
                nc.vector.bn_aggr(mv[:, t, :], stats[:, t, :])
            dve.drain()
            nc.vector.tensor_scalar(mv[:, :, 1], mv[:, :, 1], 1e-5, None, ALU.add).then_inc(var_ready, 1)
            dve.wait_ge(rstd_ready, 1)
            for t in range(NT):
                nc.vector.tensor_scalar(dst[:, t, :], src[:, t, :], mv[:, t, 0:1], rstd[:, t:t + 1],
                                        ALU.subtract, ALU.mult).then_inc(normed, 1)

        @block.gpsimd
        def _(pool):
            pool.wait_ge(var_ready, 1)
            nc.gpsimd.tensor_tensor(rstd[:], mv[:, :, 1], k.minus_half[:, 0:NT], ALU.pow).then_inc(rstd_ready, 1)

        if dstT is not None:
            @block.tensor
            def _(pe):
                for t in range(NT):
                    pe.wait_ge(normed, t + 1)
                    nc.tensor.transpose(banks[t // 4][:, t % 4 * P:t % 4 * P + P], dst[:, t, :], k.ident[:]).then_inc(transposed, 1)

            @block.scalar
            def _(act):
                for c in range(4):
                    act.wait_ge(transposed, 4 * c + 4)
                    if scale is None:
                        nc.scalar.activation(dstT[:, 512 * c:512 * c + 512], banks[c][:], ACT.Copy)
                    else:
                        nc.scalar.activation(dstT[:, 512 * c:512 * c + 512], banks[c][:], ACT.Identity,
                                             scale=scale, bias=shift)


def mlstm(nc, k, io):
    NH, HD = 8, 16
    with ExitStack() as stack:
        m = Memory(nc, stack)
        Xn, XnT = m.sb("m_Xn", [P, NT, D]), m.sb("m_XnT", [P, NTOK])
        layer_norm(nc, k, k.X, Xn, XnT, tag="m_")
        neg_max, aT, enT = m.sb("neg_max", [NH, NTOK]), m.sb("aT", [P, NT, NH]), m.sb("enT", [P, NT, NH])
        sel = m.sb("sel", [NH, NH, P])
        mlstm_gates(nc, k, io, XnT, neg_max, aT, enT, sel)
        HO = m.sb("HO", [P, NT, NH, HD + 1])
        mlstm_heads(nc, k, io, XnT, neg_max, aT, sel, HO)
        mlstm_finish(nc, k, enT, HO)


def mlstm_gates(nc, k, io, XnT, neg_max, aT, enT, sel):
    NH = 8
    with ExitStack() as stack:
        m = Memory(nc, stack)
        wi, wf = m.sb("wi", [P, 3, NH]), m.sb("wf", [P, 3, NH])
        bi, bf = m.sb("bi", [NH, 1]), m.sb("bf", [NH, 1])
        IG, F, T, CS, A, M = (m.sb("g_" + n, [NH, NTOK]) for n in ("IG", "F", "T", "CS", "A", "M"))
        banks = [m.bank(f"gate_bank{i}") for i in range(8)]
        w_in, projected, pre_ready, abs_ready, log_ready = (m.sem("mg_" + n) for n in ("w_in", "projected", "pre_ready", "abs_ready", "log_ready"))
        a_ready, sum_ready, en_ready, transposed = (m.sem("mg_" + n) for n in ("a_ready", "sum_ready", "en_ready", "transposed"))
        block = stack.enter_context(nc.Block())

        @block.sync
        def _(sp):
            sp.dma_start(wi[:], io["L0_xattn_igate_kernel"].rearrange("(c p) n -> p c n", p=P)).then_inc(w_in, 16)
            sp.dma_start(wf[:], io["L0_xattn_fgate_kernel"].rearrange("(c p) n -> p c n", p=P)).then_inc(w_in, 16)
            sp.dma_start(bi[:], io["L0_xattn_igate_bias"].rearrange("(n a) -> n a", a=1)).then_inc(w_in, 16)
            sp.dma_start(bf[:], io["L0_xattn_fgate_bias"].rearrange("(n a) -> n a", a=1)).then_inc(w_in, 16)

        @block.gpsimd
        def _(pool):
            nc.gpsimd.memset(sel[:], 0.0)
            pool.drain()
            nc.gpsimd.affine_select(out=sel[:], in_=sel[:], compare_op=ALU.not_equal, fill=1.0,
                                    base=0, pattern=[[-1, NH], [0, P]], channel_multiplier=1)

        @block.tensor
        def _(pe):
            pe.wait_ge(w_in, 64)
            for c in range(4):
                for g, w in enumerate((wi, wf)):
                    for part, src in enumerate((XnT, k.ctxT, k.ctxT)):
                        last = nc.tensor.matmul(banks[4 * g + c][0:NH, :], w[:, part, :], src[:, 512 * c:512 * c + 512],
                                                start=part == 0, stop=part == 2)
                    last.then_inc(projected, 1)
            pe.wait_ge(a_ready, 1)
            pe.wait_ge(en_ready, 1)
            for t in range(NT):
                nc.tensor.transpose(banks[0][:, NH * t:NH * t + NH], A[:, P * t:P * t + P], k.ident[0:NH, 0:NH])
                last = nc.tensor.transpose(banks[1][:, NH * t:NH * t + NH], M[:, P * t:P * t + P], k.ident[0:NH, 0:NH])
            last.then_inc(transposed, 1)

        @block.scalar
        def _(act):
            for c in range(4):
                act.wait_ge(projected, 2 * c + 2)
                nc.scalar.activation(IG[:, 512 * c:512 * c + 512], banks[c][0:NH, :], ACT.Identity, bias=bi[:, 0:1])
                nc.scalar.activation(F[:, 512 * c:512 * c + 512], banks[4 + c][0:NH, :], ACT.Identity, bias=bf[:, 0:1]).then_inc(pre_ready, 1)
            act.wait_ge(abs_ready, 1)
            nc.scalar.activation(T[:], T[:], ACT.Exp, scale=-1.0)
            act.drain()
            nc.scalar.activation(T[:], T[:], ACT.Ln, bias=k.ones[0:NH, 0:1]).then_inc(log_ready, 1)
            act.wait_ge(sum_ready, 1)
            nc.scalar.activation(M[:], CS[:], ACT.Exp, scale=-1.0).then_inc(en_ready, 1)

        @block.vector
        def _(dve):
            dve.wait_ge(pre_ready, 4)
            nc.vector.scalar_tensor_tensor(T[:], F[:], -1.0, F[:], ALU.mult, ALU.max).then_inc(abs_ready, 1)
            dve.wait_ge(log_ready, 1)
            nc.vector.scalar_tensor_tensor(F[:], F[:], 0.0, T[:], ALU.min, ALU.subtract)
            dve.drain()
            for b in range(B):
                row = slice(S * b, S * b + S)
                nc.vector.tensor_tensor_scan(CS[:, row], k.ones[0:NH, 0:S], F[:, row], 0.0, ALU.mult, ALU.add)
            dve.drain()
            nc.vector.tensor_tensor(A[:], IG[:], CS[:], ALU.subtract).then_inc(a_ready, 1)
            dve.drain()
            for b in range(B):
                row = slice(S * b, S * b + S)
                nc.vector.tensor_tensor_scan(M[:, row], A[:, row], A[:, row], -3e38, ALU.max, ALU.max)
            dve.drain()
            nc.vector.tensor_scalar(neg_max[:], M[:], -1.0, None, ALU.mult)
            nc.vector.tensor_tensor(CS[:], CS[:], M[:], ALU.add).then_inc(sum_ready, 1)
            dve.wait_ge(transposed, 1)
            nc.vector.tensor_copy(aT[:].rearrange("p t h -> p (t h)"), banks[0][:, 0:NT * NH])
            nc.vector.tensor_copy(enT[:].rearrange("p t h -> p (t h)"), banks[1][:, 0:NT * NH])


def mlstm_heads(nc, k, io, XnT, neg_max, aT, sel, HO):
    NH, HD = 8, 16
    W = S + P
    with ExitStack() as stack:
        m = Memory(nc, stack)
        q16, k16 = m.sb("q16", [HD, NH, S]), m.sb("k16", [HD, NH, S])
        a_now = m.sb("a_now", [P, TB, NH])
        DT, CT = m.sb("DT", [P, 2, W]), m.sb("CT", [P, 2, W])
        sc = [m.bank(f"mh_sc{i}") for i in range(2)]
        ex = [m.bank(f"mh_ex{i}") for i in range(2)]
        ob = m.bank("mh_out")
        split, scored, exponents, decayed, weighted, summed, stored = (
            m.sem("mh_" + n) for n in ("split", "scored", "exponents", "decayed", "weighted", "summed", "stored"))
        block = stack.enter_context(nc.Block())

        @block.sync
        def _(sp):
            def bring(b):
                for h in range(NH):
                    sp.dma_start(q16[:, h, :], XnT[HD * h:HD * h + HD, bass.ds(b * S, S)]).then_inc(split, 16)
                    sp.dma_start(k16[:, h, :], k.ctxT[HD * h:HD * h + HD, bass.ds(b * S, S)]).then_inc(split, 16)
            bring(0)
            sp.dma_start(k.v_w[:], io["L0_ffn_v_w"].rearrange("e d p -> d e p")).then_inc(k.experts_in, 16)
            sp.dma_start(k.o_w[:], io["L0_ffn_o_w"].rearrange("e p d -> p e d")).then_inc(k.experts_in, 16)
            with sp.Fori(1, B) as b:
                sp.wait_ge(scored, b * NH)
                bring(b)

        @block.tensor
        def _(pe):
            with pe.Fori(0, B) as b:
                pe.wait_ge(split, b * (32 * NH) + 32 * NH)

                def scores(h):
                    if h >= 2:
                        pe.wait_ge(weighted, b * NH + (h - 1))
                    nc.tensor.matmul(sc[h % 2][:, 0:S], k16[:, h, 0:P], q16[:, h, :], start=True, stop=True)
                    nc.tensor.matmul(sc[h % 2][:, S:W], k16[:, h, P:S], q16[:, h, P:S], start=True, stop=True).then_inc(scored, 1)
                    nc.tensor.matmul(ex[h % 2][:, 0:S], sel[:, h, :], neg_max[:, bass.ds(b * S, S)], start=True, stop=False)
                    nc.tensor.matmul(ex[h % 2][:, 0:P], k.identb[:], k.causalb[:, 1, :], start=False, stop=True)
                    nc.tensor.matmul(ex[h % 2][:, S:W], sel[:, h, :], neg_max[:, bass.ds(b * S + P, P)], start=True, stop=False)
                    nc.tensor.matmul(ex[h % 2][:, S:W], k.identb[:], k.causalb[:, 1, :], start=False, stop=True).then_inc(exponents, 1)

                scores(0)
                for h in range(NH):
                    if h + 1 < NH:
                        scores(h + 1)
                    pe.wait_ge(weighted, b * NH + (h + 1))
                    c = CT[:, h % 2, :]
                    v = lambda jt: k.ctx_ones[:, bass.ds(b * TB + jt, 1), h, :].rearrange("p a d -> p (a d)")
                    o = lambda t: ob[:, (t * NH + h) * (HD + 1):(t * NH + h + 1) * (HD + 1)]
                    nc.tensor.matmul(o(0), c[:, 0:P], v(0), start=True, stop=True)
                    nc.tensor.matmul(o(1), c[:, P:S], v(0), start=True, stop=False)
                    nc.tensor.matmul(o(1), c[:, S:W], v(1), start=False, stop=True).then_inc(summed, 1)
                pe.wait_ge(stored, b + 1)

        @block.scalar
        def _(act):
            with act.Fori(0, B) as b:
                nc.scalar.activation(a_now[:], aT[:, bass.ds(b * TB, TB), :], ACT.Copy)
                act.drain()
                for h in range(NH):
                    act.wait_ge(exponents, b * NH + (h + 1))
                    if h >= 2:
                        act.wait_ge(weighted, b * NH + (h - 1))
                    nc.scalar.activation(DT[:, h % 2, 0:S], ex[h % 2][:, 0:S], ACT.Exp, bias=a_now[:, 0, h:h + 1])
                    nc.scalar.activation(DT[:, h % 2, S:W], ex[h % 2][:, S:W], ACT.Exp, bias=a_now[:, 1, h:h + 1]).then_inc(decayed, 1)
                act.wait_ge(summed, b * NH + NH)
                nc.scalar.activation(HO[:, bass.ds(b * TB, TB), :, :].rearrange("p t h d -> p (t h d)"), ob[:, 0:TB * NH * (HD + 1)], ACT.Copy).then_inc(stored, 1)

        @block.vector
        def _(dve):
            with dve.Fori(0, B) as b:
                for h in range(NH):
                    dve.wait_ge(decayed, b * NH + (h + 1))
                    if h >= 2:
                        dve.wait_ge(summed, b * NH + (h - 1))
                    nc.vector.scalar_tensor_tensor(CT[:, h % 2, :], sc[h % 2][:, 0:W], HD ** -0.5, DT[:, h % 2, :],
                                                   ALU.mult, ALU.mult).then_inc(weighted, 1)


def mlstm_finish(nc, k, enT, HO):
    NH, HD = 8, 16
    G = NT * NH
    with ExitStack() as stack:
        m = Memory(nc, stack)
        den, ms, rms = m.sb("den", [P, G]), m.sb("ms", [P, G]), m.sb("rms", [P, G])
        Hn, SQ = m.sb("Hn", [P, G, HD]), m.sb("SQ", [P, G, HD])
        ms_ready, rms_ready = m.sem("ms_ready"), m.sem("rms_ready")
        block = stack.enter_context(nc.Block())
        ho = HO[:].rearrange("p t h d -> p (t h) d")

        @block.vector
        def _(dve):
            nc.vector.scalar_tensor_tensor(den[:], ho[:, :, HD], -1.0, ho[:, :, HD], ALU.mult, ALU.max)
            dve.drain()
            nc.vector.tensor_tensor(den[:], den[:], enT[:].rearrange("p t h -> p (t h)"), ALU.max)
            dve.drain()
            nc.vector.tensor_scalar(den[:], den[:], 1e-6, None, ALU.add)
            dve.drain()
            nc.vector.reciprocal(den[:], den[:])
            dve.drain()
            nc.vector.tensor_tensor(Hn[:], ho[:, :, 0:HD], den[:].unsqueeze(2).broadcast_to([P, G, HD]), ALU.mult)
            dve.drain()
            nc.vector.tensor_tensor(SQ[:], Hn[:], Hn[:], ALU.mult)
            dve.drain()
            nc.vector.tensor_reduce(ms[:], SQ[:], AX.X, ALU.add)
            dve.drain()
            nc.vector.tensor_scalar(ms[:], ms[:], 1.0 / HD, 1e-6, ALU.mult, ALU.add).then_inc(ms_ready, 1)
            dve.wait_ge(rms_ready, 1)
            nc.vector.tensor_tensor(Hn[:], Hn[:], rms[:].unsqueeze(2).broadcast_to([P, G, HD]), ALU.mult)
            dve.drain()
            x = k.X[:].rearrange("p t d -> p (t d)")
            nc.vector.scalar_tensor_tensor(x, Hn[:].rearrange("p g d -> p (g d)"), k.gate[:, 0:1], x, ALU.mult, ALU.add)

        @block.gpsimd
        def _(pool):
            pool.wait_ge(ms_ready, 1)
            nc.gpsimd.tensor_tensor(rms[:], ms[:], k.minus_half[:, 0:G], ALU.pow).then_inc(rms_ready, 1)


def top_two(nc, dve, p, one1, one2, m1, m2, scratch, first, rev, groups, n):
    def wide(a):
        return a.unsqueeze(2).broadcast_to([P, groups, n])
    rank = rev[:, 0:n].unsqueeze(1).broadcast_to([P, groups, n])
    for values, peak, one in ((p, m1, one1), (scratch, m2, one2)):
        if one is one2:
            nc.vector.scalar_tensor_tensor(scratch, one1, NEG, p, ALU.mult, ALU.add)
            dve.drain()
        nc.vector.tensor_reduce(peak, values, AX.X, ALU.max)
        dve.drain()
        nc.vector.tensor_tensor(scratch, values, wide(peak), ALU.is_equal)
        dve.drain()
        nc.vector.tensor_tensor(scratch, scratch, rank, ALU.mult)
        dve.drain()
        nc.vector.tensor_reduce(first, scratch, AX.X, ALU.max)
        dve.drain()
        nc.vector.tensor_tensor(one, rank, wide(first), ALU.is_equal)
        dve.drain()


def switch_head(nc, k, io):
    NH, E = 8, 8
    with ExitStack() as stack:
        m = Memory(nc, stack)
        Xn, XnT = m.sb("s_Xn", [P, NT, D]), m.sb("s_XnT", [P, NTOK])
        layer_norm(nc, k, k.X, Xn, XnT, tag="s_")
        G = m.sb("router_gates", [P, NT, 2, NH, E])
        QK = m.sb("QK", [P, NH, P])
        with ExitStack() as inner:
            switch_gates(nc, k, io, Memory(nc, inner), XnT, G, QK)
        switch_attention(nc, k, io, XnT, G, QK, Xn)
        with ExitStack() as inner:
            block = inner.enter_context(nc.Block())

            @block.vector
            def _(dve):
                nc.vector.scalar_tensor_tensor(k.X[:], Xn[:], k.gate[:, 2:3], k.X[:], ALU.mult, ALU.add)


def switch_gates(nc, k, io, m, XnT, G, QK):
    NH, E = 8, 8
    groups = NT * 2 * NH
    sel, selT = m.sb("sel_w", [P, D]), m.sb("sel_wT", [P, P])
    qn, kn = m.sb("q_w", [P, NH, D]), m.sb("k_w", [P, NH, D])
    prob, one1, one2, scratch = (m.sb("sg_" + n, [P, groups, E]) for n in ("prob", "one1", "one2", "scratch"))
    m1, m2, first, scale = (m.sb("sg_" + n, [P, groups]) for n in ("m1", "m2", "first", "scale"))
    rs = m.sb("route_scale", [P, 1])
    banks = [m.bank(f"sg_bank{i}") for i in range(4)]
    tb = m.bank("sg_selT")
    qk_bank = [m.bank(f"sg_qk{i}") for i in range(2)]
    w_in, sel_t, sel_c, qk_made, logits, exped = (m.sem("sg_" + n) for n in ("w_in", "sel_t", "sel_c", "qk_made", "logits", "exped"))
    block = m.stack.enter_context(nc.Block())

    @block.sync
    def _(sp):
        sp.dma_start(sel[0:64, :], io["L0_ffn_sel_v_w"]).then_inc(w_in, 16)
        sp.dma_start(sel[64:128, :], io["L0_ffn_sel_o_w"]).then_inc(w_in, 16)
        sp.dma_start(rs[:], io["L0_ffn_route_scale"].rearrange("(a n) -> a n", a=1).broadcast_to([P, 1])).then_inc(w_in, 16)
        sp.dma_start(qn[:], io["L0_ffn_q_w"].rearrange("(h p) d -> p h d", p=P)).then_inc(w_in, 16)
        sp.dma_start(kn[:], io["L0_ffn_k_w"].rearrange("(h p) d -> p h d", p=P)).then_inc(w_in, 16)

    @block.tensor
    def _(pe):
        pe.wait_ge(w_in, 80)
        nc.tensor.transpose(tb[:, 0:P], sel[:], k.ident[:]).then_inc(sel_t, 1)
        pe.wait_ge(sel_c, 1)
        for t in range(NT):
            nc.tensor.matmul(banks[t // 4][:, t % 4 * P:t % 4 * P + P], XnT[:, P * t:P * t + P], selT[:],
                             start=True, stop=True).then_inc(logits, 1)
        for h in range(NH):
            nc.tensor.matmul(qk_bank[h // 4][:, h % 4 * P:h % 4 * P + P], qn[:, h, :], kn[:, h, :],
                             start=True, stop=True).then_inc(qk_made, 1)

    @block.scalar
    def _(act):
        act.wait_ge(sel_t, 1)
        nc.scalar.activation(selT[:], tb[:, 0:P], ACT.Copy).then_inc(sel_c, 1)
        flat = prob[:].rearrange("p g e -> p (g e)")
        for c in range(4):
            act.wait_ge(logits, 4 * c + 4)
            nc.scalar.activation(flat[:, 512 * c:512 * c + 512], banks[c][:], ACT.Exp, scale=-1.0).then_inc(exped, 1)
        for c in range(2):
            act.wait_ge(qk_made, 4 * c + 4)
            nc.scalar.activation(QK[:, 4 * c:4 * c + 4, :].rearrange("p h d -> p (h d)"), qk_bank[c][:], ACT.Copy)

    @block.vector
    def _(dve):
        dve.wait_ge(exped, 4)
        nc.vector.tensor_scalar(prob[:], prob[:], 1.0, None, ALU.add)
        dve.drain()
        nc.vector.reciprocal(prob[:], prob[:])
        dve.drain()
        top_two(nc, dve, prob[:], one1[:], one2[:], m1[:], m2[:], scratch[:], first[:], k.rev, groups, E)
        nc.vector.tensor_tensor(scale[:], m1[:], m2[:], ALU.add)
        dve.drain()
        nc.vector.tensor_scalar(scale[:], scale[:], 1e-9, None, ALU.max)
        dve.drain()
        nc.vector.reciprocal(scale[:], scale[:])
        nc.vector.tensor_tensor(one1[:], one1[:], one2[:], ALU.add)
        dve.drain()
        dve.wait_ge(w_in, 80)
        nc.vector.tensor_scalar(scale[:], scale[:], rs[:, 0:1], None, ALU.mult)
        nc.vector.tensor_tensor(prob[:], prob[:], one1[:], ALU.mult)
        dve.drain()
        nc.vector.tensor_tensor(G[:].rearrange("p t c h e -> p (t c h) e"), prob[:],
                                scale[:].unsqueeze(2).broadcast_to([P, groups, E]), ALU.mult)


def switch_attention(nc, k, io, XnT, G, QK, out):
    NH, E = 8, 8
    STEPS = 4 * NH
    with ExitStack() as stack:
        m = Memory(nc, stack)
        xb, zT, prob, probT, cT = m.sb("xb", [P, S]), m.sb("zT", [P, S]), m.sb("sa_prob", [P, TB, S]), m.sb("sa_probT", [P, TB, S]), m.sb("cT", [P, S])
        values, rec = m.sb("sa_values", [P, 2, TB, P]), m.sb("sa_rec", [P, TB])
        neg_max, total, wo = m.sb("sa_neg_max", [P, TB]), m.sb("sa_total", [P, TB]), m.sb("sa_wo", [P, TB, E])
        product = m.sb("sa_product", [P, 2, E, P])
        pair = [m.bank(f"sa_pair{i}", cols=1024) for i in range(2)]
        sb_, tb_, zb_, cb_ = m.bank("sa_scores"), m.bank("sa_probT_bank"), m.bank("sa_z_bank"), m.bank("sa_ctx_bank")
        sem = lambda n: m.sem("sa_" + n)
        xb_ready, z_made, z_copied, scored, maxed = (sem(n) for n in ("xb_ready", "z_made", "z_copied", "scored", "maxed"))
        exped, turned, turn_copied, ctx_made, ctx_copied = (sem(n) for n in ("exped", "turned", "turn_copied", "ctx_made", "ctx_copied"))
        pair_made, product_made, halved, product_free, values_ready = (sem(n) for n in ("pair_made", "product_made", "halved", "product_free", "values_ready"))
        block = stack.enter_context(nc.Block())

        @block.tensor
        def _(pe):
            pe.wait_ge(k.experts_in, k.EXPERTS_IN)
            with pe.Fori(0, B) as b:
                pe.wait_ge(xb_ready, b + 1)

                def z(h):
                    nc.tensor.matmul(zb_[:, 0:S], QK[:, h, :], xb[:], start=True, stop=True).then_inc(z_made, 1)

                def scores(h):
                    pe.wait_ge(z_copied, b * NH + (h + 1))
                    for t in range(TB):
                        last = nc.tensor.matmul(sb_[:, S * t:S * t + S], zT[:, P * t:P * t + P], xb[:], start=True, stop=True)
                    last.then_inc(scored, 1)

                def experts(n, lhsT, w, h):
                    pe.wait_ge(product_made, b * STEPS + (n + 1))
                    for half in range(2):
                        last = nc.tensor.matmul(pair[n % 2][:, 512 * half:512 * half + 512], lhsT,
                                                w[:, E * h + 4 * half:E * h + 4 * half + 4, :].rearrange("p e d -> p (e d)"),
                                                start=True, stop=True)
                    last.then_inc(pair_made, 1)
                    return last

                def expert_values(h):
                    for t in range(TB):
                        experts(4 * h - 2 + t if h else t, xb[:, P * t:P * t + P], k.v_w, h)

                z(0)
                scores(0)
                expert_values(0)
                for h in range(NH):
                    pe.wait_ge(exped, b * NH + (h + 1))
                    for kt in range(TB):
                        for t in range(TB):
                            last = nc.tensor.transpose(tb_[:, S * kt + P * t:S * kt + P * t + P], prob[:, t, P * kt:P * kt + P], k.ident[:])
                    last.then_inc(turned, 1)
                    if h + 1 < NH:
                        z(h + 1)
                        expert_values(h + 1)
                    pe.wait_ge(turn_copied, b * NH + (h + 1))
                    pe.wait_ge(values_ready, b * (2 * NH) + (2 * h + 2))
                    for kt in range(TB):
                        last = nc.tensor.matmul(cb_[:, 0:S], values[:, h % 2, kt, :], probT[:, kt, :], start=kt == 0, stop=kt == 1)
                    last.then_inc(ctx_made, 1)
                    if h + 1 < NH:
                        scores(h + 1)
                    pe.wait_ge(ctx_copied, b * NH + (h + 1))
                    for t in range(TB):
                        experts(min(4 * h + 4, STEPS - 2) + t, cT[:, P * t:P * t + P], k.o_w, h)

        @block.scalar
        def _(act):
            with act.Fori(0, B) as b:
                nc.scalar.activation(xb[:], XnT[:, bass.ds(b * S, S)], ACT.Copy).then_inc(xb_ready, 1)

                def copy_z(h):
                    act.wait_ge(z_made, b * NH + (h + 1))
                    nc.scalar.activation(zT[:], zb_[:, 0:S], ACT.Copy, scale=float(P) ** -0.5).then_inc(z_copied, 1)

                def exps(h):
                    act.wait_ge(maxed, b * NH + (h + 1))
                    for t in range(TB):
                        last = nc.scalar.activation(prob[:, t, :], sb_[:, S * t:S * t + S], ACT.Exp, bias=neg_max[:, t:t + 1],
                                                    accum_out=total[:, t:t + 1])
                    last.then_inc(exped, 1)

                copy_z(0)
                exps(0)
                for h in range(NH):
                    act.wait_ge(turned, b * NH + (h + 1))
                    nc.scalar.activation(probT[:].rearrange("p a s -> p (a s)"), tb_[:], ACT.Copy).then_inc(turn_copied, 1)
                    if h + 1 < NH:
                        copy_z(h + 1)
                    act.wait_ge(ctx_made, b * NH + (h + 1))
                    nc.scalar.activation(cT[:], cb_[:, 0:S], ACT.Copy).then_inc(ctx_copied, 1)
                    if h + 1 < NH:
                        exps(h + 1)

        @block.vector
        def _(dve):
            dve.sem_inc(product_made, 2)
            with dve.Fori(0, B) as b:
                def find_max(h):
                    dve.wait_ge(scored, b * NH + (h + 1))
                    nc.vector.tensor_reduce(neg_max[:], sb_[:].rearrange("p (t s) -> p t s", t=TB), AX.X, ALU.max,
                                            negate=True).then_inc(maxed, 1)

                def gated(n, gate):
                    dve.wait_ge(pair_made, b * STEPS + (n + 1))
                    dve.wait_ge(product_free, b * STEPS + (n + 1))
                    nc.vector.tensor_tensor(product[:, n % 2, :, :], pair[n % 2][:].rearrange("p (e d) -> p e d", e=E),
                                            gate.unsqueeze(2).broadcast_to([P, E, P]), ALU.mult).then_inc(product_made, 1)
                    dve.drain()
                    p = product[:, n % 2, :, :]
                    nc.vector.tensor_tensor(p[:, 0:4, :], p[:, 0:4, :], p[:, 4:8, :], ALU.add).then_inc(halved, 1)

                def gated_values(h):
                    for t in range(TB):
                        gated(4 * h - 2 + t if h else t, G[:, bass.ds(b * TB + t, 1), 0, h, :].rearrange("p a e -> p (a e)"))

                find_max(0)
                gated_values(0)
                for h in range(NH):
                    if h + 1 < NH:
                        gated_values(h + 1)
                    dve.wait_ge(exped, b * NH + (h + 1))
                    nc.vector.reciprocal(rec[:], total[:])
                    dve.drain()
                    for t in range(TB):
                        nc.vector.tensor_scalar(wo[:, t, :], G[:, bass.ds(b * TB + t, 1), 1, h, :].rearrange("p a e -> p (a e)"),
                                                rec[:, t:t + 1], None, ALU.mult)
                    if h + 1 < NH:
                        find_max(h + 1)
                    dve.drain()
                    for t in range(TB):
                        gated(min(4 * h + 4, STEPS - 2) + t, wo[:, t, :])

        @block.gpsimd
        def _(pool):
            pool.sem_inc(product_free, 2)
            with pool.Fori(0, B) as b:
                for n in range(STEPS):
                    is_values = n < 2 or (n % 4 >= 2 and n < STEPS - 2)
                    h, t = (n + 2) // 4 if is_values else (n - 4) // 4 if n < STEPS - 2 else NH - 1, n % 2
                    pool.wait_ge(halved, b * STEPS + (n + 1))
                    p = product[:, n % 2, :, :]
                    nc.gpsimd.tensor_tensor(p[:, 0:2, :], p[:, 0:2, :], p[:, 2:4, :], ALU.add)
                    pool.drain()
                    if is_values:
                        nc.gpsimd.tensor_tensor(values[:, h % 2, t, :], p[:, 0, :], p[:, 1, :], ALU.add).then_inc(values_ready, 1)
                        pool.drain().then_inc(product_free, 1)
                        continue
                    y = out[:, bass.ds(b * TB + t, 1), :].rearrange("p a d -> p (a d)")
                    if h == 0:
                        nc.gpsimd.tensor_tensor(y, p[:, 0, :], p[:, 1, :], ALU.add)
                    else:
                        nc.gpsimd.tensor_tensor(p[:, 0, :], p[:, 0, :], p[:, 1, :], ALU.add)
                        pool.drain()
                        nc.gpsimd.tensor_tensor(y, y, p[:, 0, :], ALU.add)
                    pool.drain().then_inc(product_free, 1)


WQ, WK, WV, WO_S, WQ_C, WK_C, WV_C, WO_C, WG, WU, WD = 0, 1, 2, 3, 4, 5, 6, 7, 8, 12, 16
BLOCKS = 20


def decoder(nc, k, io):
    with ExitStack() as stack:
        m = Memory(nc, stack)
        XX = m.sb("d_XX", [P, NT, D])
        layer_norm(nc, k, k.X, XX, tag="d_")
        c = DecoderConstants(m)
        decoder_constants(nc, k, io, c)
        decoder_layers(nc, k, io, c, XX)
        decoder_end(nc, k, c, XX)


class DecoderConstants:

    def __init__(self, m):
        self.cos, self.sin = m.sb("cos", [P, S]), m.sb("sin", [P, S])
        self.rot = m.sb("rot", [P, P])
        self.own = m.sb("own", [P, 4])
        self.blocked = m.sb("blocked", [P, NT, S], BF16)
        self.norms, self.bias_qk = m.sb("norms", [P, 3, LAYERS]), m.sb("bias_qk", [P, LAYERS, 2])
        self.bias_v, self.bias_o = m.sb("bias_v", [P, LAYERS, D]), m.sb("bias_o", [P, LAYERS, D])
        self.nf = m.sb("nf", [P, D])


def decoder_constants(nc, k, io, c):
    SCALE = 8 ** -0.5
    with ExitStack() as stack:
        m = Memory(nc, stack)
        ids, seg, low = m.sb("ids", [P, NT], mybir.dt.int32), m.sb("seg", [P, NT]), m.sb("low", [P, NT])
        jj, key = m.sb("jj", [P, S], mybir.dt.int32), m.sb("key", [P, S])
        above, below = m.sb("above", [P, NT, S]), m.sb("below", [P, NT, S])
        own = c.own
        loaded, iota_made = m.sem("dc_loaded"), m.sem("dc_iota_made")
        block = stack.enter_context(nc.Block())

        @block.sync
        def _(sp):
            def load(dst, src):
                sp.dma_start(dst, src).then_inc(loaded, 16)
            with nc.allow_non_contiguous_dma("small parameters, a column each"):
                load(ids[:], io["itok_BxS_0_255"].rearrange("b (t p) -> p (b t)", p=P))
                load(c.cos[:], io["rope_cos"])
                load(c.sin[:], io["rope_sin"])
                load(c.rot[:], io["rope_turn"])
                load(c.own[:], io["head_of_quadrant"])
                for i, n in enumerate(("n1", "n2", "n3")):
                    load(c.norms[:, i, :], io["L1_xattn_" + n].rearrange("l d -> d l"))
                for i in range(2):
                    load(c.bias_qk[:, :, i], io["L1_xattn_bqkv"][:, D * i:D * i + D].rearrange("l d -> d l"))
                load(c.bias_v[:], io["L1_xattn_bqkv"][:, 2 * D:3 * D].rearrange("(a l) d -> a l d", a=1).broadcast_to([P, LAYERS, D]))
                load(c.bias_o[:], io["L1_xattn_bo"].rearrange("(a l) d -> a l d", a=1).broadcast_to([P, LAYERS, D]))
                load(c.nf[:], io["L1_xattn_nf"].rearrange("(a d) -> a d", a=1).broadcast_to([P, D]))

        @block.gpsimd
        def _(pool):
            nc.gpsimd.iota(jj[:], pattern=[[1, S]], base=0, channel_multiplier=0)
            pool.drain()
            nc.gpsimd.tensor_copy(key[:], jj[:]).then_inc(iota_made, 1)

        @block.vector
        def _(dve):
            dve.wait_ge(loaded, 13 * 16)
            nc.vector.tensor_copy(seg[:], ids[:])
            nc.vector.tensor_scalar(c.bias_qk[:, :, 0], c.bias_qk[:, :, 0], SCALE, None, ALU.mult)
            dve.drain()
            nc.vector.tensor_scalar(low[:], seg[:], -128.0, None, ALU.add)
            dve.wait_ge(iota_made, 1)
            dve.drain()
            for t in range(NT):
                nc.vector.tensor_scalar(above[:, t, :], key[:], seg[:, t:t + 1], NEG, ALU.is_gt, ALU.mult)
                nc.vector.tensor_scalar(below[:, t, :], key[:], low[:, t:t + 1], NEG, ALU.is_le, ALU.mult)
            dve.drain()
            nc.vector.tensor_tensor(c.blocked[:], above[:], below[:], ALU.add)


def decoder_layers(nc, k, io, c, XX):
    NH, HD, PAIRS = 16, 8, B // 2
    GROUPS, HG = 2, NH // 2
    ROWS = P // HG
    SLOT = P + ROWS
    SCALE = HD ** -0.5
    W_LOADS = 8
    SELF, CROSS = 0, 1
    TURNS = [(0, SELF), (1, SELF), (0, CROSS), (1, CROSS)]
    FIRST_AT, MIDDLE_AT, END_AT = (1, 4, 7, 9), (1, 3, 5, 8, 10), (1, 3, 5, 7, 9, 11, 13)
    with ExitStack() as stack:
        m = Memory(nc, stack)
        WN, WT = m.sb("d_WN", [P, BLOCKS, P]), m.sb("d_WT", [P, BLOCKS, P])
        norm_w, bias, bias_v = m.sb("d_norm_w", [P, 3]), m.sb("d_bias", [P, 2]), m.sb("d_bias_v", [P, D])

        def rows(name, shape):
            return [m.sb(f"d_{name}{r}", shape) for r in range(2)]
        mem = rows("mem", [P, S])
        ss, rs, h, hT = rows("ss", [P, TB]), rows("rs", [P, TB]), rows("h", [P, TB, D]), rows("hT", [P, S])
        qm = rows("qm", [P, 4, S])
        kr, kc, qc = rows("kr", [P, S]), rows("kc", [P, S]), rows("qc", [P, S])
        V, VC = rows("V", [P, TB, GROUPS, HG * SLOT]), rows("VC", [P, TB, GROUPS, HG * SLOT])
        OT, o, oT = rows("OT", [P, GROUPS, S]), rows("o", [P, TB, D]), rows("oT", [P, S])
        qk, turned_sin, qr = m.sb("d_qk", [P, 2, S]), m.sb("d_turned_sin", [P, 2, S]), rows("qr", [P, S])
        rec, proj = m.sb("d_rec", [P, TB, NH]), m.sb("d_proj", [P, TB, D])
        tg, aT = m.sb("d_tg", [P, 2, S]), m.sb("d_aT", [P, 4, S])
        neg_max = m.sb("d_neg_max", [P, 4, TB])
        prob, probT = m.sb("d_prob", [P, 2, 512]), m.sb("d_probT", [P, 2, 512])
        A = [m.bank(f"d_A{i}") for i in range(2)]
        T = [m.bank(f"d_T{i}") for i in range(2)]
        O = [m.bank(f"d_O{i}") for i in range(2)]
        G = [m.bank(f"d_G{i}") for i in range(2)]
        sem = lambda n: m.sem("dl_" + n)
        both = lambda n: [sem(n + str(r)) for r in range(2)]
        w_in, w_read, w_turned, w_ready, zeros_set = (sem(n) for n in ("w_in", "w_read", "w_turned", "w_ready", "zeros_set"))
        ss_ready, r_ready, h_ready, h_turned, hT_ready = (both(n) for n in ("ss_ready", "r_ready", "h_ready", "h_turned", "hT_ready"))
        qk_made, qk_biased, qk_turned, roped, queries_ready = (both(n) for n in ("qk_made", "qk_biased", "qk_turned", "roped", "queries_ready"))
        mem_ready, kc_made, kc_ready, vc_made, vc_ready, v_made, v_ready, qc_made, qc_ready = (
            both(n) for n in ("mem_ready", "kc_made", "kc_ready", "vc_made", "vc_ready", "v_made", "v_ready", "qc_made", "qc_ready"))
        scored, maxed, exped, turned, turn_copied, attended, O_copied = (
            sem(n) for n in ("scored", "maxed", "exped", "turned", "turn_copied", "attended", "O_copied"))
        O_turned, o_ready, o_turned, oT_ready, projected = (both(n) for n in ("O_turned", "o_ready", "o_turned", "oT_ready", "projected"))
        gated, upped, tanhed, act_ready, downed, row_done = (both(n) for n in ("gated", "upped", "tanhed", "act_ready", "downed", "row_done"))
        block = stack.enter_context(nc.Block())

        TILES = {SELF: [(0, P, 0), (1, S, P)], CROSS: [(0, S, 0), (1, S, S)]}
        WIDTH = {SELF: P + S, CROSS: 2 * S}
        BLOCKS_OF = {SELF: [(0, 0), (P, P), (2 * P, 2 * P)], CROSS: [(0, 0), (S, P), (P, S), (S + P, S + P)]}
        WEIGHTED = {SELF: [(0, 0, S, 0), (1, P, P, S)], CROSS: [(0, 0, S, 0), (1, 0, S, S)]}

        def place(n):
            return n // 4, n % 4

        def value_columns(v, kt, n):
            g, i = n // HG, n % HG
            return v[:, kt, g, P * i:P * i + P]

        def value_slots(v):
            return v[:].rearrange("p t g (n w) -> p (t g) n w", w=SLOT)

        @block.sync
        def _(sp):
            with sp.Fori(0, LAYERS) as l:
                sp.wait_ge(w_read, l + 1)
                def load(at, n, name, cols):
                    w = io["L1_xattn_" + name][bass.ds(l, 1)]
                    if cols:
                        src = w.rearrange("a p (c d) -> p (a c) d", c=n)
                    else:
                        src = w.rearrange("a (c p) d -> p (a c) d", c=n)
                    sp.dma_start(WN[:, at:at + n, :], src).then_inc(w_in, 16)
                load(WQ, 3, "Wqkv", False)
                load(WO_S, 1, "Wo", False)
                load(WQ_C, 1, "Wq_c", False)
                load(WK_C, 2, "Wkv_c", False)
                load(WO_C, 1, "Wo_c", False)
                load(WG, 4, "Wg", False)
                load(WU, 4, "Wu", False)
                load(WD, 4, "Wd", True)

        @block.tensor
        def _(pe):
            pe.sem_inc(w_read, 1)
            pe.wait_ge(zeros_set, 1)
            with pe.Fori(0, LAYERS) as l:
                pe.wait_ge(w_in, l * (16 * W_LOADS) + 16 * W_LOADS)
                for g in range(BLOCKS // 4):
                    bank = (A + T + O)[g]
                    for i in range(4):
                        last = nc.tensor.transpose(bank[:, P * i:P * i + P], WN[:, 4 * g + i, :], k.ident[:])
                    last.then_inc(w_turned, 1)
                pe.wait_ge(w_ready, l + 1)
                pe.sem_inc(w_read, 1)

                with pe.Fori(0, PAIRS) as bp:
                    it = l * PAIRS + bp

                    def memory(r):
                        pe.wait_ge(mem_ready[r], it + 1)
                        nc.tensor.matmul(G[0][:, 0:S], WT[:, WK_C, :], mem[r][:], start=True, stop=True).then_inc(kc_made[r], 1)
                        for t in range(TB):
                            last = nc.tensor.matmul(G[1][:, P * t:P * t + P], mem[r][:, P * t:P * t + P], WT[:, WV_C, :], start=True, stop=True)
                        last.then_inc(vc_made[r], 1)
                        pe.wait_ge(kc_ready[r], it + 1)

                    def turn_h(r, j):
                        pe.wait_ge(h_ready[r], it * 3 + (j + 1))
                        for t in range(TB):
                            last = nc.tensor.transpose(G[0][:, P * t:P * t + P], h[r][:, t, :], k.ident[:])
                        last.then_inc(h_turned[r], 1)

                    def project_self(r):
                        pe.wait_ge(hT_ready[r], it * 3 + 1)
                        pe.wait_ge(vc_ready[r], it + 1)
                        for i, w in enumerate((WQ, WK)):
                            last = nc.tensor.matmul(G[1][:, S * i:S * i + S], WT[:, w, :], hT[r][:], start=True, stop=True)
                        last.then_inc(qk_made[r], 1)
                        for t in range(TB):
                            last = nc.tensor.matmul(G[0][:, P * t:P * t + P], hT[r][:, P * t:P * t + P], WT[:, WV, :], start=True, stop=True)
                        last.then_inc(v_made[r], 1)

                    def turn_qk(r):
                        pe.wait_ge(qk_biased[r], it + 1)
                        nc.tensor.matmul(G[1][:], c.rot[:], qk[:].rearrange("p c s -> p (c s)"), start=True, stop=True).then_inc(qk_turned[r], 1)

                    def turn_O(r, a):
                        pe.wait_ge(O_copied, it * 4 + (2 * a + r + 2))
                        for t in range(TB):
                            for g in range(GROUPS):
                                at = (t * GROUPS + g) * P
                                last = nc.tensor.transpose(G[0][:, at:at + P], OT[r][:, g, P * t:P * t + P], k.ident[:])
                        last.then_inc(O_turned[r], 1)

                    def turn_o(r, a):
                        pe.wait_ge(o_ready[r], it * 2 + (a + 1))
                        for t in range(TB):
                            last = nc.tensor.transpose(G[0][:, P * t:P * t + P], o[r][:, t, :], k.ident[:])
                        last.then_inc(o_turned[r], 1)

                    def project_out(r, a):
                        pe.wait_ge(oT_ready[r], it * 2 + (a + 1))
                        for t in range(TB):
                            last = nc.tensor.matmul(G[1][:, P * t:P * t + P], oT[r][:, P * t:P * t + P], WT[:, (WO_S, WO_C)[a], :], start=True, stop=True)
                        last.then_inc(projected[r], 1)

                    def project_cross(r):
                        pe.wait_ge(hT_ready[r], it * 3 + 2)
                        nc.tensor.matmul(G[1][:, 0:S], WT[:, WQ_C, :], hT[r][:], start=True, stop=True).then_inc(qc_made[r], 1)

                    def feed(r, i):
                        pe.wait_ge(hT_ready[r], it * 3 + 3)
                        if i:
                            pe.wait_ge(act_ready[r], it * 2 + 1)
                        for w, bank, made in ((WG, G[0], gated[r]), (WU, G[1], upped[r])):
                            for f in range(2):
                                last = nc.tensor.matmul(bank[:, S * f:S * f + S], WT[:, w + 2 * i + f, :], hT[r][:], start=True, stop=True)
                            last.then_inc(made, 1)

                    def down(r):
                        pe.wait_ge(act_ready[r], it * 2 + 2)
                        for t in range(TB):
                            for f in range(4):
                                last = nc.tensor.matmul(G[1][:, P * t:P * t + P], aT[:, f, P * t:P * t + P], WT[:, WD + f, :], start=f == 0, stop=f == 3)
                        last.then_inc(downed[r], 1)

                    def first(r, step):
                        if step == 0:
                            memory(r)
                        elif step == 1:
                            turn_h(r, 0)
                        elif step == 2:
                            project_self(r)
                        elif step == 3:
                            turn_qk(r)

                    def middle(r, step):
                        if step == 0:
                            turn_O(r, SELF)
                        elif step == 1:
                            turn_o(r, SELF)
                        elif step == 2:
                            project_out(r, SELF)
                        elif step == 3:
                            turn_h(r, 1)
                        elif step == 4:
                            project_cross(r)

                    def end(r, step):
                        if step == 0:
                            turn_O(r, CROSS)
                        elif step == 1:
                            turn_o(r, CROSS)
                        elif step == 2:
                            project_out(r, CROSS)
                        elif step == 3:
                            turn_h(r, 2)
                        elif step == 4:
                            feed(r, 0)
                        elif step == 5:
                            feed(r, 1)
                        elif step == 6:
                            down(r)

                    def steps_after(turn, n):
                        if turn == 0 and n in FIRST_AT:
                            first(1, FIRST_AT.index(n))
                        if turn in (1, 2) and n in MIDDLE_AT:
                            middle(turn - 1, MIDDLE_AT.index(n))
                        if turn == 3 and n in END_AT:
                            end(0, END_AT.index(n))

                    def scores(turn, n):
                        r, kind = TURNS[turn]
                        if n == 0:
                            pe.wait_ge(queries_ready[r], it * 2 + (kind + 1))
                            if kind == SELF:
                                pe.wait_ge(v_ready[r], it + 1)
                        j, quadrant = place(n)
                        at = 32 * quadrant
                        keys = (kr, kc)[kind][r]
                        for t, keys_n, col in TILES[kind]:
                            nc.tensor.matmul(A[n % 2][:, col:col + keys_n], qm[r][at:at + 32, j, P * t:P * t + P], keys[at:at + 32, 0:keys_n],
                                             start=True, stop=False)
                            if kind == SELF:
                                d = col + t * P
                                last = nc.tensor.matmul(A[n % 2][:, d:d + P], k.identb[:], k.causalb[:, 0, :], start=False, stop=True)
                            else:
                                last = nc.tensor.matmul(A[n % 2][:, col:col + keys_n], k.identb[:],
                                                        c.blocked[:, bass.ds(bp * (2 * TB) + (r * TB + t), 1), :].rearrange("p a s -> p (a s)"),
                                                        start=False, stop=True)
                        last.then_inc(scored, 1)

                    def weighted(turn, n):
                        r, kind = TURNS[turn]
                        pe.wait_ge(turn_copied, it * (4 * NH) + (turn * NH + n + 1))
                        if n == 0:
                            pe.wait_ge(O_copied, it * 4 + (turn + 1))
                        for kt, q0, queries, col in WEIGHTED[kind]:
                            last = nc.tensor.matmul(O[n // HG][:, q0:q0 + queries], value_columns((V, VC)[kind][r], kt, n),
                                                    probT[:, n % 2, col:col + queries], start=n % HG == 0 and kt == 0, stop=n % HG == HG - 1 and kt == 1)
                        if n == NH - 1:
                            last.then_inc(attended, 1)

                    for step in range(4):
                        first(0, step)
                    scores(0, 0)
                    scores(0, 1)
                    for turn in range(4):
                        kind = TURNS[turn][1]
                        for n in range(NH):
                            pe.wait_ge(exped, it * (4 * NH) + (turn * NH + n + 1))
                            for col, colT in BLOCKS_OF[kind]:
                                last = nc.tensor.transpose(T[n % 2][:, colT:colT + P], prob[:, n % 2, col:col + P], k.ident[:])
                            last.then_inc(turned, 1)
                            if n + 2 < NH:
                                scores(turn, n + 2)
                            elif turn < 3:
                                scores(turn + 1, n + 2 - NH)
                            if n:
                                weighted(turn, n - 1)
                            steps_after(turn, n)
                        weighted(turn, NH - 1)
                    for step in range(7):
                        end(1, step)
                    pe.wait_ge(row_done[1], it + 1)

        @block.scalar
        def _(act):
            act.sem_inc(O_copied, 1)
            with act.Fori(0, LAYERS) as l:
                for g in range(BLOCKS // 4):
                    act.wait_ge(w_turned, l * (BLOCKS // 4) + (g + 1))
                    last = nc.scalar.activation(WT[:, 4 * g:4 * g + 4, :].rearrange("p c d -> p (c d)"), (A + T + O)[g][:], ACT.Copy)
                nc.scalar.activation(norm_w[:], c.norms[:, :, bass.ds(l, 1)].rearrange("p n a -> p (n a)"), ACT.Copy)
                nc.scalar.activation(bias[:], c.bias_qk[:, bass.ds(l, 1), :].rearrange("p a n -> p (a n)"), ACT.Copy)
                act.drain().then_inc(w_ready, 1)
                with act.Fori(0, PAIRS) as bp:
                    it = l * PAIRS + bp

                    def copy_kc(r):
                        act.wait_ge(kc_made[r], it + 1)
                        nc.scalar.activation(kc[r][:], G[0][:, 0:S], ACT.Copy).then_inc(kc_ready[r], 1)

                    def copy_h(r, j):
                        act.wait_ge(h_turned[r], it * 3 + (j + 1))
                        nc.scalar.activation(hT[r][:], G[0][:, 0:S], ACT.Copy, scale=norm_w[:, j:j + 1]).then_inc(hT_ready[r], 1)

                    def copy_qk(r):
                        act.wait_ge(qk_made[r], it + 1)
                        nc.scalar.activation(qk[:, 0, :], G[1][:, 0:S], ACT.Identity, scale=SCALE, bias=bias[:, 0:1])
                        nc.scalar.activation(qk[:, 1, :], G[1][:, S:2 * S], ACT.Identity, bias=bias[:, 1:2]).then_inc(qk_biased[r], 1)

                    def copy_o(r, a):
                        act.wait_ge(o_turned[r], it * 2 + (a + 1))
                        nc.scalar.activation(oT[r][:], G[0][:, 0:S], ACT.Copy).then_inc(oT_ready[r], 1)

                    def copy_qc(r):
                        act.wait_ge(qc_made[r], it + 1)
                        nc.scalar.activation(qc[r][:], G[1][:, 0:S], ACT.Copy, scale=SCALE).then_inc(qc_ready[r], 1)

                    def tanh(r, i):
                        act.wait_ge(gated[r], it * 2 + (i + 1))
                        nc.scalar.activation(tg[:].rearrange("p f s -> p (f s)"), G[0][:], ACT.Tanh, scale=0.5).then_inc(tanhed[r], 1)

                    def first(r, step):
                        if step == 0:
                            copy_kc(r)
                        elif step == 1:
                            copy_h(r, 0)
                        elif step == 2:
                            copy_qk(r)

                    def middle(r, step):
                        if step == 1:
                            copy_o(r, SELF)
                        elif step == 3:
                            copy_h(r, 1)
                        elif step == 4:
                            copy_qc(r)

                    def end(r, step):
                        if step == 1:
                            copy_o(r, CROSS)
                        elif step == 3:
                            copy_h(r, 2)
                        elif step in (4, 5):
                            tanh(r, step - 4)

                    def steps_after(turn, n):
                        if turn == 0 and n in FIRST_AT:
                            first(1, FIRST_AT.index(n))
                        if turn in (1, 2) and n in MIDDLE_AT:
                            middle(turn - 1, MIDDLE_AT.index(n))
                        if turn == 3 and n in END_AT:
                            end(0, END_AT.index(n))

                    def exps(turn, n):
                        kind = TURNS[turn][1]
                        act.wait_ge(maxed, it * (4 * NH) + (turn * NH + n + 1))
                        for t, keys_n, col in TILES[kind]:
                            last = nc.scalar.activation(prob[:, n % 2, col:col + keys_n], A[n % 2][:, col:col + keys_n], ACT.Exp,
                                                        bias=neg_max[:, n % 4, t:t + 1])
                        last.then_inc(exped, 1)

                    def copy_O(turn):
                        r = TURNS[turn][0]
                        act.wait_ge(attended, it * 4 + (turn + 1))
                        for g in range(GROUPS):
                            last = nc.scalar.activation(OT[r][:, g, :], O[g][:, 0:S], ACT.Copy)
                        last.then_inc(O_copied, 1)

                    for r in range(2):
                        nc.scalar.activation(mem[r][:], k.ctxT[:, bass.ds(bp * (2 * S) + r * S, S)], ACT.Copy).then_inc(mem_ready[r], 1)
                    for step in range(4):
                        first(0, step)
                    for turn in range(4):
                        for n in range(NH):
                            exps(turn, n)
                            if turn and n == 0:
                                copy_O(turn - 1)
                            if n >= 2:
                                steps_after(turn, n - 2)
                    copy_O(3)
                    for step in range(7):
                        end(1, step)

        @block.gpsimd
        def _(pool):
            with pool.Fori(0, LAYERS * PAIRS) as it:
                def root(r, j):
                    pool.wait_ge(ss_ready[r], it * 3 + (j + 1))
                    nc.gpsimd.tensor_tensor(rs[r][:], ss[r][:], k.minus_half[:, 0:TB], ALU.pow).then_inc(r_ready[r], 1)

                def mask(r, src):
                    nc.gpsimd.tensor_tensor(qm[r][:], src.unsqueeze(1).broadcast_to([P, 4, S]), c.own[:].unsqueeze(2).broadcast_to([P, 4, S]),
                                            ALU.mult).then_inc(queries_ready[r], 1)

                for r in range(2):
                    root(r, 0)
                    pool.wait_ge(roped[r], it + 1)
                    mask(r, qr[r][:])
                for r in range(2):
                    root(r, 1)
                    pool.wait_ge(qc_ready[r], it + 1)
                    mask(r, qc[r][:])
                for r in range(2):
                    root(r, 2)

        @block.vector
        def _(dve):
            for v in V + VC:
                nc.vector.memset(v[:], 0.0)
            dve.drain()
            for v in V + VC:
                nc.vector.memset(value_slots(v)[:, :, :, HD:HD + 1], 1.0)
            dve.drain().then_inc(zeros_set, 1)
            with dve.Fori(0, LAYERS) as l:
                with dve.Fori(0, PAIRS) as bp:
                    it = l * PAIRS + bp

                    def row(r):
                        return XX[:, bass.ds(bp * (2 * TB) + r * TB, TB), :]

                    def slots(v):
                        return v[:].rearrange("p t g (n w) -> p t (g n) w", w=SLOT)[:, :, :, 0:HD]

                    def copy_vc(r):
                        dve.wait_ge(vc_made[r], it + 1)
                        for t in range(TB):
                            last = nc.vector.tensor_copy(slots(VC[r])[:, t].rearrange("p (j q) d -> p j q d", j=4),
                                                         G[1][:, P * t:P * t + P].rearrange("p (q j d) -> p j q d", q=4, j=4))
                        last.then_inc(vc_ready[r], 1)

                    def normed(r, j):
                        x = row(r)
                        nc.vector.tensor_tensor(h[r][:], x, x, ALU.mult)
                        dve.drain()
                        nc.vector.tensor_reduce(ss[r][:], h[r][:], AX.X, ALU.add)
                        dve.drain()
                        nc.vector.tensor_scalar(ss[r][:], ss[r][:], 1.0 / D, 1e-6, ALU.mult, ALU.add).then_inc(ss_ready[r], 1)

                    def scaled_h(r, j):
                        dve.wait_ge(r_ready[r], it * 3 + (j + 1))
                        nc.vector.tensor_tensor(h[r][:], row(r), rs[r][:].unsqueeze(2).broadcast_to([P, TB, D]), ALU.mult).then_inc(h_ready[r], 1)

                    def copy_v(r):
                        dve.wait_ge(v_made[r], it + 1)
                        for t in range(TB):
                            last = nc.vector.tensor_tensor(slots(V[r])[:, t].rearrange("p (j q) d -> p j q d", j=4),
                                                           G[0][:, P * t:P * t + P].rearrange("p (q j d) -> p j q d", q=4, j=4),
                                                           bias_v[:].rearrange("p (q j d) -> p j q d", q=4, j=4), ALU.add)
                        last.then_inc(v_ready[r], 1)

                    def rope(r):
                        wide = lambda a: a.unsqueeze(1).broadcast_to([P, 2, S])
                        dve.wait_ge(qk_turned[r], it + 1)
                        nc.vector.tensor_tensor(turned_sin[:], G[1][:].rearrange("p (c s) -> p c s", c=2), wide(c.sin[:]), ALU.mult)
                        nc.vector.tensor_tensor(qk[:], qk[:], wide(c.cos[:]), ALU.mult)
                        dve.drain()
                        nc.vector.tensor_tensor(kr[r][:], qk[:, 1, :], turned_sin[:, 1, :], ALU.add)
                        nc.vector.tensor_tensor(qr[r][:], qk[:, 0, :], turned_sin[:, 0, :], ALU.add)
                        dve.drain().then_inc(roped[r], 1)

                    def normalise(r, a):
                        dve.wait_ge(O_turned[r], it * 2 + (a + 1))
                        wide = G[0][:].rearrange("p (t n w) -> p t n w", t=TB, w=ROWS)
                        nc.vector.reciprocal(rec[:], wide[:, :, :, HD])
                        dve.drain()
                        for t in range(TB):
                            last = nc.vector.tensor_tensor(o[r][:, t].rearrange("p (q j d) -> p j q d", q=4, j=4),
                                                           wide[:, t, :, 0:HD].rearrange("p (j q) d -> p j q d", j=4),
                                                           rec[:, t].rearrange("p (j q) -> p j q", j=4).unsqueeze(3).broadcast_to([P, 4, 4, HD]), ALU.mult)
                        last.then_inc(o_ready[r], 1)

                    def add_out(r, a):
                        dve.wait_ge(projected[r], it * 2 + (a + 1))
                        y = G[1][:, 0:TB * D].rearrange("p (t d) -> p t d", t=TB)
                        if a == SELF:
                            nc.vector.tensor_tensor(proj[:], y, c.bias_o[:, bass.ds(l, 1), :].broadcast_to([P, TB, D]), ALU.add)
                            dve.drain()
                            y = proj[:]
                        nc.vector.tensor_tensor(row(r), row(r), y, ALU.add)
                        dve.drain()
                        normed(r, 1 + a)

                    def activate(r, i):
                        dve.wait_ge(tanhed[r], it * 2 + (i + 1))
                        g = tg[:].rearrange("p f s -> p (f s)")
                        nc.vector.scalar_tensor_tensor(g, g, 1.0, G[0][:], ALU.add, ALU.mult)
                        dve.drain()
                        dve.wait_ge(upped[r], it * 2 + (i + 1))
                        nc.vector.scalar_tensor_tensor(aT[:, 2 * i:2 * i + 2, :].rearrange("p f s -> p (f s)"), g, 0.5, G[1][:],
                                                       ALU.mult, ALU.mult).then_inc(act_ready[r], 1)

                    def add_down(r):
                        dve.wait_ge(downed[r], it + 1)
                        nc.vector.tensor_tensor(row(r), row(r), G[1][:, 0:TB * D].rearrange("p (t d) -> p t d", t=TB), ALU.add)
                        dve.drain().then_inc(row_done[r], 1)

                    def first(r, step):
                        if step == 0:
                            copy_vc(r)
                            scaled_h(r, 0)
                        elif step == 2:
                            copy_v(r)
                        elif step == 3:
                            rope(r)

                    def middle(r, step):
                        if step == 0:
                            normalise(r, SELF)
                        elif step == 2:
                            add_out(r, SELF)

                    def end(r, step):
                        if step == 0:
                            normalise(r, CROSS)
                        elif step == 2:
                            add_out(r, CROSS)
                        elif step in (4, 5):
                            activate(r, step - 4)
                        elif step == 6:
                            add_down(r)

                    def steps_after(turn, n):
                        if turn == 0 and n in FIRST_AT:
                            first(1, FIRST_AT.index(n))
                        if turn in (1, 2):
                            if n in MIDDLE_AT:
                                middle(turn - 1, MIDDLE_AT.index(n))
                            if n == MIDDLE_AT[2] + 1:
                                scaled_h(turn - 1, 1)
                        if turn == 3:
                            if n in END_AT:
                                end(0, END_AT.index(n))
                            if n == END_AT[2] + 1:
                                scaled_h(0, 2)

                    def find_max(turn, n):
                        kind = TURNS[turn][1]
                        dve.wait_ge(scored, it * (4 * NH) + (turn * NH + n + 1))
                        if kind == CROSS:
                            last = nc.vector.tensor_reduce(neg_max[:, n % 4, :], A[n % 2][:].rearrange("p (t s) -> p t s", t=TB), AX.X, ALU.max, negate=True)
                        else:
                            for t, keys_n, col in TILES[kind]:
                                last = nc.vector.tensor_reduce(neg_max[:, n % 4, t:t + 1], A[n % 2][:, col:col + keys_n], AX.X, ALU.max, negate=True)
                        last.then_inc(maxed, 1)

                    nc.vector.tensor_copy(bias_v[:], c.bias_v[:, bass.ds(l, 1), :].rearrange("p a d -> p (a d)"))
                    for r in range(2):
                        normed(r, 0)
                    for step in range(4):
                        first(0, step)
                    find_max(0, 0)
                    for turn in range(4):
                        width = WIDTH[TURNS[turn][1]]
                        for n in range(NH):
                            if n + 1 < NH:
                                find_max(turn, n + 1)
                            elif turn < 3:
                                find_max(turn + 1, 0)
                            dve.wait_ge(turned, it * (4 * NH) + (turn * NH + n + 1))
                            nc.vector.tensor_copy(probT[:, n % 2, 0:width], T[n % 2][:, 0:width]).then_inc(turn_copied, 1)
                            if n >= 1:
                                steps_after(turn, n - 1)
                    end(1, 0)
                    end(1, 2)
                    scaled_h(1, 2)
                    for step in range(3, 7):
                        end(1, step)


def decoder_end(nc, k, c, XX):
    with ExitStack() as stack:
        m = Memory(nc, stack)
        SQ, ss, r = m.sb("e_SQ", [P, NT, D]), m.sb("e_ss", [P, NT]), m.sb("e_r", [P, NT])
        ss_ready, r_ready = m.sem("e_ss_ready"), m.sem("e_r_ready")
        block = stack.enter_context(nc.Block())

        @block.vector
        def _(dve):
            nc.vector.tensor_tensor(SQ[:], XX[:], XX[:], ALU.mult)
            dve.drain()
            nc.vector.tensor_reduce(ss[:], SQ[:], AX.X, ALU.add)
            dve.drain()
            nc.vector.tensor_scalar(ss[:], ss[:], 1.0 / D, 1e-6, ALU.mult, ALU.add).then_inc(ss_ready, 1)
            dve.wait_ge(r_ready, 1)
            nc.vector.tensor_tensor(XX[:], XX[:], r[:].unsqueeze(2).broadcast_to([P, NT, D]), ALU.mult)
            dve.drain()
            nc.vector.tensor_tensor(XX[:], XX[:], c.nf[:].unsqueeze(1).broadcast_to([P, NT, D]), ALU.mult)
            dve.drain()
            nc.vector.scalar_tensor_tensor(k.X[:], XX[:], k.gate[:, 1:2], k.X[:], ALU.mult, ALU.add)

        @block.gpsimd
        def _(pool):
            pool.wait_ge(ss_ready, 1)
            nc.gpsimd.tensor_tensor(r[:], ss[:], k.minus_half[:, 0:NT], ALU.pow).then_inc(r_ready, 1)


def moe(nc, k, io):
    with ExitStack() as stack:
        m = Memory(nc, stack)
        hT = m.sb("f_hT", [P, NTOK])
        acc = m.sb("f_acc", [P, NT, D])
        weight = m.sb("f_weight", [P, NT, 8])
        ln = m.sb("f_ln", [P, 2])
        wr = m.sb("f_wr", [P, 7])
        with ExitStack() as inner:
            n = Memory(nc, inner)
            loaded = n.sem("f_loaded")
            block = inner.enter_context(nc.Block())

            @block.sync
            def _(sp):
                sp.dma_start(ln[:, 0:1], io["L1_ffn_ln_g"].rearrange("(d a) -> d a", a=1)).then_inc(loaded, 16)
                sp.dma_start(ln[:, 1:2], io["L1_ffn_ln_b"].rearrange("(d a) -> d a", a=1)).then_inc(loaded, 16)
                sp.dma_start(wr[:], io["L1_ffn_Wr"]).then_inc(loaded, 16)
                sp.wait_ge(loaded, 48)
        with ExitStack() as inner:
            n = Memory(nc, inner)
            Xn = n.sb("f_Xn", [P, NT, D])
            layer_norm(nc, k, k.X, Xn, tag="f_")
            layer_norm(nc, k, Xn, Xn, hT, scale=ln[:, 0:1], shift=ln[:, 1:2], tag="fh_")
        moe_router(nc, k, hT, wr, weight)
        moe_experts(nc, k, io, hT, weight, acc)
        with ExitStack() as inner:
            block = inner.enter_context(nc.Block())

            @block.vector
            def _(dve):
                nc.vector.scalar_tensor_tensor(k.X[:], acc[:], k.gate[:, 3:4], k.X[:], ALU.mult, ALU.add)


def moe_router(nc, k, hT, wr, weight):
    E = 7
    with ExitStack() as stack:
        m = Memory(nc, stack)
        logit, scratch = m.sb("r_logit", [P, NT, E]), m.sb("r_scratch", [P, NT, E])
        one = m.sb("r_one", [P, 2, NT, E])
        oneb = m.sb("r_oneb", [P, 2, NT, E], BF16)
        m1, m2, first, e = (m.sb("r_" + n, [P, NT]) for n in ("m1", "m2", "first", "e"))
        gates = m.sb("r_gates", [P, 2, NT])
        before, beforeb, allb = m.sb("r_before", [P, P]), m.sb("r_beforeb", [P, P], BF16), m.sb("r_allb", [P, P], BF16)
        total, through = m.sb("r_total", [P, 2 * NT, E]), m.sb("r_through", [P, 2 * NT, E])
        lb, rb, tb = m.bank("r_logit_bank"), m.bank("r_rank_bank"), m.bank("r_total_bank")
        made, logits, diff_ready, exp_ready, one_ready, ranked = (m.sem("r_" + n) for n in ("made", "logits", "diff_ready", "exp_ready", "one_ready", "ranked"))
        block = stack.enter_context(nc.Block())

        @block.gpsimd
        def _(pool):
            nc.gpsimd.memset(before[:], 1.0)
            nc.gpsimd.memset(allb[:], 1.0)
            pool.drain()
            nc.gpsimd.affine_select(out=before[:], in_=before[:], compare_op=ALU.is_gt, fill=0.0,
                                    base=0, pattern=[[1, P]], channel_multiplier=-1)
            pool.drain()
            nc.gpsimd.tensor_copy(beforeb[:], before[:]).then_inc(made, 1)

        @block.tensor
        def _(pe):
            for t in range(NT):
                last = nc.tensor.matmul(lb[:, E * t:E * t + E], hT[:, P * t:P * t + P], wr[:], start=True, stop=True)
            last.then_inc(logits, 1)
            pe.wait_ge(made, 1)
            pe.wait_ge(one_ready, 1)
            flat = oneb[:].rearrange("p s t e -> p (s t e)")
            nc.tensor.matmul(rb[:, 0:2 * NT * E], beforeb[:], flat, start=True, stop=True)
            nc.tensor.matmul(tb[:, 0:2 * NT * E], allb[:], flat, start=True, stop=True).then_inc(ranked, 1)

        @block.scalar
        def _(act):
            act.wait_ge(diff_ready, 1)
            nc.scalar.activation(e[:], e[:], ACT.Exp).then_inc(exp_ready, 1)

        @block.vector
        def _(dve):
            dve.wait_ge(logits, 1)
            nc.vector.tensor_copy(logit[:].rearrange("p t e -> p (t e)"), lb[:, 0:NT * E])
            dve.drain()
            top_two(nc, dve, logit[:], one[:, 0], one[:, 1], m1[:], m2[:], scratch[:], first[:], k.rev, NT, E)
            nc.vector.tensor_copy(oneb[:], one[:]).then_inc(one_ready, 1)
            nc.vector.tensor_tensor(e[:], m2[:], m1[:], ALU.subtract).then_inc(diff_ready, 1)
            dve.wait_ge(exp_ready, 1)
            nc.vector.tensor_scalar(m1[:], e[:], 1.0, None, ALU.add)
            dve.drain()
            nc.vector.reciprocal(gates[:, 0, :], m1[:])
            dve.drain()
            nc.vector.tensor_tensor(gates[:, 1, :], e[:], gates[:, 0, :], ALU.mult)
            dve.wait_ge(ranked, 1)
            nc.vector.tensor_copy(total[:].rearrange("p t e -> p (t e)"), tb[:, 0:2 * NT * E])
            dve.drain()
            for x in range(E):
                nc.vector.tensor_tensor_scan(through[:, :, x], k.ones[:, 0:2 * NT], total[:, :, x], 0.0, ALU.mult, ALU.add)
            dve.drain()
            nc.vector.tensor_tensor(through[:], through[:], total[:], ALU.subtract)
            dve.drain()
            nc.vector.tensor_tensor(through[:].rearrange("p t e -> p (t e)"), through[:].rearrange("p t e -> p (t e)"),
                                    rb[:, 0:2 * NT * E], ALU.add)
            dve.drain()
            ones = one[:].rearrange("p s t e -> p (s t) e")
            nc.vector.scalar_tensor_tensor(ones, through[:], float(CAPACITY), ones, ALU.is_lt, ALU.mult)
            dve.drain()
            nc.vector.tensor_tensor(ones, ones, gates[:].rearrange("p s t -> p (s t)").unsqueeze(2).broadcast_to([P, 2 * NT, E]), ALU.mult)
            nc.vector.memset(weight[:], 1.0)
            dve.drain()
            nc.vector.tensor_tensor(weight[:, :, 0:E], one[:, 0], one[:, 1], ALU.add)


def moe_experts(nc, k, io, hT, weight, acc):
    E, F, N = 8, 4, 512
    CH = NTOK // N
    STEPS = 2 * CH
    with ExitStack() as stack:
        m = Memory(nc, stack)
        W1, W3, W2 = (m.sb("x_" + n, [P, 2, F, P]) for n in ("W1", "W3", "W2"))
        tg, aT, scaled_y = m.sb("x_tg", [P, 2, N]), m.sb("x_aT", [P, 2, F, N]), m.sb("x_scaled_y", [P, 2, 4, D])
        A, U, Y = ([m.bank(f"x_{n}{i}") for i in range(2)] for n in "AUY")
        w_in = [m.sem("x_w_in0"), m.sem("x_w_in1")]
        made, tanhed, acted, y_made, scaled, added = (m.sem("x_" + n) for n in ("made", "tanhed", "acted", "y_made", "scaled", "added"))
        block = stack.enter_context(nc.Block())

        @block.sync
        def _(sp):
            with sp.Fori(0, E // 2) as e2:
                for s in range(2):
                    e = e2 * 2 + s
                    sp.wait_ge(added, e * CH + CH)
                    sp.dma_start(W1[:, s], io["experts_W1"][bass.ds(e, 1)].rearrange("a d (f p) -> d (a f) p", p=P)).then_inc(w_in[s], 16)
                    sp.dma_start(W3[:, s], io["experts_W3"][bass.ds(e, 1)].rearrange("a d (f p) -> d (a f) p", p=P)).then_inc(w_in[s], 16)
                    sp.dma_start(W2[:, s], io["experts_W2"][bass.ds(e, 1)].rearrange("a (f p) d -> p (a f) d", p=P)).then_inc(w_in[s], 16)

        @block.tensor
        def _(pe):
            with pe.Fori(0, E // 2) as e2:
                def up(i):
                    s, c = i // CH, i % CH
                    if c == 0:
                        pe.wait_ge(w_in[s], e2 * 48 + 48)
                    for f in range(F):
                        pe.wait_ge(acted, e2 * (STEPS * F) + (i * F + f + 1))
                        nc.tensor.matmul(A[f % 2][:], W1[:, s, f, :], hT[:, N * c:N * c + N], start=True, stop=True)
                        nc.tensor.matmul(U[f % 2][:], W3[:, s, f, :], hT[:, N * c:N * c + N], start=True, stop=True).then_inc(made, 1)

                def down(i):
                    s = i // CH
                    pe.wait_ge(acted, e2 * (STEPS * F) + (i * F + F + 2))
                    pe.wait_ge(scaled, e2 * STEPS + (i + 1))
                    for t in range(4):
                        for f in range(F):
                            last = nc.tensor.matmul(Y[i % 2][:, P * t:P * t + P], aT[:, i % 2, f, P * t:P * t + P], W2[:, s, f, :],
                                                    start=f == 0, stop=f == F - 1)
                    last.then_inc(y_made, 1)

                up(0)
                for i in range(STEPS):
                    if i + 1 < STEPS:
                        up(i + 1)
                    down(i)

        @block.scalar
        def _(act):
            with act.Fori(0, E // 2) as e2:
                for n in range(STEPS * F):
                    act.wait_ge(made, e2 * (STEPS * F) + (n + 1))
                    nc.scalar.activation(tg[:, n % 2, :], A[n % 2][:], ACT.Tanh, scale=0.5).then_inc(tanhed, 1)

        @block.vector
        def _(dve):
            dve.sem_inc(acted, 2)
            dve.sem_inc(scaled, 2)
            with dve.Fori(0, E // 2) as e2:
                def hidden(i):
                    for f in range(F):
                        n = i * F + f
                        dve.wait_ge(tanhed, e2 * (STEPS * F) + (n + 1))
                        nc.vector.scalar_tensor_tensor(tg[:, n % 2, :], tg[:, n % 2, :], 1.0, A[n % 2][:], ALU.add, ALU.mult)
                        dve.drain()
                        nc.vector.scalar_tensor_tensor(aT[:, i % 2, f, :], tg[:, n % 2, :], 0.5, U[n % 2][:],
                                                       ALU.mult, ALU.mult).then_inc(acted, 1)

                def weigh(i):
                    s, c = i // CH, i % CH
                    dve.wait_ge(y_made, e2 * STEPS + (i + 1))
                    dve.wait_ge(added, e2 * STEPS + (i + 2 * CH - 1))
                    nc.vector.tensor_tensor(scaled_y[:, i % 2], Y[i % 2][:].rearrange("p (t d) -> p t d", t=4),
                                            weight[:, 4 * c:4 * c + 4, bass.ds(e2 * 2 + s, 1)].broadcast_to([P, 4, D]), ALU.mult).then_inc(scaled, 1)

                hidden(0)
                for i in range(STEPS):
                    if i + 1 < STEPS:
                        hidden(i + 1)
                    weigh(i)

        @block.gpsimd
        def _(pool):
            nc.gpsimd.memset(acc[:], 0.0)
            pool.drain().then_inc(added, 2 * CH)
            with pool.Fori(0, E // 2) as e2:
                for i in range(STEPS):
                    c = i % CH
                    pool.wait_ge(scaled, e2 * STEPS + (i + 3))
                    nc.gpsimd.tensor_tensor(acc[:, 4 * c:4 * c + 4, :], acc[:, 4 * c:4 * c + 4, :], scaled_y[:, i % 2], ALU.add).then_inc(added, 1)


class Kept:

    EXPERTS_IN = 32

    def __init__(self, nc, stack):
        m = Memory(nc, stack)
        self.X = m.sb("X", [P, NT, D])
        self.ctxT = m.sb("ctxT", [P, NTOK])
        self.ctx_ones = m.sb("ctx_ones", [P, NT, 8, 17])
        self.ident, self.identb = m.sb("ident", [P, P]), m.sb("identb", [P, P], BF16)
        self.causal, self.causalb = m.sb("causal", [P, 2, P]), m.sb("causalb", [P, 2, P], BF16)
        self.ones, self.minus_half = m.sb("ones", [P, S]), m.sb("minus_half", [P, S])
        self.gate = m.sb("gate", [P, 4])
        self.rev = m.sb("rev", [P, 8])


def build(nc, io, out):
    with ExitStack() as stack:
        k = Kept(nc, stack)
        load_inputs(nc, k, io)
        with ExitStack() as inner:
            m = Memory(nc, inner)
            k.v_w, k.o_w, k.experts_in = m.sb("v_w", [P, 64, P]), m.sb("o_w", [P, 64, P]), m.sem("experts_in")
            mlstm(nc, k, io)
            switch_head(nc, k, io)
        decoder(nc, k, io)
        moe(nc, k, io)
        store(nc, k, out)


def store(nc, k, out):
    with ExitStack() as stack:
        stored = Memory(nc, stack).sem("out_stored")
        block = stack.enter_context(nc.Block())

        @block.sync
        def _(sp):
            sp.dma_start(out.rearrange("b (t p) d -> p (b t) d", p=P), k.X[:]).then_inc(stored, 16)
            sp.wait_ge(stored, 16)


def rope_tables():
    import numpy as np
    hd, heads = 8, 16
    inv = (1.0 / np.float32(10000.0) ** (np.arange(0, hd, 2, dtype=np.float32) / np.float32(hd))).astype(np.float32)
    f = np.arange(S, dtype=np.float32)[:, None] * inv[None, :]
    emb = np.concatenate([f, f], axis=-1)
    turn = np.zeros((P, P), np.float32)
    for r in range(P):
        turn[r + 4 if r % hd < 4 else r - 4, r] = -1.0 if r % hd < 4 else 1.0
    own = (np.arange(P)[:, None] // hd % 4 == np.arange(4)[None, :]).astype(np.float32)
    return dict(rope_cos=np.tile(np.cos(emb).T, (heads, 1)).astype(np.float32),
                rope_sin=np.tile(np.sin(emb).T, (heads, 1)).astype(np.float32), rope_turn=turn, head_of_quadrant=own)


_OUTS = [((8, 256, 128), "float32")]


def kernel(**inputs):
    import numpy as _np
    import concourse.bacc as _bacc
    from concourse import mybir as _mybir
    from concourse.bass_utils import run_bass_kernel_spmd as _run

    nc = _bacc.Bacc("TRN2", target_bir_lowering=False, num_devices=1)
    laid = {name: _np.ascontiguousarray(a) for name, a in inputs.items()}
    laid.update(rope_tables())
    for w in ("W1", "W3", "W2"):
        laid["experts_" + w] = _np.concatenate([laid.pop("L1_ffn_" + w), laid.pop("L1_ffn_" + w + "s")[None]])
    arrays, io = {}, {}
    for name, a in laid.items():
        arrays[f"in_{name}"] = a
        io[name] = nc.dram_tensor(f"in_{name}", a.shape, _mybir.dt.from_np(a.dtype), kind="ExternalInput").ap()
    shape, dtype = _OUTS[0]
    out = nc.dram_tensor("out_0", shape, _mybir.dt.from_np(_np.dtype(dtype)), kind="ExternalOutput").ap()
    build(nc, io, out)
    r = _run(nc, [arrays], core_ids=[0])
    return r.results[0]["out_0"]
```

```python
import concourse.bass as bass
from concourse import mybir
from contextlib import ExitStack

FP32 = mybir.dt.float32
BF16 = mybir.dt.bfloat16
R32 = mybir.dt.float32r
HIGH, LOW = 0, 1
HALVES = ((HIGH, HIGH), (HIGH, LOW), (LOW, HIGH), (LOW, LOW))
ALU = mybir.AluOpType
ACT = mybir.ActivationFunctionType
AX = mybir.AxisListType

P = 128
B, S, D = 8, 256, 128
TB = S // P
NT = B * TB
NTOK = B * S
NEG = -1e30
CAPACITY = 366
LAYERS = 4


class Memory:

    def __init__(self, nc, stack):
        self.nc, self.stack = nc, stack

    def sb(self, name, shape, dtype=FP32):
        return self.stack.enter_context(self.nc.sbuf_tensor(name, shape, dtype))

    def bank(self, name, dtype=FP32, cols=512):
        return self.stack.enter_context(self.nc.psum_tensor(name, [P, cols], dtype))

    def sem(self, name):
        return self.stack.enter_context(self.nc.semaphore(name))


def load_inputs(nc, k, io):
    with ExitStack() as stack:
        m = Memory(nc, stack)
        C = m.sb("ctx_natural", [P, NT, D])
        graw = m.sb("graw", [P, 4])
        banks = [m.bank(f"ctxT_bank{i}") for i in range(4)]
        x_in, ctx_in, g_in = m.sem("x_in"), m.sem("ctx_in"), m.sem("g_in")
        const_made, transposed = m.sem("const_made"), m.sem("ctx_transposed")
        block = stack.enter_context(nc.Block())

        @block.sync
        def _(sp):
            sp.dma_start(C[:], io["ctx_1024"].rearrange("b (t p) d -> p (b t) d", p=P)).then_inc(ctx_in, 16)
            sp.dma_start(k.X[:], io["x"].rearrange("b (t p) d -> p (b t) d", p=P)).then_inc(x_in, 16)
            sp.dma_start(graw[:, 0:2], io["g_xattn"].rearrange("(a n) -> a n", a=1).broadcast_to([P, 2])).then_inc(g_in, 16)
            sp.dma_start(graw[:, 2:4], io["g_ffn"].rearrange("(a n) -> a n", a=1).broadcast_to([P, 2])).then_inc(g_in, 16)
            sp.wait_ge(x_in, 16)

        @block.gpsimd
        def _(pool):
            nc.gpsimd.memset(k.ident[:], 0.0)
            nc.gpsimd.memset(k.ones[:], 1.0)
            nc.gpsimd.memset(k.minus_half[:], -0.5)
            for e in range(8):
                nc.gpsimd.memset(k.rev[:, e:e + 1], 8.0 - e)
            nc.gpsimd.memset(k.causal[:], 0.0)
            pool.drain()
            nc.gpsimd.affine_select(out=k.ident[:], in_=k.ident[:], compare_op=ALU.not_equal, fill=1.0,
                                    base=0, pattern=[[-1, P]], channel_multiplier=1)
            nc.gpsimd.affine_select(out=k.causal[:, 0, :], in_=k.causal[:, 0, :], compare_op=ALU.is_ge, fill=NEG,
                                    base=0, pattern=[[-1, P]], channel_multiplier=1)
            nc.gpsimd.affine_select(out=k.causal[:, 1, :], in_=k.causal[:, 1, :], compare_op=ALU.is_ge, fill=NEG,
                                    base=0, pattern=[[1, P]], channel_multiplier=-1)
            pool.drain()
            nc.gpsimd.tensor_copy(k.identb[:], k.ident[:])
            nc.gpsimd.tensor_copy(k.causalb[:], k.causal[:]).then_inc(const_made, 1)

        @block.tensor
        def _(pe):
            pe.wait_ge(const_made, 1)
            pe.wait_ge(ctx_in, 16)
            for t in range(NT):
                nc.tensor.transpose(banks[t // 4][:, t % 4 * P:t % 4 * P + P], C[:, t, :], k.ident[:]).then_inc(transposed, 1)

        @block.scalar
        def _(act):
            act.wait_ge(g_in, 32)
            nc.scalar.activation(k.gate[:], graw[:], ACT.Tanh)
            for c in range(4):
                act.wait_ge(transposed, 4 * c + 4)
                nc.scalar.activation(k.ctxT[:, 512 * c:512 * c + 512], banks[c][:], ACT.Copy)

        @block.vector
        def _(dve):
            nc.vector.memset(k.ctx_ones[:, :, :, 16:17], 1.0)
            dve.wait_ge(ctx_in, 16)
            nc.vector.tensor_copy(k.ctx_ones[:, :, :, 0:16], C[:].rearrange("p t (h d) -> p t h d", h=8))


def layer_norm(nc, k, src, dst, dstT=None, scale=None, shift=None, tag=""):
    with ExitStack() as stack:
        m = Memory(nc, stack)
        stats, mv, rstd = m.sb(tag + "stats", [P, NT, 6]), m.sb(tag + "mv", [P, NT, 2]), m.sb(tag + "rstd", [P, NT])
        banks = [m.bank(f"{tag}nT_bank{i}") for i in range(4)]
        var_ready, rstd_ready, normed, transposed = k.norm_sems
        use = k.norms
        k.norms += 1
        turned_before = k.norms_turned * NT
        k.norms_turned += dstT is not None
        block = stack.enter_context(nc.Block())

        @block.vector
        def _(dve):
            for t in range(NT):
                nc.vector.bn_stats(stats[:, t, :], src[:, t, :])
            dve.drain()
            for t in range(NT):
                nc.vector.bn_aggr(mv[:, t, :], stats[:, t, :])
            dve.drain()
            nc.vector.tensor_scalar(mv[:, :, 1], mv[:, :, 1], 1e-5, None, ALU.add).then_inc(var_ready, 1)
            dve.wait_ge(rstd_ready, use + 1)
            for t in range(NT):
                nc.vector.tensor_scalar(dst[:, t, :], src[:, t, :], mv[:, t, 0:1], rstd[:, t:t + 1],
                                        ALU.subtract, ALU.mult).then_inc(normed, 1)

        @block.gpsimd
        def _(pool):
            pool.wait_ge(var_ready, use + 1)
            nc.gpsimd.tensor_tensor(rstd[:], mv[:, :, 1], k.minus_half[:, 0:NT], ALU.pow).then_inc(rstd_ready, 1)

        if dstT is not None:
            @block.tensor
            def _(pe):
                for t in range(NT):
                    pe.wait_ge(normed, use * NT + t + 1)
                    nc.tensor.transpose(banks[t // 4][:, t % 4 * P:t % 4 * P + P], dst[:, t, :], k.ident[:]).then_inc(transposed, 1)

            @block.scalar
            def _(act):
                for c in range(4):
                    act.wait_ge(transposed, turned_before + 4 * c + 4)
                    if scale is None:
                        nc.scalar.activation(dstT[:, 512 * c:512 * c + 512], banks[c][:], ACT.Copy)
                    else:
                        nc.scalar.activation(dstT[:, 512 * c:512 * c + 512], banks[c][:], ACT.Identity,
                                             scale=scale, bias=shift)


def mlstm(nc, k, io):
    NH, HD = 8, 16
    with ExitStack() as stack:
        m = Memory(nc, stack)
        XnT = m.sb("m_XnT", [P, NTOK])
        with ExitStack() as inner:
            layer_norm(nc, k, k.X, Memory(nc, inner).sb("m_Xn", [P, NT, D]), XnT, tag="m_")
        aT, enT = m.sb("aT", [P, NT, NH]), m.sb("enT", [P, NT, NH])
        neg_max2, sel2 = m.sb("neg_max2", [NH, 2, NTOK], R32), m.sb("sel2", [NH, NH, P], R32)
        with ExitStack() as inner:
            n = Memory(nc, inner)
            neg_max, sel = n.sb("neg_max", [NH, NTOK]), n.sb("sel", [NH, NH, P])
            mlstm_gates(nc, k, io, XnT, neg_max, aT, enT, sel)
            split_halves(nc, [(neg_max, neg_max2)], [(sel, sel2)], "m")
        HO = m.sb("HO", [P, NT, NH, HD + 1])
        mlstm_heads(nc, k, io, XnT, neg_max2, aT, sel2, HO)
        mlstm_finish(nc, k, enT, HO)


def mlstm_gates(nc, k, io, XnT, neg_max, aT, enT, sel):
    NH = 8
    with ExitStack() as stack:
        m = Memory(nc, stack)
        wi, wf = m.sb("wi", [P, 3, NH]), m.sb("wf", [P, 3, NH])
        bi, bf = m.sb("bi", [NH, 1]), m.sb("bf", [NH, 1])
        IG, F, T, CS, A, M = (m.sb("g_" + n, [NH, NTOK]) for n in ("IG", "F", "T", "CS", "A", "M"))
        banks = [m.bank(f"gate_bank{i}") for i in range(8)]
        w_in, projected, pre_ready, abs_ready, log_ready = (m.sem("mg_" + n) for n in ("w_in", "projected", "pre_ready", "abs_ready", "log_ready"))
        a_ready, sum_ready, en_ready, transposed = (m.sem("mg_" + n) for n in ("a_ready", "sum_ready", "en_ready", "transposed"))
        block = stack.enter_context(nc.Block())

        @block.sync
        def _(sp):
            sp.dma_start(wi[:], io["L0_xattn_igate_kernel"].rearrange("(c p) n -> p c n", p=P)).then_inc(w_in, 16)
            sp.dma_start(wf[:], io["L0_xattn_fgate_kernel"].rearrange("(c p) n -> p c n", p=P)).then_inc(w_in, 16)
            sp.dma_start(bi[:], io["L0_xattn_igate_bias"].rearrange("(n a) -> n a", a=1)).then_inc(w_in, 16)
            sp.dma_start(bf[:], io["L0_xattn_fgate_bias"].rearrange("(n a) -> n a", a=1)).then_inc(w_in, 16)

        @block.gpsimd
        def _(pool):
            nc.gpsimd.memset(sel[:], 0.0)
            pool.drain()
            nc.gpsimd.affine_select(out=sel[:], in_=sel[:], compare_op=ALU.not_equal, fill=1.0,
                                    base=0, pattern=[[-1, NH], [0, P]], channel_multiplier=1)

        @block.tensor
        def _(pe):
            pe.wait_ge(w_in, 64)
            for c in range(4):
                for g, w in enumerate((wi, wf)):
                    for part, src in enumerate((XnT, k.ctxT, k.ctxT)):
                        last = nc.tensor.matmul(banks[4 * g + c][0:NH, :], w[:, part, :], src[:, 512 * c:512 * c + 512],
                                                start=part == 0, stop=part == 2)
                    last.then_inc(projected, 1)
            pe.wait_ge(a_ready, 1)
            pe.wait_ge(en_ready, 1)
            for t in range(NT):
                nc.tensor.transpose(banks[0][:, NH * t:NH * t + NH], A[:, P * t:P * t + P], k.ident[0:NH, 0:NH])
                last = nc.tensor.transpose(banks[1][:, NH * t:NH * t + NH], M[:, P * t:P * t + P], k.ident[0:NH, 0:NH])
            last.then_inc(transposed, 1)

        @block.scalar
        def _(act):
            for c in range(4):
                act.wait_ge(projected, 2 * c + 2)
                nc.scalar.activation(IG[:, 512 * c:512 * c + 512], banks[c][0:NH, :], ACT.Identity, bias=bi[:, 0:1])
                nc.scalar.activation(F[:, 512 * c:512 * c + 512], banks[4 + c][0:NH, :], ACT.Identity, bias=bf[:, 0:1]).then_inc(pre_ready, 1)
            act.wait_ge(abs_ready, 1)
            nc.scalar.activation(T[:], T[:], ACT.Exp, scale=-1.0)
            act.drain()
            nc.scalar.activation(T[:], T[:], ACT.Ln, bias=k.ones[0:NH, 0:1]).then_inc(log_ready, 1)
            act.wait_ge(sum_ready, 1)
            nc.scalar.activation(M[:], CS[:], ACT.Exp, scale=-1.0).then_inc(en_ready, 1)

        @block.vector
        def _(dve):
            dve.wait_ge(pre_ready, 4)
            nc.vector.scalar_tensor_tensor(T[:], F[:], -1.0, F[:], ALU.mult, ALU.max).then_inc(abs_ready, 1)
            dve.wait_ge(log_ready, 1)
            nc.vector.scalar_tensor_tensor(F[:], F[:], 0.0, T[:], ALU.min, ALU.subtract)
            dve.drain()
            for b in range(B):
                row = slice(S * b, S * b + S)
                nc.vector.tensor_tensor_scan(CS[:, row], k.ones[0:NH, 0:S], F[:, row], 0.0, ALU.mult, ALU.add)
            dve.drain()
            nc.vector.tensor_tensor(A[:], IG[:], CS[:], ALU.subtract).then_inc(a_ready, 1)
            dve.drain()
            for b in range(B):
                row = slice(S * b, S * b + S)
                nc.vector.tensor_tensor_scan(M[:, row], A[:, row], A[:, row], -3e38, ALU.max, ALU.max)
            dve.drain()
            nc.vector.tensor_scalar(neg_max[:], M[:], -1.0, None, ALU.mult)
            nc.vector.tensor_tensor(CS[:], CS[:], M[:], ALU.add).then_inc(sum_ready, 1)
            dve.wait_ge(transposed, 1)
            nc.vector.tensor_copy(aT[:].rearrange("p t h -> p (t h)"), banks[0][:, 0:NT * NH])
            nc.vector.tensor_copy(enT[:].rearrange("p t h -> p (t h)"), banks[1][:, 0:NT * NH])


def split_halves(nc, pairs, exact, tag):
    with ExitStack() as stack:
        high_ready = Memory(nc, stack).sem(tag + "_high_ready")
        block = stack.enter_context(nc.Block())

        @block.scalar
        def _(act):
            for src, dst in pairs:
                nc.scalar.activation(dst[:, HIGH, :], src[:], ACT.Copy).then_inc(high_ready, 1)
            for src, dst in exact:
                nc.scalar.activation(dst[:], src[:], ACT.Copy)

        @block.vector
        def _(dve):
            for i, (src, dst) in enumerate(pairs):
                dve.wait_ge(high_ready, i + 1)
                nc.vector.tensor_tensor(dst[:, LOW, :], src[:], dst[:, HIGH, :].bitcast(FP32), ALU.subtract)


def mlstm_heads(nc, k, io, XnT, neg_max2, aT, sel2, HO):
    NH, HD = 8, 16
    W = S + P
    with ExitStack() as stack:
        m = Memory(nc, stack)
        qk2 = m.sb("qk2", [P, 4, NTOK], R32)
        split_halves(nc, [(XnT, qk2[:, 0:2, :]), (k.ctxT, qk2[:, 2:4, :])], [], "qk")
        qk16 = m.sb("qk16", [HD, NH, 4, S], R32)
        q16, k16 = qk16[:, :, 0:2, :], qk16[:, :, 2:4, :]
        BUFFERS, PAIRS, HEADS = 3, B // 2, 2 * NH
        a_now = m.sb("a_now", [P, 2 * TB, NH])
        DT, CT = m.sb("DT", [P, BUFFERS, W]), m.sb("CT", [P, BUFFERS, W])
        sc = [m.bank(f"mh_sc{i}") for i in range(BUFFERS)]
        ex = [m.bank(f"mh_ex{i}") for i in range(BUFFERS)]
        ob = [m.bank(f"mh_out{i}") for i in range(2)]
        brought = [m.sem(f"mh_brought{h}") for h in range(NH)]
        scored, exponents, decayed, weighted, summed, stored = (
            m.sem("mh_" + n) for n in ("scored", "exponents", "decayed", "weighted", "summed", "stored"))
        block = stack.enter_context(nc.Block())

        @block.sync
        def _(sp):
            sp.dma_start(k.v_w[:], io["L0_ffn_v_w"].rearrange("e d p -> d e p")).then_inc(k.experts_in, 16)
            sp.dma_start(k.o_w[:], io["L0_ffn_o_w"].rearrange("e p d -> p e d")).then_inc(k.experts_in, 16)

        @block.gpsimd
        def _(pool):
            def bring(b, h):
                pool.dma_start(qk16[:, h, :, :], qk2[HD * h:HD * h + HD, :, bass.ds(b * S, S)]).then_inc(brought[h], 16)
            for h in range(NH):
                bring(0, h)
            with pool.Fori(1, B) as b:
                for h in range(NH):
                    pool.wait_ge(scored, b * NH + (h + 1 - NH))
                    bring(b, h)

        @block.tensor
        def _(pe):
            pe.sem_inc(stored, 2)
            with pe.Fori(0, PAIRS) as pair:
                def scores(g):
                    r, h = divmod(g, NH)
                    sc_bank, ex_bank = sc[g % BUFFERS], ex[g % BUFFERS]
                    pe.wait_ge(brought[h], pair * 32 + 16 * (r + 1))
                    for keys, first, at, n in ((0, 0, 0, S), (P, P, S, P)):
                        for i, (kh, qh) in enumerate(HALVES):
                            last = nc.tensor.matmul(sc_bank[:, at:at + n], k16[:, h, kh, keys:keys + P], q16[:, h, qh, first:first + n],
                                                    start=i == 0, stop=i == len(HALVES) - 1)
                    last.then_inc(scored, 1)
                    for first, at, n in ((0, 0, S), (P, S, P)):
                        for half in (HIGH, LOW):
                            nc.tensor.matmul(ex_bank[:, at:at + n], sel2[:, h, :], neg_max2[:, half, bass.ds(pair * (2 * S) + (r * S + first), n)],
                                             start=half == HIGH, stop=False)
                        last = nc.tensor.matmul(ex_bank[:, at:at + P], k.identb[:], k.causalb[:, 1, :], start=False, stop=True)
                    last.then_inc(exponents, 1)

                scores(0)
                scores(1)
                for g in range(HEADS):
                    r, h = divmod(g, NH)
                    if g + 2 < HEADS:
                        scores(g + 2)
                    if h == 0:
                        pe.wait_ge(stored, pair * 2 + (r + 1))
                    pe.wait_ge(weighted, pair * HEADS + (g + 1))
                    c = CT[:, g % BUFFERS, :]
                    v = lambda jt: k.ctx_ones[:, bass.ds(pair * (2 * TB) + (r * TB + jt), 1), h, :].rearrange("p a d -> p (a d)")
                    o = lambda t: ob[r][:, (t * NH + h) * (HD + 1):(t * NH + h + 1) * (HD + 1)]
                    nc.tensor.matmul(o(0), c[:, 0:P], v(0), start=True, stop=True)
                    nc.tensor.matmul(o(1), c[:, P:S], v(0), start=True, stop=False)
                    nc.tensor.matmul(o(1), c[:, S:W], v(1), start=False, stop=True).then_inc(summed, 1)

        @block.scalar
        def _(act):
            with act.Fori(0, PAIRS) as pair:
                def store(r):
                    act.wait_ge(summed, pair * HEADS + NH * (r + 1))
                    nc.scalar.activation(HO[:, bass.ds(pair * (2 * TB) + r * TB, TB), :, :].rearrange("p t h d -> p (t h d)"),
                                         ob[r][:, 0:TB * NH * (HD + 1)], ACT.Copy).then_inc(stored, 1)

                nc.scalar.activation(a_now[:], aT[:, bass.ds(pair * (2 * TB), 2 * TB), :], ACT.Copy)
                act.drain()
                for g in range(HEADS):
                    r, h = divmod(g, NH)
                    act.wait_ge(exponents, pair * HEADS + (g + 1))
                    if g >= BUFFERS:
                        act.wait_ge(weighted, pair * HEADS + (g + 1 - BUFFERS))
                    bank, decay = ex[g % BUFFERS], DT[:, g % BUFFERS, :]
                    nc.scalar.activation(decay[:, 0:S], bank[:, 0:S], ACT.Exp, bias=a_now[:, TB * r, h:h + 1])
                    nc.scalar.activation(decay[:, S:W], bank[:, S:W], ACT.Exp, bias=a_now[:, TB * r + 1, h:h + 1]).then_inc(decayed, 1)
                    if g == NH + 2:
                        store(0)
                store(1)

        @block.vector
        def _(dve):
            with dve.Fori(0, PAIRS) as pair:
                for g in range(HEADS):
                    dve.wait_ge(decayed, pair * HEADS + (g + 1))
                    if g >= BUFFERS:
                        dve.wait_ge(summed, pair * HEADS + (g + 1 - BUFFERS))
                    nc.vector.scalar_tensor_tensor(CT[:, g % BUFFERS, :], sc[g % BUFFERS][:, 0:W], HD ** -0.5, DT[:, g % BUFFERS, :],
                                                   ALU.mult, ALU.mult).then_inc(weighted, 1)


def mlstm_finish(nc, k, enT, HO):
    NH, HD = 8, 16
    G = NT * NH
    with ExitStack() as stack:
        m = Memory(nc, stack)
        den, ms, rms = m.sb("den", [P, G]), m.sb("ms", [P, G]), m.sb("rms", [P, G])
        Hn, SQ = m.sb("Hn", [P, G, HD]), m.sb("SQ", [P, G, HD])
        ms_ready, rms_ready = m.sem("ms_ready"), m.sem("rms_ready")
        block = stack.enter_context(nc.Block())
        ho = HO[:].rearrange("p t h d -> p (t h) d")

        @block.vector
        def _(dve):
            nc.vector.scalar_tensor_tensor(den[:], ho[:, :, HD], -1.0, ho[:, :, HD], ALU.mult, ALU.max)
            dve.drain()
            nc.vector.tensor_tensor(den[:], den[:], enT[:].rearrange("p t h -> p (t h)"), ALU.max)
            dve.drain()
            nc.vector.tensor_scalar(den[:], den[:], 1e-6, None, ALU.add)
            dve.drain()
            nc.vector.reciprocal(den[:], den[:])
            dve.drain()
            nc.vector.tensor_tensor(Hn[:], ho[:, :, 0:HD], den[:].unsqueeze(2).broadcast_to([P, G, HD]), ALU.mult)
            dve.drain()
            nc.vector.tensor_tensor(SQ[:], Hn[:], Hn[:], ALU.mult)
            dve.drain()
            nc.vector.tensor_reduce(ms[:], SQ[:], AX.X, ALU.add)
            dve.drain()
            nc.vector.tensor_scalar(ms[:], ms[:], 1.0 / HD, 1e-6, ALU.mult, ALU.add).then_inc(ms_ready, 1)
            dve.wait_ge(rms_ready, 1)
            nc.vector.tensor_tensor(Hn[:], Hn[:], rms[:].unsqueeze(2).broadcast_to([P, G, HD]), ALU.mult)
            dve.drain()
            x = k.X[:].rearrange("p t d -> p (t d)")
            nc.vector.scalar_tensor_tensor(x, Hn[:].rearrange("p g d -> p (g d)"), k.gate[:, 0:1], x, ALU.mult, ALU.add)

        @block.gpsimd
        def _(pool):
            pool.wait_ge(ms_ready, 1)
            nc.gpsimd.tensor_tensor(rms[:], ms[:], k.minus_half[:, 0:G], ALU.pow).then_inc(rms_ready, 1)


def top_two(nc, dve, p, one1, one2, m1, m2, scratch, first, rev, groups, n):
    def wide(a):
        return a.unsqueeze(2).broadcast_to([P, groups, n])
    rank = rev[:, 0:n].unsqueeze(1).broadcast_to([P, groups, n])
    for values, peak, one in ((p, m1, one1), (scratch, m2, one2)):
        if one is one2:
            nc.vector.scalar_tensor_tensor(scratch, one1, NEG, p, ALU.mult, ALU.add)
            dve.drain()
        nc.vector.tensor_reduce(peak, values, AX.X, ALU.max)
        dve.drain()
        nc.vector.tensor_tensor(scratch, values, wide(peak), ALU.is_equal)
        dve.drain()
        nc.vector.tensor_tensor(scratch, scratch, rank, ALU.mult)
        dve.drain()
        nc.vector.tensor_reduce(first, scratch, AX.X, ALU.max)
        dve.drain()
        nc.vector.tensor_tensor(one, rank, wide(first), ALU.is_equal)
        dve.drain()


def switch_head(nc, k, io):
    NH, E = 8, 8
    with ExitStack() as stack:
        m = Memory(nc, stack)
        Xn, XnT = m.sb("s_Xn", [P, NT, D]), m.sb("s_XnT", [P, NTOK])
        layer_norm(nc, k, k.X, Xn, XnT, tag="s_")
        G = m.sb("router_gates", [P, NT, 2, NH, E])
        QK = m.sb("QK", [P, NH, P])
        with ExitStack() as inner:
            switch_gates(nc, k, io, Memory(nc, inner), XnT, G, QK)
        switch_attention(nc, k, io, XnT, G, QK, Xn)
        with ExitStack() as inner:
            block = inner.enter_context(nc.Block())

            @block.vector
            def _(dve):
                nc.vector.scalar_tensor_tensor(k.X[:], Xn[:], k.gate[:, 2:3], k.X[:], ALU.mult, ALU.add)


def switch_gates(nc, k, io, m, XnT, G, QK):
    NH, E = 8, 8
    groups = NT * 2 * NH
    sel, selT = m.sb("sel_w", [P, D]), m.sb("sel_wT", [P, P])
    qn, kn = m.sb("q_w", [P, NH, D]), m.sb("k_w", [P, NH, D])
    prob, one1, one2, scratch = (m.sb("sg_" + n, [P, groups, E]) for n in ("prob", "one1", "one2", "scratch"))
    m1, m2, first, scale = (m.sb("sg_" + n, [P, groups]) for n in ("m1", "m2", "first", "scale"))
    rs = m.sb("route_scale", [P, 1])
    banks = [m.bank(f"sg_bank{i}") for i in range(4)]
    tb = m.bank("sg_selT")
    qk_bank = [m.bank(f"sg_qk{i}") for i in range(2)]
    w_in, sel_t, sel_c, qk_made, logits, exped = (m.sem("sg_" + n) for n in ("w_in", "sel_t", "sel_c", "qk_made", "logits", "exped"))
    block = m.stack.enter_context(nc.Block())

    @block.sync
    def _(sp):
        sp.dma_start(sel[0:64, :], io["L0_ffn_sel_v_w"]).then_inc(w_in, 16)
        sp.dma_start(sel[64:128, :], io["L0_ffn_sel_o_w"]).then_inc(w_in, 16)
        sp.dma_start(rs[:], io["L0_ffn_route_scale"].rearrange("(a n) -> a n", a=1).broadcast_to([P, 1])).then_inc(w_in, 16)
        sp.dma_start(qn[:], io["L0_ffn_q_w"].rearrange("(h p) d -> p h d", p=P)).then_inc(w_in, 16)
        sp.dma_start(kn[:], io["L0_ffn_k_w"].rearrange("(h p) d -> p h d", p=P)).then_inc(w_in, 16)

    @block.tensor
    def _(pe):
        pe.wait_ge(w_in, 80)
        nc.tensor.transpose(tb[:, 0:P], sel[:], k.ident[:]).then_inc(sel_t, 1)
        pe.wait_ge(sel_c, 1)
        for t in range(NT):
            nc.tensor.matmul(banks[t // 4][:, t % 4 * P:t % 4 * P + P], XnT[:, P * t:P * t + P], selT[:],
                             start=True, stop=True).then_inc(logits, 1)
        for h in range(NH):
            nc.tensor.matmul(qk_bank[h // 4][:, h % 4 * P:h % 4 * P + P], qn[:, h, :], kn[:, h, :],
                             start=True, stop=True).then_inc(qk_made, 1)

    @block.scalar
    def _(act):
        act.wait_ge(sel_t, 1)
        nc.scalar.activation(selT[:], tb[:, 0:P], ACT.Copy).then_inc(sel_c, 1)
        flat = prob[:].rearrange("p g e -> p (g e)")
        for c in range(4):
            act.wait_ge(logits, 4 * c + 4)
            nc.scalar.activation(flat[:, 512 * c:512 * c + 512], banks[c][:], ACT.Exp, scale=-1.0).then_inc(exped, 1)
        for c in range(2):
            act.wait_ge(qk_made, 4 * c + 4)
            nc.scalar.activation(QK[:, 4 * c:4 * c + 4, :].rearrange("p h d -> p (h d)"), qk_bank[c][:], ACT.Copy)

    @block.vector
    def _(dve):
        dve.wait_ge(exped, 4)
        nc.vector.tensor_scalar(prob[:], prob[:], 1.0, None, ALU.add)
        dve.drain()
        nc.vector.reciprocal(prob[:], prob[:])
        dve.drain()
        top_two(nc, dve, prob[:], one1[:], one2[:], m1[:], m2[:], scratch[:], first[:], k.rev, groups, E)
        nc.vector.tensor_tensor(scale[:], m1[:], m2[:], ALU.add)
        dve.drain()
        nc.vector.tensor_scalar(scale[:], scale[:], 1e-9, None, ALU.max)
        dve.drain()
        nc.vector.reciprocal(scale[:], scale[:])
        nc.vector.tensor_tensor(one1[:], one1[:], one2[:], ALU.add)
        dve.drain()
        dve.wait_ge(w_in, 80)
        nc.vector.tensor_scalar(scale[:], scale[:], rs[:, 0:1], None, ALU.mult)
        nc.vector.tensor_tensor(prob[:], prob[:], one1[:], ALU.mult)
        dve.drain()
        nc.vector.tensor_tensor(G[:].rearrange("p t c h e -> p (t c h) e"), prob[:],
                                scale[:].unsqueeze(2).broadcast_to([P, groups, E]), ALU.mult)


def switch_attention(nc, k, io, XnT, G, QK, out):
    NH, E = 8, 8
    STEPS = 4 * NH
    with ExitStack() as stack:
        m = Memory(nc, stack)
        xb, zT, prob, probT, cT = m.sb("xb", [P, S]), m.sb("zT", [P, S]), m.sb("sa_prob", [P, TB, S]), m.sb("sa_probT", [P, TB, S]), m.sb("cT", [P, S])
        values, rec = m.sb("sa_values", [P, 2, TB, P]), m.sb("sa_rec", [P, TB])
        neg_max, total, wo = m.sb("sa_neg_max", [P, TB]), m.sb("sa_total", [P, TB]), m.sb("sa_wo", [P, TB, E])
        product = m.sb("sa_product", [P, 2, E, P])
        pair = [m.bank(f"sa_pair{i}", cols=1024) for i in range(2)]
        sb_, tb_, zb_, cb_ = m.bank("sa_scores"), m.bank("sa_probT_bank"), m.bank("sa_z_bank"), m.bank("sa_ctx_bank")
        sem = lambda n: m.sem("sa_" + n)
        xb_ready, z_made, z_copied, scored, maxed = (sem(n) for n in ("xb_ready", "z_made", "z_copied", "scored", "maxed"))
        exped, turned, turn_copied, ctx_made, ctx_copied = (sem(n) for n in ("exped", "turned", "turn_copied", "ctx_made", "ctx_copied"))
        pair_made, product_made, halved, product_free, values_ready = (sem(n) for n in ("pair_made", "product_made", "halved", "product_free", "values_ready"))
        block = stack.enter_context(nc.Block())

        @block.tensor
        def _(pe):
            pe.wait_ge(k.experts_in, k.EXPERTS_IN)
            with pe.Fori(0, B) as b:
                pe.wait_ge(xb_ready, b + 1)

                def z(h):
                    nc.tensor.matmul(zb_[:, 0:S], QK[:, h, :], xb[:], start=True, stop=True).then_inc(z_made, 1)

                def scores(h):
                    pe.wait_ge(z_copied, b * NH + (h + 1))
                    for t in range(TB):
                        last = nc.tensor.matmul(sb_[:, S * t:S * t + S], zT[:, P * t:P * t + P], xb[:], start=True, stop=True)
                    last.then_inc(scored, 1)

                def experts(n, lhsT, w, h):
                    pe.wait_ge(product_made, b * STEPS + (n + 1))
                    for half in range(2):
                        last = nc.tensor.matmul(pair[n % 2][:, 512 * half:512 * half + 512], lhsT,
                                                w[:, E * h + 4 * half:E * h + 4 * half + 4, :].rearrange("p e d -> p (e d)"),
                                                start=True, stop=True)
                    last.then_inc(pair_made, 1)
                    return last

                def expert_values(h):
                    for t in range(TB):
                        experts(4 * h - 2 + t if h else t, xb[:, P * t:P * t + P], k.v_w, h)

                z(0)
                scores(0)
                expert_values(0)
                for h in range(NH):
                    pe.wait_ge(exped, b * NH + (h + 1))
                    for kt in range(TB):
                        for t in range(TB):
                            last = nc.tensor.transpose(tb_[:, S * kt + P * t:S * kt + P * t + P], prob[:, t, P * kt:P * kt + P], k.ident[:])
                    last.then_inc(turned, 1)
                    if h + 1 < NH:
                        z(h + 1)
                        expert_values(h + 1)
                    pe.wait_ge(turn_copied, b * NH + (h + 1))
                    pe.wait_ge(values_ready, b * (2 * NH) + (2 * h + 2))
                    for kt in range(TB):
                        last = nc.tensor.matmul(cb_[:, 0:S], values[:, h % 2, kt, :], probT[:, kt, :], start=kt == 0, stop=kt == 1)
                    last.then_inc(ctx_made, 1)
                    if h + 1 < NH:
                        scores(h + 1)
                    pe.wait_ge(ctx_copied, b * NH + (h + 1))
                    for t in range(TB):
                        experts(min(4 * h + 4, STEPS - 2) + t, cT[:, P * t:P * t + P], k.o_w, h)

        @block.scalar
        def _(act):
            with act.Fori(0, B) as b:
                nc.scalar.activation(xb[:], XnT[:, bass.ds(b * S, S)], ACT.Copy).then_inc(xb_ready, 1)

                def copy_z(h):
                    act.wait_ge(z_made, b * NH + (h + 1))
                    nc.scalar.activation(zT[:], zb_[:, 0:S], ACT.Copy, scale=float(P) ** -0.5).then_inc(z_copied, 1)

                def exps(h):
                    act.wait_ge(maxed, b * NH + (h + 1))
                    for t in range(TB):
                        last = nc.scalar.activation(prob[:, t, :], sb_[:, S * t:S * t + S], ACT.Exp, bias=neg_max[:, t:t + 1],
                                                    accum_out=total[:, t:t + 1])
                    last.then_inc(exped, 1)

                copy_z(0)
                exps(0)
                for h in range(NH):
                    act.wait_ge(turned, b * NH + (h + 1))
                    nc.scalar.activation(probT[:].rearrange("p a s -> p (a s)"), tb_[:], ACT.Copy).then_inc(turn_copied, 1)
                    if h + 1 < NH:
                        copy_z(h + 1)
                    act.wait_ge(ctx_made, b * NH + (h + 1))
                    nc.scalar.activation(cT[:], cb_[:, 0:S], ACT.Copy).then_inc(ctx_copied, 1)
                    if h + 1 < NH:
                        exps(h + 1)

        @block.vector
        def _(dve):
            dve.sem_inc(product_made, 2)
            with dve.Fori(0, B) as b:
                def find_max(h):
                    dve.wait_ge(scored, b * NH + (h + 1))
                    nc.vector.tensor_reduce(neg_max[:], sb_[:].rearrange("p (t s) -> p t s", t=TB), AX.X, ALU.max,
                                            negate=True).then_inc(maxed, 1)

                def gated(n, gate):
                    dve.wait_ge(pair_made, b * STEPS + (n + 1))
                    dve.wait_ge(product_free, b * STEPS + (n + 1))
                    nc.vector.tensor_tensor(product[:, n % 2, :, :], pair[n % 2][:].rearrange("p (e d) -> p e d", e=E),
                                            gate.unsqueeze(2).broadcast_to([P, E, P]), ALU.mult).then_inc(product_made, 1)
                    dve.drain()
                    p = product[:, n % 2, :, :]
                    nc.vector.tensor_tensor(p[:, 0:4, :], p[:, 0:4, :], p[:, 4:8, :], ALU.add).then_inc(halved, 1)

                def gated_values(h):
                    for t in range(TB):
                        gated(4 * h - 2 + t if h else t, G[:, bass.ds(b * TB + t, 1), 0, h, :].rearrange("p a e -> p (a e)"))

                find_max(0)
                gated_values(0)
                for h in range(NH):
                    if h + 1 < NH:
                        gated_values(h + 1)
                    dve.wait_ge(exped, b * NH + (h + 1))
                    nc.vector.reciprocal(rec[:], total[:])
                    dve.drain()
                    for t in range(TB):
                        nc.vector.tensor_scalar(wo[:, t, :], G[:, bass.ds(b * TB + t, 1), 1, h, :].rearrange("p a e -> p (a e)"),
                                                rec[:, t:t + 1], None, ALU.mult)
                    if h + 1 < NH:
                        find_max(h + 1)
                    dve.drain()
                    for t in range(TB):
                        gated(min(4 * h + 4, STEPS - 2) + t, wo[:, t, :])

        @block.gpsimd
        def _(pool):
            pool.sem_inc(product_free, 2)
            with pool.Fori(0, B) as b:
                for n in range(STEPS):
                    is_values = n < 2 or (n % 4 >= 2 and n < STEPS - 2)
                    h, t = (n + 2) // 4 if is_values else (n - 4) // 4 if n < STEPS - 2 else NH - 1, n % 2
                    pool.wait_ge(halved, b * STEPS + (n + 1))
                    p = product[:, n % 2, :, :]
                    nc.gpsimd.tensor_tensor(p[:, 0:2, :], p[:, 0:2, :], p[:, 2:4, :], ALU.add)
                    pool.drain()
                    if is_values:
                        nc.gpsimd.tensor_tensor(values[:, h % 2, t, :], p[:, 0, :], p[:, 1, :], ALU.add).then_inc(values_ready, 1)
                        pool.drain().then_inc(product_free, 1)
                        continue
                    y = out[:, bass.ds(b * TB + t, 1), :].rearrange("p a d -> p (a d)")
                    if h == 0:
                        nc.gpsimd.tensor_tensor(y, p[:, 0, :], p[:, 1, :], ALU.add)
                    else:
                        nc.gpsimd.tensor_tensor(p[:, 0, :], p[:, 0, :], p[:, 1, :], ALU.add)
                        pool.drain()
                        nc.gpsimd.tensor_tensor(y, y, p[:, 0, :], ALU.add)
                    pool.drain().then_inc(product_free, 1)


WQ, WK, WV, WO_S, WQ_C, WK_C, WV_C, WO_C, WG, WU, WD = 0, 1, 2, 3, 4, 5, 6, 7, 8, 12, 16
BLOCKS = 20


def decoder(nc, k, io):
    with ExitStack() as stack:
        m = Memory(nc, stack)
        XX = m.sb("d_XX", [P, NT, D])
        layer_norm(nc, k, k.X, XX, tag="d_")
        c = DecoderConstants(m)
        decoder_constants(nc, k, io, c)
        decoder_layers(nc, k, io, c, XX)
        decoder_end(nc, k, c, XX)


class DecoderConstants:

    def __init__(self, m):
        self.cos, self.sin = m.sb("cos", [P, S]), m.sb("sin", [P, S])
        self.rot = m.sb("rot", [P, P])
        self.spread = m.sb("spread", [P, 2, 2, 4, P], R32)
        self.blocked = m.sb("blocked", [P, NT, S], BF16)
        self.norms, self.bias_qk = m.sb("norms", [P, 3, LAYERS]), m.sb("bias_qk", [P, LAYERS, 2])
        self.bias_v, self.bias_o = m.sb("bias_v", [P, LAYERS, D]), m.sb("bias_o", [P, LAYERS, D])
        self.nf = m.sb("nf", [P, D])


def decoder_constants(nc, k, io, c):
    SCALE = 8 ** -0.5
    with ExitStack() as stack:
        m = Memory(nc, stack)
        ids, seg, low = m.sb("ids", [P, NT], mybir.dt.int32), m.sb("seg", [P, NT]), m.sb("low", [P, NT])
        jj, key = m.sb("jj", [P, S], mybir.dt.int32), m.sb("key", [P, S])
        above, below = m.sb("above", [P, NT, S]), m.sb("below", [P, NT, S])
        spread = m.sb("spread_f", [P, 16, P])
        loaded, iota_made = m.sem("dc_loaded"), m.sem("dc_iota_made")
        block = stack.enter_context(nc.Block())

        @block.sync
        def _(sp):
            def load(dst, src):
                sp.dma_start(dst, src).then_inc(loaded, 16)
            with nc.allow_non_contiguous_dma("small parameters, a column each"):
                load(ids[:], io["itok_BxS_0_255"].rearrange("b (t p) -> p (b t)", p=P))
                load(c.cos[:], io["rope_cos"])
                load(c.sin[:], io["rope_sin"])
                load(c.rot[:], io["rope_turn"])
                load(spread[:], io["spread_rows"])
                for i, n in enumerate(("n1", "n2", "n3")):
                    load(c.norms[:, i, :], io["L1_xattn_" + n].rearrange("l d -> d l"))
                for i in range(2):
                    load(c.bias_qk[:, :, i], io["L1_xattn_bqkv"][:, D * i:D * i + D].rearrange("l d -> d l"))
                load(c.bias_v[:], io["L1_xattn_bqkv"][:, 2 * D:3 * D].rearrange("(a l) d -> a l d", a=1).broadcast_to([P, LAYERS, D]))
                load(c.bias_o[:], io["L1_xattn_bo"].rearrange("(a l) d -> a l d", a=1).broadcast_to([P, LAYERS, D]))
                load(c.nf[:], io["L1_xattn_nf"].rearrange("(a d) -> a d", a=1).broadcast_to([P, D]))

        @block.gpsimd
        def _(pool):
            nc.gpsimd.iota(jj[:], pattern=[[1, S]], base=0, channel_multiplier=0)
            pool.drain()
            nc.gpsimd.tensor_copy(key[:], jj[:]).then_inc(iota_made, 1)

        @block.scalar
        def _(act):
            act.wait_ge(loaded, 13 * 16)
            nc.scalar.activation(c.spread[:].rearrange("p a b j r -> p (a b j r)"), spread[:].rearrange("p n r -> p (n r)"), ACT.Copy)

        @block.vector
        def _(dve):
            dve.wait_ge(loaded, 13 * 16)
            nc.vector.tensor_copy(seg[:], ids[:])
            nc.vector.tensor_scalar(c.bias_qk[:, :, 0], c.bias_qk[:, :, 0], SCALE, None, ALU.mult)
            dve.drain()
            nc.vector.tensor_scalar(low[:], seg[:], -128.0, None, ALU.add)
            dve.wait_ge(iota_made, 1)
            dve.drain()
            for t in range(NT):
                nc.vector.tensor_scalar(above[:, t, :], key[:], seg[:, t:t + 1], NEG, ALU.is_gt, ALU.mult)
                nc.vector.tensor_scalar(below[:, t, :], key[:], low[:, t:t + 1], NEG, ALU.is_le, ALU.mult)
            dve.drain()
            nc.vector.tensor_tensor(c.blocked[:], above[:], below[:], ALU.add)


def decoder_layers(nc, k, io, c, XX):
    NH, HD, PAIRS = 16, 8, B // 2
    HG, ROWS = 4, 32
    ONE = 2 * HD
    SCALE = HD ** -0.5
    W_LOADS = 8
    SELF, CROSS = 0, 1
    TURNS = [(0, SELF), (1, SELF), (0, CROSS), (1, CROSS)]
    FIRST_AT, MEMORY_AT, MIDDLE_AT, END_AT = (2, 3, 5, 8, 10), [(12,), (0,), (0,)], (2, 5, 6, 9, 10, 12), (2, 5, 6, 9, 10, 12, 14)
    QUERIES, KEYS = 0, 1
    WEIGHTS, SCORES = "last weighted values", "first scores"
    FIRST_STEPS, END_STEPS = ["first%d" % i for i in range(5)], ["end%d" % i for i in range(7)]
    BOUNDARY = {False: ["first0", WEIGHTS, "first1", "end0", "first2", "end1", "end2", "first3", "end3", "first4", "end4", SCORES, "end5", "end6"],
                True: [WEIGHTS] + END_STEPS}
    SPREADS = 4
    with ExitStack() as stack:
        m = Memory(nc, stack)
        WN, WT = m.sb("d_WN", [P, BLOCKS, P]), m.sb("d_WT", [P, BLOCKS, P])
        norm_w, bias, bias_v = m.sb("d_norm_w", [P, 3]), m.sb("d_bias", [P, 2]), m.sb("d_bias_v", [P, D])

        def rows(name, shape, dtype=FP32):
            return [m.sb(f"d_{name}{r}", shape, dtype) for r in range(2)]
        mem = m.sb("mem", [P, 2 * S])
        ss, rs, h, hT = rows("ss", [P, TB]), rows("rs", [P, TB]), rows("h", [P, TB, D]), rows("hT", [P, S])
        qs, ks = rows("qs", [P, 4, S], R32), [rows("ks", [P, 4, S], R32), rows("ks_memory", [P, 4, S], R32)]
        V = rows("V", [P, TB, NH * P], R32)
        OT, o, oT = rows("OT", [P, 4, S]), rows("o", [P, TB, D]), rows("oT", [P, S])
        qk, turned_sin = m.sb("d_qk", [P, 2, S]), m.sb("d_turned_sin", [P, 2, S])
        kc, vc = m.sb("d_kc", [P, 2, S]), m.sb("d_vc", [P, 2, TB * D])
        qc, vf = m.sb("d_qc", [P, S]), m.sb("d_vf", [P, TB * D])
        halves = m.sb("d_halves", [P, 2, 2, S], R32)
        rec, proj = m.sb("d_rec", [P, TB, NH]), m.sb("d_proj", [P, TB, D])
        tg, aT = m.sb("d_tg", [P, 2, S]), m.sb("d_aT", [P, 4, S])
        neg_max = m.sb("d_neg_max", [P, 4, TB])
        prob, probT = m.sb("d_prob", [P, 2, 512]), m.sb("d_probT", [P, 4, 2, 512], R32)
        A = [m.bank(f"d_A{i}") for i in range(2)]
        T = [m.bank(f"d_T{i}") for i in range(2)]
        O = [m.bank(f"d_O{i}") for i in range(2)]
        G = [m.bank(f"d_G{i}") for i in range(2)]
        sem = lambda n: m.sem("dl_" + n)
        both = lambda n: [sem(n + str(r)) for r in range(2)]
        w_in, w_read, w_turned, w_ready, zeros_set = (sem(n) for n in ("w_in", "w_read", "w_turned", "w_ready", "zeros_set"))
        ss_ready, r_ready, h_ready, h_turned, hT_ready = (both(n) for n in ("ss_ready", "r_ready", "h_ready", "h_turned", "hT_ready"))
        qk_made, qk_biased, qk_turned, roped = (both(n) for n in ("qk_made", "qk_biased", "qk_turned", "roped"))
        mem_ready, memory_made, memory_in, memory_halved = (sem(n) for n in ("mem_ready", "memory_made", "memory_in", "memory_halved"))
        v_made, v_in, values_ready, qc_made, qc_in, halved = (
            both(n) for n in ("v_made", "v_in", "values_ready", "qc_made", "qc_in", "halved"))
        spread, spread_copied = both("spread"), both("spread_copied")
        scored, maxed, exped, turned, high_ready, low_ready, attended, O_copied = (
            sem(n) for n in ("scored", "maxed", "exped", "turned", "high_ready", "low_ready", "attended", "O_copied"))
        O_turned, o_ready, o_turned, oT_ready, projected = (both(n) for n in ("O_turned", "o_ready", "o_turned", "oT_ready", "projected"))
        gated, upped, tanhed, act_ready, downed, row_done = (both(n) for n in ("gated", "upped", "tanhed", "act_ready", "downed", "row_done"))
        block = stack.enter_context(nc.Block())

        FIRST_BANKS = [A, G]

        TILES = {SELF: [(0, P, 0), (1, S, P)], CROSS: [(0, S, 0), (1, S, S)]}
        WIDTH = {SELF: P + S, CROSS: 2 * S}
        BLOCKS_OF = {SELF: [(0, 0), (P, P), (2 * P, 2 * P)], CROSS: [(0, 0), (S, P), (P, S), (S + P, S + P)]}
        WEIGHTED = {SELF: [(0, 0, S, 0), (1, P, P, S)], CROSS: [(0, 0, S, 0), (1, 0, S, S)]}

        def value_columns(r, kt, n):
            at = P * n - ROWS * (n % HG)
            return V[r][:, kt, at:at + P]

        def value_slots(r, kt, first, count):
            return V[r][:, kt, :].rearrange("p (j q w) -> p j q w", j=4, q=4)[:, :, :, first:first + count]

        def by_place(columns):
            return columns.rearrange("p (q j d) -> p j q d", q=4, j=4)

        @block.sync
        def _(sp):
            with sp.Fori(0, LAYERS) as l:
                sp.wait_ge(w_read, l + 1)
                def load(at, n, name, cols):
                    w = io["L1_xattn_" + name][bass.ds(l, 1)]
                    if cols:
                        src = w.rearrange("a p (c d) -> p (a c) d", c=n)
                    else:
                        src = w.rearrange("a (c p) d -> p (a c) d", c=n)
                    sp.dma_start(WN[:, at:at + n, :], src).then_inc(w_in, 16)
                load(WQ, 3, "Wqkv", False)
                load(WO_S, 1, "Wo", False)
                load(WQ_C, 1, "Wq_c", False)
                load(WK_C, 2, "Wkv_c", False)
                load(WO_C, 1, "Wo_c", False)
                load(WG, 4, "Wg", False)
                load(WU, 4, "Wu", False)
                load(WD, 4, "Wd", True)

        @block.tensor
        def _(pe):
            pe.sem_inc(w_read, 1)
            pe.sem_inc(row_done[1], 1)
            pe.wait_ge(zeros_set, 1)
            with pe.Fori(0, LAYERS) as l:
                pe.wait_ge(w_in, l * (16 * W_LOADS) + 16 * W_LOADS)
                for g in range(BLOCKS // 4):
                    bank = (A + T + O)[g]
                    for i in range(4):
                        last = nc.tensor.transpose(bank[:, P * i:P * i + P], WN[:, 4 * g + i, :], k.ident[:])
                    last.then_inc(w_turned, 1)
                pe.wait_ge(w_ready, l + 1)
                pe.sem_inc(w_read, 1)

                def spread_out(r, which, at=None, banks=G):
                    at = which if at is None else at
                    for j in range(4):
                        for half in (HIGH, LOW):
                            last = nc.tensor.matmul(banks[j // 2][:, S * (j % 2):S * (j % 2) + S], c.spread[:, which, half, j, :], halves[:, at, half, :],
                                                    start=half == HIGH, stop=half == LOW)
                    last.then_inc(spread[r], 1)

                def turn_h(it, r, j, bank):
                    pe.wait_ge(h_ready[r], it * 3 + (j + 1))
                    for t in range(TB):
                        last = nc.tensor.transpose(bank[:, P * t:P * t + P], h[r][:, t, :], k.ident[:])
                    last.then_inc(h_turned[r], 1)

                def project_self(it, r, banks):
                    pe.wait_ge(hT_ready[r], it * 3 + 1)
                    if r == 1:
                        pe.wait_ge(row_done[1], it + 1)
                    for i, w in enumerate((WQ, WK)):
                        last = nc.tensor.matmul(banks[1][:, S * i:S * i + S], WT[:, w, :], hT[r][:], start=True, stop=True)
                    last.then_inc(qk_made[r], 1)
                    for t in range(TB):
                        last = nc.tensor.matmul(banks[0][:, P * t:P * t + P], hT[r][:, P * t:P * t + P], WT[:, WV, :], start=True, stop=True)
                    last.then_inc(v_made[r], 1)

                def turn_qk(it, r, banks):
                    pe.wait_ge(qk_biased[r], it + 1)
                    nc.tensor.matmul(banks[1][:], c.rot[:], qk[:].rearrange("p c s -> p (c s)"), start=True, stop=True).then_inc(qk_turned[r], 1)

                def first(it, r, step):
                    banks = FIRST_BANKS[r]
                    if step == 0:
                        turn_h(it, r, 0, banks[0])
                    elif step == 1:
                        project_self(it, r, banks)
                    elif step == 2:
                        turn_qk(it, r, banks)
                    elif step == 3:
                        pe.wait_ge(halved[r], it * 3 + 1)
                        spread_out(r, QUERIES, banks=banks)
                    elif step == 4:
                        pe.wait_ge(spread_copied[r], it * SPREADS + 1)
                        pe.wait_ge(halved[r], it * 3 + 2)
                        spread_out(r, KEYS, banks=banks)

                def scores(it, bp, turn, n):
                    r, kind = TURNS[turn]
                    if n == 0:
                        pe.wait_ge(spread_copied[r], it * SPREADS + (2 * kind + 2))
                    place, at = n // 4, n % 4 * ROWS
                    for t, keys_n, col in TILES[kind]:
                        nc.tensor.matmul(A[n % 2][:, col:col + keys_n], qs[r][at:at + ROWS, place, P * t:P * t + P],
                                         ks[kind][r][at:at + ROWS, place, 0:keys_n], start=True, stop=False)
                        if kind == SELF:
                            d = col + t * P
                            last = nc.tensor.matmul(A[n % 2][:, d:d + P], k.identb[:], k.causalb[:, 0, :], start=False, stop=True)
                        else:
                            last = nc.tensor.matmul(A[n % 2][:, col:col + keys_n], k.identb[:],
                                                    c.blocked[:, bass.ds(bp * (2 * TB) + (r * TB + t), 1), :].rearrange("p a s -> p (a s)"),
                                                    start=False, stop=True)
                    last.then_inc(scored, 1)

                def pair(bp, last_pair):
                    it = l * PAIRS + bp

                    def memory():
                        pe.wait_ge(spread_copied[1], it * SPREADS + 2)
                        pe.wait_ge(mem_ready, it + 1)
                        nc.tensor.matmul(G[0][:], WT[:, WK_C, :], mem[:], start=True, stop=True)
                        for t in range(2 * TB):
                            last = nc.tensor.matmul(G[1][:, P * t:P * t + P], mem[:, P * t:P * t + P], WT[:, WV_C, :], start=True, stop=True)
                        last.then_inc(memory_made, 1)

                    def turn_O(r, a):
                        pe.wait_ge(O_copied, it * 4 + (2 * a + r + 2))
                        for t in range(TB):
                            for g in range(4):
                                last = nc.tensor.transpose(G[t][:, P * g:P * g + P], OT[r][:, g, P * t:P * t + P], k.ident[:])
                        last.then_inc(O_turned[r], 1)

                    def turn_o(r, a):
                        pe.wait_ge(o_ready[r], it * 2 + (a + 1))
                        for t in range(TB):
                            last = nc.tensor.transpose(G[0][:, P * t:P * t + P], o[r][:, t, :], k.ident[:])
                        last.then_inc(o_turned[r], 1)

                    def project_out(r, a):
                        pe.wait_ge(oT_ready[r], it * 2 + (a + 1))
                        for t in range(TB):
                            last = nc.tensor.matmul(G[1][:, P * t:P * t + P], oT[r][:, P * t:P * t + P], WT[:, (WO_S, WO_C)[a], :], start=True, stop=True)
                        last.then_inc(projected[r], 1)

                    def project_cross(r):
                        pe.wait_ge(hT_ready[r], it * 3 + 2)
                        nc.tensor.matmul(G[1][:, 0:S], WT[:, WQ_C, :], hT[r][:], start=True, stop=True).then_inc(qc_made[r], 1)

                    def feed(r, i):
                        pe.wait_ge(hT_ready[r], it * 3 + 3)
                        if i:
                            pe.wait_ge(act_ready[r], it * 2 + 1)
                        for w, bank, made in ((WG, G[0], gated[r]), (WU, G[1], upped[r])):
                            for f in range(2):
                                last = nc.tensor.matmul(bank[:, S * f:S * f + S], WT[:, w + 2 * i + f, :], hT[r][:], start=True, stop=True)
                            last.then_inc(made, 1)

                    def down(r):
                        pe.wait_ge(act_ready[r], it * 2 + 2)
                        for t in range(TB):
                            for f in range(4):
                                last = nc.tensor.matmul(G[1][:, P * t:P * t + P], aT[:, f, P * t:P * t + P], WT[:, WD + f, :], start=f == 0, stop=f == 3)
                        last.then_inc(downed[r], 1)

                    def of_memory(turn, n):
                        if turn == 0:
                            memory()
                        elif turn == 1:
                            pe.wait_ge(memory_in, it + 1)
                            pe.wait_ge(memory_halved, it * 2 + 1)
                            spread_out(0, KEYS, at=0)
                        else:
                            pe.wait_ge(spread_copied[0], it * SPREADS + 4)
                            pe.wait_ge(memory_halved, it * 2 + 2)
                            spread_out(1, KEYS, at=1)

                    def middle(r, step):
                        if step == 0:
                            pe.wait_ge(spread_copied[r], it * SPREADS + 3)
                            turn_O(r, SELF)
                        elif step == 1:
                            turn_o(r, SELF)
                        elif step == 2:
                            project_out(r, SELF)
                        elif step == 3:
                            turn_h(it, r, 1, G[0])
                        elif step == 4:
                            project_cross(r)
                        elif step == 5:
                            pe.wait_ge(halved[r], it * 3 + 3)
                            spread_out(r, QUERIES)

                    def end(r, step):
                        if step == 0:
                            if r == 1:
                                pe.wait_ge(row_done[0], it + 1)
                            turn_O(r, CROSS)
                        elif step == 1:
                            turn_o(r, CROSS)
                        elif step == 2:
                            project_out(r, CROSS)
                        elif step == 3:
                            turn_h(it, r, 2, G[0])
                        elif step == 4:
                            feed(r, 0)
                        elif step == 5:
                            feed(r, 1)
                        elif step == 6:
                            down(r)

                    def steps_after(turn, n):
                        if turn == 0 and n in FIRST_AT:
                            first(it, 1, FIRST_AT.index(n))
                        if turn < 3 and n in MEMORY_AT[turn]:
                            of_memory(turn, n)
                        if turn in (1, 2) and n in MIDDLE_AT:
                            middle(turn - 1, MIDDLE_AT.index(n))
                        if turn == 3 and n in END_AT:
                            end(0, END_AT.index(n))

                    def weighted(turn, n):
                        r, kind = TURNS[turn]
                        if n == 0:
                            pe.wait_ge(O_copied, it * 4 + (turn + 1))
                            pe.wait_ge(values_ready[r], it * 2 + (kind + 1))
                        for kt, q0, queries, col in WEIGHTED[kind]:
                            at = n // HG % 2 * S + q0
                            for half in (HIGH, LOW):
                                last = nc.tensor.matmul(O[n // HG // 2][:, at:at + queries], value_columns(r, kt, n),
                                                        probT[:, n % 4, half, col:col + queries],
                                                        start=n % HG == 0 and kt == 0 and half == HIGH, stop=n % HG == HG - 1 and kt == 1 and half == LOW)
                        if n == NH - 1:
                            last.then_inc(attended, 1)

                    for turn in range(4):
                        kind = TURNS[turn][1]
                        for n in range(NH):
                            at = turn * NH + n
                            pe.wait_ge(exped, it * (4 * NH) + (at + 1))
                            if at >= 2:
                                pe.wait_ge(low_ready, it * (4 * NH) + (at - 1))
                            for col, colT in BLOCKS_OF[kind]:
                                last = nc.tensor.transpose(T[n % 2][:, colT:colT + P], prob[:, n % 2, col:col + P], k.ident[:])
                            last.then_inc(turned, 1)
                            if at + 2 < 4 * NH:
                                scores(it, bp, (at + 2) // NH, (at + 2) % NH)
                            if at >= 2:
                                weighted((at - 2) // NH, (at - 2) % NH)
                            steps_after(turn, n)
                    def last_weighted():
                        for n in (NH - 2, NH - 1):
                            pe.wait_ge(low_ready, it * (4 * NH) + (3 * NH + n + 1))
                            weighted(3, n)

                    for work in BOUNDARY[last_pair]:
                        if work == WEIGHTS:
                            last_weighted()
                        elif work == SCORES:
                            for n in range(2):
                                scores(it + 1, bp, 0, n)
                        elif work in FIRST_STEPS:
                            first(it + 1, 0, FIRST_STEPS.index(work))
                        else:
                            end(1, END_STEPS.index(work))

                for step in range(5):
                    first(l * PAIRS, 0, step)
                for n in range(2):
                    scores(l * PAIRS, 0, 0, n)
                with pe.Fori(0, PAIRS - 1) as bp:
                    pair(bp, False)
                pair(PAIRS - 1, True)

        @block.scalar
        def _(act):
            act.sem_inc(O_copied, 1)
            with act.Fori(0, LAYERS) as l:
                for g in range(BLOCKS // 4):
                    act.wait_ge(w_turned, l * (BLOCKS // 4) + (g + 1))
                    last = nc.scalar.activation(WT[:, 4 * g:4 * g + 4, :].rearrange("p c d -> p (c d)"), (A + T + O)[g][:], ACT.Copy)
                nc.scalar.activation(norm_w[:], c.norms[:, :, bass.ds(l, 1)].rearrange("p n a -> p (n a)"), ACT.Copy)
                nc.scalar.activation(bias[:], c.bias_qk[:, bass.ds(l, 1), :].rearrange("p a n -> p (a n)"), ACT.Copy)
                act.drain().then_inc(w_ready, 1)
                def copy_spread(it, r, which, count, kind=SELF, banks=G):
                    act.wait_ge(spread[r], it * SPREADS + count)
                    dst = (qs, ks[kind])[which][r]
                    for i in range(2):
                        last = nc.scalar.activation(dst[:, 2 * i:2 * i + 2, :].rearrange("p j s -> p (j s)"), banks[i][:], ACT.Copy)
                    last.then_inc(spread_copied[r], 1)

                def copy_h(it, r, j, bank=G[0]):
                    act.wait_ge(h_turned[r], it * 3 + (j + 1))
                    nc.scalar.activation(hT[r][:], bank[:, 0:S], ACT.Copy, scale=norm_w[:, j:j + 1]).then_inc(hT_ready[r], 1)

                def copy_qk(it, r, bank):
                    act.wait_ge(qk_made[r], it + 1)
                    nc.scalar.activation(qk[:, 0, :], bank[:, 0:S], ACT.Identity, scale=SCALE, bias=bias[:, 0:1])
                    nc.scalar.activation(qk[:, 1, :], bank[:, S:2 * S], ACT.Identity, bias=bias[:, 1:2]).then_inc(qk_biased[r], 1)

                def first(it, r, step):
                    banks = FIRST_BANKS[r]
                    if step == 0:
                        copy_h(it, r, 0, banks[0])
                    elif step == 1:
                        copy_qk(it, r, banks[1])
                    elif step == 3:
                        copy_spread(it, r, QUERIES, 1, banks=banks)
                    elif step == 4:
                        copy_spread(it, r, KEYS, 2, banks=banks)

                def pair(bp, last_pair):
                    it = l * PAIRS + bp

                    def copy_memory():
                        act.wait_ge(memory_made, it + 1)
                        nc.scalar.activation(kc[:].rearrange("p r s -> p (r s)"), G[0][:], ACT.Copy)
                        nc.scalar.activation(vc[:].rearrange("p r s -> p (r s)"), G[1][:], ACT.Copy).then_inc(memory_in, 1)

                    def copy_o(r, a):
                        act.wait_ge(o_turned[r], it * 2 + (a + 1))
                        nc.scalar.activation(oT[r][:], G[0][:, 0:S], ACT.Copy).then_inc(oT_ready[r], 1)

                    def copy_qc(r):
                        act.wait_ge(qc_made[r], it + 1)
                        nc.scalar.activation(qc[:], G[1][:, 0:S], ACT.Copy, scale=SCALE).then_inc(qc_in[r], 1)

                    def tanh(r, i):
                        act.wait_ge(gated[r], it * 2 + (i + 1))
                        nc.scalar.activation(tg[:].rearrange("p f s -> p (f s)"), G[0][:], ACT.Tanh, scale=0.5).then_inc(tanhed[r], 1)

                    def of_memory(turn, n):
                        if turn == 0:
                            copy_memory()
                        else:
                            copy_spread(it, turn - 1, KEYS, 3, kind=CROSS)

                    def middle(r, step):
                        if step == 1:
                            copy_o(r, SELF)
                        elif step == 3:
                            copy_h(it, r, 1)
                        elif step == 4:
                            copy_qc(r)
                        elif step == 5:
                            copy_spread(it, r, QUERIES, 4)

                    def end(r, step):
                        if step == 1:
                            copy_o(r, CROSS)
                        elif step == 3:
                            copy_h(it, r, 2)
                        elif step in (4, 5):
                            tanh(r, step - 4)

                    def steps_after(turn, n):
                        if turn == 0 and n in FIRST_AT:
                            first(it, 1, FIRST_AT.index(n))
                        if turn < 3 and n in MEMORY_AT[turn]:
                            of_memory(turn, n)
                        if turn in (1, 2) and n in MIDDLE_AT:
                            middle(turn - 1, MIDDLE_AT.index(n))
                        if turn == 3 and n in END_AT:
                            end(0, END_AT.index(n))

                    def exps(turn, n):
                        kind = TURNS[turn][1]
                        act.wait_ge(maxed, it * (4 * NH) + (turn * NH + n + 1))
                        for t, keys_n, col in TILES[kind]:
                            last = nc.scalar.activation(prob[:, n % 2, col:col + keys_n], A[n % 2][:, col:col + keys_n], ACT.Exp,
                                                        bias=neg_max[:, n % 4, t:t + 1])
                        last.then_inc(exped, 1)

                    def copy_high(turn, n):
                        act.wait_ge(turned, it * (4 * NH) + (turn * NH + n + 1))
                        width = WIDTH[TURNS[turn][1]]
                        nc.scalar.activation(probT[:, n % 4, HIGH, 0:width], T[n % 2][:, 0:width], ACT.Copy).then_inc(high_ready, 1)

                    def copy_O(turn):
                        r = TURNS[turn][0]
                        act.wait_ge(attended, it * 4 + (turn + 1))
                        for i in range(2):
                            last = nc.scalar.activation(OT[r][:, 2 * i:2 * i + 2, :].rearrange("p g s -> p (g s)"), O[i][:], ACT.Copy)
                        last.then_inc(O_copied, 1)

                    nc.scalar.activation(mem[:], k.ctxT[:, bass.ds(bp * (2 * S), 2 * S)], ACT.Copy).then_inc(mem_ready, 1)
                    for turn in range(4):
                        for n in range(NH):
                            exps(turn, n)
                            if turn and n == 2:
                                copy_O(turn - 1)
                            if n:
                                copy_high(turn, n - 1)
                            elif turn:
                                copy_high(turn - 1, NH - 1)
                            if n >= 2:
                                steps_after(turn, n - 2)
                    copy_high(3, NH - 1)
                    for work in BOUNDARY[last_pair]:
                        if work in FIRST_STEPS:
                            first(it + 1, 0, FIRST_STEPS.index(work))
                        elif work in END_STEPS:
                            if work == END_STEPS[0]:
                                copy_O(3)
                            end(1, END_STEPS.index(work))

                for step in range(5):
                    first(l * PAIRS, 0, step)
                with act.Fori(0, PAIRS - 1) as bp:
                    pair(bp, False)
                pair(PAIRS - 1, True)

        @block.gpsimd
        def _(pool):
            def root(it, r, j):
                pool.wait_ge(ss_ready[r], it * 3 + (j + 1))
                nc.gpsimd.tensor_tensor(rs[r][:], ss[r][:], k.minus_half[:, 0:TB], ALU.pow).then_inc(r_ready[r], 1)

            def split(dst, src):
                nc.gpsimd.tensor_tensor(dst(HIGH), src, k.ones[:], ALU.mult)
                pool.drain()
                return nc.gpsimd.tensor_tensor(dst(LOW), src, dst(HIGH).bitcast(FP32), ALU.subtract)

            def split_values(it, r, kind):
                if kind == SELF:
                    pool.wait_ge(v_in[r], it + 1)
                else:
                    pool.wait_ge(attended, it * 4 + (r + 1))
                src = (vf[:], vc[:, r, :])[kind]
                one = by_place(k.ones[:, 0:1].broadcast_to([P, D]))
                for kt in range(TB):
                    nc.gpsimd.tensor_tensor(value_slots(r, kt, 0, HD), by_place(src[:, P * kt:P * kt + P]), one, ALU.mult)
                pool.drain()
                for kt in range(TB):
                    last = nc.gpsimd.tensor_tensor(value_slots(r, kt, HD, HD), by_place(src[:, P * kt:P * kt + P]),
                                                   value_slots(r, kt, 0, HD).bitcast(FP32), ALU.subtract)
                last.then_inc(values_ready[r], 1)

            def first(it, r):
                split_values(it, r, SELF)
                pool.wait_ge(roped[r], it + 1)
                for which in (QUERIES, KEYS):
                    split(lambda half: halves[:, which, half, :], qk[:, which, :]).then_inc(halved[r], 1)

            def pair(it, last_pair):
                root(it, 1, 0)
                first(it, 1)
                pool.wait_ge(memory_in, it + 1)
                for r in range(2):
                    split(lambda half: halves[:, r, half, :], kc[:, r, :]).then_inc(memory_halved, 1)
                for r in range(2):
                    split_values(it, r, CROSS)
                    root(it, r, 1)
                    pool.wait_ge(qc_in[r], it + 1)
                    split(lambda half: halves[:, QUERIES, half, :], qc[:]).then_inc(halved[r], 1)
                root(it, 0, 2)
                if not last_pair:
                    root(it + 1, 0, 0)
                    first(it + 1, 0)
                root(it, 1, 2)

            with pool.Fori(0, LAYERS) as l:
                root(l * PAIRS, 0, 0)
                first(l * PAIRS, 0)
                with pool.Fori(0, PAIRS - 1) as bp:
                    pair(l * PAIRS + bp, False)
                pair(l * PAIRS + (PAIRS - 1), True)

        @block.vector
        def _(dve):
            for v in V:
                nc.vector.memset(v[:].bitcast(FP32), 0.0)
            dve.drain()
            for r in range(2):
                for kt in range(TB):
                    nc.vector.memset(value_slots(r, kt, ONE, 1).bitcast(FP32), 1.0)
            dve.drain().then_inc(zeros_set, 1)
            with dve.Fori(0, LAYERS) as l:
                def row(bp, r):
                    return XX[:, bass.ds(bp * (2 * TB) + r * TB, TB), :]

                def normed(bp, r):
                    x = row(bp, r)
                    nc.vector.tensor_tensor(h[r][:], x, x, ALU.mult)
                    dve.drain()
                    nc.vector.tensor_reduce(ss[r][:], h[r][:], AX.X, ALU.add)
                    dve.drain()
                    nc.vector.tensor_scalar(ss[r][:], ss[r][:], 1.0 / D, 1e-6, ALU.mult, ALU.add).then_inc(ss_ready[r], 1)

                def scaled_h(bp, r, j):
                    dve.wait_ge(r_ready[r], (l * PAIRS + bp) * 3 + (j + 1))
                    nc.vector.tensor_tensor(h[r][:], row(bp, r), rs[r][:].unsqueeze(2).broadcast_to([P, TB, D]), ALU.mult).then_inc(h_ready[r], 1)

                def add_bias_v(it, r, bank):
                    dve.wait_ge(v_made[r], it + 1)
                    nc.vector.tensor_tensor(vf[:].rearrange("p (t d) -> p t d", t=TB), bank[:, 0:TB * D].rearrange("p (t d) -> p t d", t=TB),
                                            bias_v[:].unsqueeze(1).broadcast_to([P, TB, D]), ALU.add).then_inc(v_in[r], 1)

                def rope(it, r, bank):
                    wide = lambda a: a.unsqueeze(1).broadcast_to([P, 2, S])
                    dve.wait_ge(qk_turned[r], it + 1)
                    nc.vector.tensor_tensor(turned_sin[:], bank[:].rearrange("p (c s) -> p c s", c=2), wide(c.sin[:]), ALU.mult)
                    nc.vector.tensor_tensor(qk[:], qk[:], wide(c.cos[:]), ALU.mult)
                    dve.drain()
                    nc.vector.tensor_tensor(qk[:], qk[:], turned_sin[:], ALU.add).then_inc(roped[r], 1)

                def first(it, r, step):
                    if step == 1:
                        add_bias_v(it, r, FIRST_BANKS[r][0])
                    elif step == 2:
                        rope(it, r, FIRST_BANKS[r][1])

                def find_max(it, turn, n):
                    kind = TURNS[turn][1]
                    dve.wait_ge(scored, it * (4 * NH) + (turn * NH + n + 1))
                    if kind == CROSS:
                        last = nc.vector.tensor_reduce(neg_max[:, n % 4, :], A[n % 2][:].rearrange("p (t s) -> p t s", t=TB), AX.X, ALU.max, negate=True)
                    else:
                        for t, keys_n, col in TILES[kind]:
                            last = nc.vector.tensor_reduce(neg_max[:, n % 4, t:t + 1], A[n % 2][:, col:col + keys_n], AX.X, ALU.max, negate=True)
                    last.then_inc(maxed, 1)

                def pair(bp, last_pair):
                    it = l * PAIRS + bp

                    def normalise(r, a):
                        dve.wait_ge(O_turned[r], it * 2 + (a + 1))
                        wide = [G[t][:].rearrange("p (n w) -> p n w", w=ROWS) for t in range(TB)]
                        of_heads = lambda t, first: wide[t][:, :, first:first + HD].rearrange("p (j q) d -> p j q d", j=4)
                        for t in range(TB):
                            nc.vector.reciprocal(rec[:, t], wide[t][:, :, ONE])
                            nc.vector.tensor_copy(by_place(proj[:, t]), of_heads(t, 0))
                        dve.drain()
                        for t in range(TB):
                            nc.vector.tensor_tensor(by_place(proj[:, t]), by_place(proj[:, t]), of_heads(t, HD), ALU.add)
                        dve.drain()
                        for t in range(TB):
                            last = nc.vector.tensor_tensor(by_place(o[r][:, t]), by_place(proj[:, t]),
                                                           rec[:, t].rearrange("p (j q) -> p j q", j=4).unsqueeze(3).broadcast_to([P, 4, 4, HD]), ALU.mult)
                        last.then_inc(o_ready[r], 1)

                    def add_out(r, a):
                        dve.wait_ge(projected[r], it * 2 + (a + 1))
                        y = G[1][:, 0:TB * D].rearrange("p (t d) -> p t d", t=TB)
                        if a == SELF:
                            nc.vector.tensor_tensor(proj[:], y, c.bias_o[:, bass.ds(l, 1), :].broadcast_to([P, TB, D]), ALU.add)
                            dve.drain()
                            y = proj[:]
                        nc.vector.tensor_tensor(row(bp, r), row(bp, r), y, ALU.add)
                        dve.drain()
                        normed(bp, r)

                    def activate(r, i):
                        dve.wait_ge(tanhed[r], it * 2 + (i + 1))
                        g = tg[:].rearrange("p f s -> p (f s)")
                        nc.vector.scalar_tensor_tensor(g, g, 1.0, G[0][:], ALU.add, ALU.mult)
                        dve.drain()
                        dve.wait_ge(upped[r], it * 2 + (i + 1))
                        nc.vector.scalar_tensor_tensor(aT[:, 2 * i:2 * i + 2, :].rearrange("p f s -> p (f s)"), g, 0.5, G[1][:],
                                                       ALU.mult, ALU.mult).then_inc(act_ready[r], 1)

                    def add_down(r):
                        dve.wait_ge(downed[r], it + 1)
                        nc.vector.tensor_tensor(row(bp, r), row(bp, r), G[1][:, 0:TB * D].rearrange("p (t d) -> p t d", t=TB), ALU.add)
                        dve.drain().then_inc(row_done[r], 1)

                    def middle(r, step):
                        if step == 0:
                            normalise(r, SELF)
                        elif step == 2:
                            add_out(r, SELF)

                    def end(r, step):
                        if step == 0:
                            normalise(r, CROSS)
                        elif step == 2:
                            add_out(r, CROSS)
                        elif step in (4, 5):
                            activate(r, step - 4)
                        elif step == 6:
                            add_down(r)

                    def steps_after(turn, n):
                        if turn == 0 and n in FIRST_AT:
                            first(it, 1, FIRST_AT.index(n))
                        if turn in (1, 2):
                            if n in MIDDLE_AT:
                                middle(turn - 1, MIDDLE_AT.index(n))
                            if n == MIDDLE_AT[2] + 1:
                                scaled_h(bp, turn - 1, 1)
                        if turn == 3:
                            if n in END_AT:
                                end(0, END_AT.index(n))
                            if n == END_AT[2] + 1:
                                scaled_h(bp, 0, 2)
                            if n == END_AT[3] + 1 and not last_pair:
                                dve.wait_ge(h_turned[0], it * 3 + 3)
                                normed(bp + 1, 0)
                            if n == END_AT[3] + 3 and not last_pair:
                                scaled_h(bp + 1, 0, 0)

                    for turn in range(4):
                        width = WIDTH[TURNS[turn][1]]
                        for n in range(NH):
                            if n + 2 < NH:
                                find_max(it, turn, n + 2)
                            elif turn < 3:
                                find_max(it, turn + 1, n + 2 - NH)
                            dve.wait_ge(high_ready, it * (4 * NH) + (turn * NH + n + 1))
                            nc.vector.tensor_tensor(probT[:, n % 4, LOW, 0:width], T[n % 2][:, 0:width],
                                                    probT[:, n % 4, HIGH, 0:width].bitcast(FP32), ALU.subtract).then_inc(low_ready, 1)
                            if turn == 0 and n == 0:
                                normed(bp, 1)
                            if turn == 0 and n == 1:
                                scaled_h(bp, 1, 0)
                            if n >= 1:
                                steps_after(turn, n - 1)
                    for work in BOUNDARY[last_pair]:
                        if work == SCORES:
                            for n in range(2):
                                find_max(it + 1, 0, n)
                        elif work in FIRST_STEPS:
                            first(it + 1, 0, FIRST_STEPS.index(work))
                        elif work in END_STEPS:
                            if work == END_STEPS[3]:
                                scaled_h(bp, 1, 2)
                            end(1, END_STEPS.index(work))

                nc.vector.tensor_copy(bias_v[:], c.bias_v[:, bass.ds(l, 1), :].rearrange("p a d -> p (a d)"))
                normed(0, 0)
                scaled_h(0, 0, 0)
                for step in range(5):
                    first(l * PAIRS, 0, step)
                for n in range(2):
                    find_max(l * PAIRS, 0, n)
                with dve.Fori(0, PAIRS - 1) as bp:
                    pair(bp, False)
                pair(PAIRS - 1, True)


def decoder_end(nc, k, c, XX):
    with ExitStack() as stack:
        m = Memory(nc, stack)
        SQ, ss, r = m.sb("e_SQ", [P, NT, D]), m.sb("e_ss", [P, NT]), m.sb("e_r", [P, NT])
        ss_ready, r_ready = m.sem("e_ss_ready"), m.sem("e_r_ready")
        block = stack.enter_context(nc.Block())

        @block.vector
        def _(dve):
            nc.vector.tensor_tensor(SQ[:], XX[:], XX[:], ALU.mult)
            dve.drain()
            nc.vector.tensor_reduce(ss[:], SQ[:], AX.X, ALU.add)
            dve.drain()
            nc.vector.tensor_scalar(ss[:], ss[:], 1.0 / D, 1e-6, ALU.mult, ALU.add).then_inc(ss_ready, 1)
            dve.wait_ge(r_ready, 1)
            nc.vector.tensor_tensor(XX[:], XX[:], r[:].unsqueeze(2).broadcast_to([P, NT, D]), ALU.mult)
            dve.drain()
            nc.vector.tensor_tensor(XX[:], XX[:], c.nf[:].unsqueeze(1).broadcast_to([P, NT, D]), ALU.mult)
            dve.drain()
            nc.vector.scalar_tensor_tensor(k.X[:], XX[:], k.gate[:, 1:2], k.X[:], ALU.mult, ALU.add)

        @block.gpsimd
        def _(pool):
            pool.wait_ge(ss_ready, 1)
            nc.gpsimd.tensor_tensor(r[:], ss[:], k.minus_half[:, 0:NT], ALU.pow).then_inc(r_ready, 1)


def moe(nc, k, io):
    with ExitStack() as stack:
        m = Memory(nc, stack)
        hT = m.sb("f_hT", [P, NTOK])
        acc = m.sb("f_acc", [P, NT, D])
        weight = m.sb("f_weight", [P, NT, 8])
        ln = m.sb("f_ln", [P, 2])
        wr = m.sb("f_wr", [P, 7])
        with ExitStack() as inner:
            n = Memory(nc, inner)
            loaded = n.sem("f_loaded")
            block = inner.enter_context(nc.Block())

            @block.sync
            def _(sp):
                sp.dma_start(ln[:, 0:1], io["L1_ffn_ln_g"].rearrange("(d a) -> d a", a=1)).then_inc(loaded, 16)
                sp.dma_start(ln[:, 1:2], io["L1_ffn_ln_b"].rearrange("(d a) -> d a", a=1)).then_inc(loaded, 16)
                sp.dma_start(wr[:], io["L1_ffn_Wr"]).then_inc(loaded, 16)
                sp.wait_ge(loaded, 48)
        with ExitStack() as inner:
            n = Memory(nc, inner)
            Xn = n.sb("f_Xn", [P, NT, D])
            layer_norm(nc, k, k.X, Xn, tag="f_")
            layer_norm(nc, k, Xn, Xn, hT, scale=ln[:, 0:1], shift=ln[:, 1:2], tag="fh_")
        moe_router(nc, k, hT, wr, weight)
        moe_experts(nc, k, io, hT, weight, acc)
        with ExitStack() as inner:
            block = inner.enter_context(nc.Block())

            @block.vector
            def _(dve):
                nc.vector.scalar_tensor_tensor(k.X[:], acc[:], k.gate[:, 3:4], k.X[:], ALU.mult, ALU.add)


def moe_router(nc, k, hT, wr, weight):
    E = 7
    with ExitStack() as stack:
        m = Memory(nc, stack)
        logit, scratch = m.sb("r_logit", [P, NT, E]), m.sb("r_scratch", [P, NT, E])
        one = m.sb("r_one", [P, 2, NT, E])
        oneb = m.sb("r_oneb", [P, 2, NT, E], BF16)
        m1, m2, first, e = (m.sb("r_" + n, [P, NT]) for n in ("m1", "m2", "first", "e"))
        gates = m.sb("r_gates", [P, 2, NT])
        before, beforeb, allb = m.sb("r_before", [P, P]), m.sb("r_beforeb", [P, P], BF16), m.sb("r_allb", [P, P], BF16)
        total, through = m.sb("r_total", [P, 2 * NT, E]), m.sb("r_through", [P, 2 * NT, E])
        lb, rb, tb = m.bank("r_logit_bank"), m.bank("r_rank_bank"), m.bank("r_total_bank")
        made, logits, diff_ready, exp_ready, one_ready, ranked = (m.sem("r_" + n) for n in ("made", "logits", "diff_ready", "exp_ready", "one_ready", "ranked"))
        block = stack.enter_context(nc.Block())

        @block.gpsimd
        def _(pool):
            nc.gpsimd.memset(before[:], 1.0)
            nc.gpsimd.memset(allb[:], 1.0)
            pool.drain()
            nc.gpsimd.affine_select(out=before[:], in_=before[:], compare_op=ALU.is_gt, fill=0.0,
                                    base=0, pattern=[[1, P]], channel_multiplier=-1)
            pool.drain()
            nc.gpsimd.tensor_copy(beforeb[:], before[:]).then_inc(made, 1)

        @block.tensor
        def _(pe):
            for t in range(NT):
                last = nc.tensor.matmul(lb[:, E * t:E * t + E], hT[:, P * t:P * t + P], wr[:], start=True, stop=True)
            last.then_inc(logits, 1)
            pe.wait_ge(made, 1)
            pe.wait_ge(one_ready, 1)
            flat = oneb[:].rearrange("p s t e -> p (s t e)")
            nc.tensor.matmul(rb[:, 0:2 * NT * E], beforeb[:], flat, start=True, stop=True)
            nc.tensor.matmul(tb[:, 0:2 * NT * E], allb[:], flat, start=True, stop=True).then_inc(ranked, 1)

        @block.scalar
        def _(act):
            act.wait_ge(diff_ready, 1)
            nc.scalar.activation(e[:], e[:], ACT.Exp).then_inc(exp_ready, 1)

        @block.vector
        def _(dve):
            dve.wait_ge(logits, 1)
            nc.vector.tensor_copy(logit[:].rearrange("p t e -> p (t e)"), lb[:, 0:NT * E])
            dve.drain()
            top_two(nc, dve, logit[:], one[:, 0], one[:, 1], m1[:], m2[:], scratch[:], first[:], k.rev, NT, E)
            nc.vector.tensor_copy(oneb[:], one[:]).then_inc(one_ready, 1)
            nc.vector.tensor_tensor(e[:], m2[:], m1[:], ALU.subtract).then_inc(diff_ready, 1)
            dve.wait_ge(exp_ready, 1)
            nc.vector.tensor_scalar(m1[:], e[:], 1.0, None, ALU.add)
            dve.drain()
            nc.vector.reciprocal(gates[:, 0, :], m1[:])
            dve.drain()
            nc.vector.tensor_tensor(gates[:, 1, :], e[:], gates[:, 0, :], ALU.mult)
            dve.wait_ge(ranked, 1)
            nc.vector.tensor_copy(total[:].rearrange("p t e -> p (t e)"), tb[:, 0:2 * NT * E])
            dve.drain()
            for x in range(E):
                nc.vector.tensor_tensor_scan(through[:, :, x], k.ones[:, 0:2 * NT], total[:, :, x], 0.0, ALU.mult, ALU.add)
            dve.drain()
            nc.vector.tensor_tensor(through[:], through[:], total[:], ALU.subtract)
            dve.drain()
            nc.vector.tensor_tensor(through[:].rearrange("p t e -> p (t e)"), through[:].rearrange("p t e -> p (t e)"),
                                    rb[:, 0:2 * NT * E], ALU.add)
            dve.drain()
            ones = one[:].rearrange("p s t e -> p (s t) e")
            nc.vector.scalar_tensor_tensor(ones, through[:], float(CAPACITY), ones, ALU.is_lt, ALU.mult)
            dve.drain()
            nc.vector.tensor_tensor(ones, ones, gates[:].rearrange("p s t -> p (s t)").unsqueeze(2).broadcast_to([P, 2 * NT, E]), ALU.mult)
            nc.vector.memset(weight[:], 1.0)
            dve.drain()
            nc.vector.tensor_tensor(weight[:, :, 0:E], one[:, 0], one[:, 1], ALU.add)


def moe_experts(nc, k, io, hT, weight, acc):
    E, F, N = 8, 4, 512
    CH = NTOK // N
    STEPS = 2 * CH
    with ExitStack() as stack:
        m = Memory(nc, stack)
        W1, W3, W2 = (m.sb("x_" + n, [P, 2, F, P]) for n in ("W1", "W3", "W2"))
        tg, aT, scaled_y = m.sb("x_tg", [P, 2, N]), m.sb("x_aT", [P, 2, F, N]), m.sb("x_scaled_y", [P, 2, 4, D])
        A, U, Y = ([m.bank(f"x_{n}{i}") for i in range(2)] for n in "AUY")
        w_in = [m.sem("x_w_in0"), m.sem("x_w_in1")]
        made, tanhed, acted, y_made, scaled, added = (m.sem("x_" + n) for n in ("made", "tanhed", "acted", "y_made", "scaled", "added"))
        block = stack.enter_context(nc.Block())

        @block.sync
        def _(sp):
            with sp.Fori(0, E // 2) as e2:
                for s in range(2):
                    e = e2 * 2 + s
                    sp.wait_ge(added, e * CH + CH)
                    sp.dma_start(W1[:, s], io["experts_W1"][bass.ds(e, 1)].rearrange("a d (f p) -> d (a f) p", p=P)).then_inc(w_in[s], 16)
                    sp.dma_start(W3[:, s], io["experts_W3"][bass.ds(e, 1)].rearrange("a d (f p) -> d (a f) p", p=P)).then_inc(w_in[s], 16)
                    sp.dma_start(W2[:, s], io["experts_W2"][bass.ds(e, 1)].rearrange("a (f p) d -> p (a f) d", p=P)).then_inc(w_in[s], 16)

        @block.tensor
        def _(pe):
            with pe.Fori(0, E // 2) as e2:
                def up(i):
                    s, c = i // CH, i % CH
                    if c == 0:
                        pe.wait_ge(w_in[s], e2 * 48 + 48)
                    for f in range(F):
                        pe.wait_ge(acted, e2 * (STEPS * F) + (i * F + f + 1))
                        nc.tensor.matmul(A[f % 2][:], W1[:, s, f, :], hT[:, N * c:N * c + N], start=True, stop=True)
                        nc.tensor.matmul(U[f % 2][:], W3[:, s, f, :], hT[:, N * c:N * c + N], start=True, stop=True).then_inc(made, 1)

                def down(i):
                    s = i // CH
                    pe.wait_ge(acted, e2 * (STEPS * F) + (i * F + F + 2))
                    pe.wait_ge(scaled, e2 * STEPS + (i + 1))
                    for t in range(4):
                        for f in range(F):
                            last = nc.tensor.matmul(Y[i % 2][:, P * t:P * t + P], aT[:, i % 2, f, P * t:P * t + P], W2[:, s, f, :],
                                                    start=f == 0, stop=f == F - 1)
                    last.then_inc(y_made, 1)

                up(0)
                for i in range(STEPS):
                    if i + 1 < STEPS:
                        up(i + 1)
                    down(i)

        @block.scalar
        def _(act):
            with act.Fori(0, E // 2) as e2:
                for n in range(STEPS * F):
                    act.wait_ge(made, e2 * (STEPS * F) + (n + 1))
                    nc.scalar.activation(tg[:, n % 2, :], A[n % 2][:], ACT.Tanh, scale=0.5).then_inc(tanhed, 1)

        @block.vector
        def _(dve):
            dve.sem_inc(acted, 2)
            dve.sem_inc(scaled, 2)
            with dve.Fori(0, E // 2) as e2:
                def hidden(i):
                    for f in range(F):
                        n = i * F + f
                        dve.wait_ge(tanhed, e2 * (STEPS * F) + (n + 1))
                        nc.vector.scalar_tensor_tensor(tg[:, n % 2, :], tg[:, n % 2, :], 1.0, A[n % 2][:], ALU.add, ALU.mult)
                        dve.drain()
                        nc.vector.scalar_tensor_tensor(aT[:, i % 2, f, :], tg[:, n % 2, :], 0.5, U[n % 2][:],
                                                       ALU.mult, ALU.mult).then_inc(acted, 1)

                def weigh(i):
                    s, c = i // CH, i % CH
                    dve.wait_ge(y_made, e2 * STEPS + (i + 1))
                    dve.wait_ge(added, e2 * STEPS + (i + 2 * CH - 1))
                    nc.vector.tensor_tensor(scaled_y[:, i % 2], Y[i % 2][:].rearrange("p (t d) -> p t d", t=4),
                                            weight[:, 4 * c:4 * c + 4, bass.ds(e2 * 2 + s, 1)].broadcast_to([P, 4, D]), ALU.mult).then_inc(scaled, 1)

                hidden(0)
                for i in range(STEPS):
                    if i + 1 < STEPS:
                        hidden(i + 1)
                    weigh(i)

        @block.gpsimd
        def _(pool):
            nc.gpsimd.memset(acc[:], 0.0)
            pool.drain().then_inc(added, 2 * CH)
            with pool.Fori(0, E // 2) as e2:
                for i in range(STEPS):
                    c = i % CH
                    pool.wait_ge(scaled, e2 * STEPS + (i + 3))
                    nc.gpsimd.tensor_tensor(acc[:, 4 * c:4 * c + 4, :], acc[:, 4 * c:4 * c + 4, :], scaled_y[:, i % 2], ALU.add).then_inc(added, 1)


class Kept:

    EXPERTS_IN = 32

    def __init__(self, nc, stack):
        m = Memory(nc, stack)
        self.X = m.sb("X", [P, NT, D])
        self.ctxT = m.sb("ctxT", [P, NTOK])
        self.ctx_ones = m.sb("ctx_ones", [P, NT, 8, 17])
        self.ident, self.identb = m.sb("ident", [P, P]), m.sb("identb", [P, P], BF16)
        self.causal, self.causalb = m.sb("causal", [P, 2, P]), m.sb("causalb", [P, 2, P], BF16)
        self.ones, self.minus_half = m.sb("ones", [P, S]), m.sb("minus_half", [P, S])
        self.gate = m.sb("gate", [P, 4])
        self.rev = m.sb("rev", [P, 8])
        self.norm_sems = [m.sem("norm_" + n) for n in ("var_ready", "rstd_ready", "normed", "transposed")]
        self.norms = self.norms_turned = 0


def build(nc, io, out):
    with ExitStack() as stack:
        k = Kept(nc, stack)
        load_inputs(nc, k, io)
        with ExitStack() as inner:
            m = Memory(nc, inner)
            k.v_w, k.o_w, k.experts_in = m.sb("v_w", [P, 64, P]), m.sb("o_w", [P, 64, P]), m.sem("experts_in")
            mlstm(nc, k, io)
            switch_head(nc, k, io)
        decoder(nc, k, io)
        moe(nc, k, io)
        store(nc, k, out)


def store(nc, k, out):
    with ExitStack() as stack:
        stored = Memory(nc, stack).sem("out_stored")
        block = stack.enter_context(nc.Block())

        @block.sync
        def _(sp):
            sp.dma_start(out.rearrange("b (t p) d -> p (b t) d", p=P), k.X[:]).then_inc(stored, 16)
            sp.wait_ge(stored, 16)


def rope_tables():
    import numpy as np
    hd, heads = 8, 16
    inv = (1.0 / np.float32(10000.0) ** (np.arange(0, hd, 2, dtype=np.float32) / np.float32(hd))).astype(np.float32)
    f = np.arange(S, dtype=np.float32)[:, None] * inv[None, :]
    emb = np.concatenate([f, f], axis=-1)
    turn = np.zeros((P, P), np.float32)
    for r in range(P):
        turn[r + 4 if r % hd < 4 else r - 4, r] = -1.0 if r % hd < 4 else 1.0
    spread = np.zeros((P, 2, 2, 4, P), np.float32)
    for r in range(P):
        quadrant, slot, dim = r // 32, r // hd % 4, r % hd
        for j in range(4):
            for which, half in enumerate((slot // 2, slot % 2)):
                spread[32 * quadrant + hd * j + dim, which, half, j, r] = 1.0
    return dict(rope_cos=np.tile(np.cos(emb).T, (heads, 1)).astype(np.float32),
                rope_sin=np.tile(np.sin(emb).T, (heads, 1)).astype(np.float32), rope_turn=turn, spread_rows=spread.reshape(P, 16, P))


_OUTS = [((8, 256, 128), "float32")]


def kernel(**inputs):
    import numpy as _np
    import concourse.bacc as _bacc
    from concourse import mybir as _mybir
    from concourse.bass_utils import run_bass_kernel_spmd as _run

    nc = _bacc.Bacc("TRN2", target_bir_lowering=False, num_devices=1)
    laid = {name: _np.ascontiguousarray(a) for name, a in inputs.items()}
    laid.update(rope_tables())
    for w in ("W1", "W3", "W2"):
        laid["experts_" + w] = _np.concatenate([laid.pop("L1_ffn_" + w), laid.pop("L1_ffn_" + w + "s")[None]])
    arrays, io = {}, {}
    for name, a in laid.items():
        arrays[f"in_{name}"] = a
        io[name] = nc.dram_tensor(f"in_{name}", a.shape, _mybir.dt.from_np(a.dtype), kind="ExternalInput").ap()
    shape, dtype = _OUTS[0]
    out = nc.dram_tensor("out_0", shape, _mybir.dt.from_np(_np.dtype(dtype)), kind="ExternalOutput").ap()
    build(nc, io, out)
    r = _run(nc, [arrays], core_ids=[0])
    return r.results[0]["out_0"]
```
